# Optimizing a Trainium2 kernel written in Bass

```python
import numpy as np
import jax
import jax.numpy as jnp

def _softmax(x, axis=-1):
    return jax.nn.softmax(x, axis=axis)

def _gelu(x):
    return jax.nn.gelu(x, approximate=True)

def _silu(x):
    return jax.nn.silu(x)

def _sigmoid(x):
    return jax.nn.sigmoid(x)

def _layernorm(x, axis=-1, eps=1e-05):
    m = jnp.mean(x, axis=axis, keepdims=True)
    v = jnp.var(x, axis=axis, keepdims=True)
    return (x - m) / jnp.sqrt(v + eps)

def _scatter_add(tgt, idx, src, axis=0):
    return tgt.at[idx].add(src)

def _segment_sum(src, seg, n):
    return jax.ops.segment_sum(src, seg, n)
kernel_name = 'mk_xattn_ffn_d1_seqx_r2_f4ff48'

def setup_inputs(seed: int=0):
    np.random.seed(seed)
    _w = jnp.asarray

    def _rec_inputs():
        import jax
        import jax.numpy as jnp
        _rk = jax.random.key(seed)
        x = -0.0003929 + 0.9999 * jax.random.normal(jax.random.fold_in(_rk, 1), (2, 1024, 512), jnp.float32)
        _lenS = 1024 - jax.random.randint(jax.random.fold_in(_rk, 7), (2,), 0, max(1, 1024 // 4) + 1, jnp.int32)
        _lenS2 = 2048 - jax.random.randint(jax.random.fold_in(_rk, 8), (2,), 0, max(1, 2048 // 4) + 1, jnp.int32)
        _ctx_768P = jax.random.normal(jax.random.fold_in(_rk, 11), (2, 16, 384), jnp.float32)
        _ctx_768c = jax.random.dirichlet(jax.random.fold_in(_rk, 511), 0.3 * jnp.ones((16,), jnp.float32), (2, 2048))
        _ctx_768t = jnp.einsum('bsk,bkd->bsd', _ctx_768c, _ctx_768P)
        _ctx_768t = _ctx_768t * jax.lax.rsqrt(jnp.mean(jnp.square(_ctx_768t)) + 1e-12) * 0.953939
        ctx_768 = -7.36909e-05 + 0.999899 * (_ctx_768t + 0.3 * jax.random.normal(jax.random.fold_in(_rk, 611), (2, 2048, 384), jnp.float32))
        return (x, ctx_768)
    x, ctx_768 = _rec_inputs()

    def _L0_xattn_setup():
        import jax, jax.numpy as jnp
        import numpy as np
        EPS = 1e-05

        def layernorm(x, g, b):
            mu = jnp.mean(x, axis=-1, keepdims=True)
            var = jnp.mean(jnp.square(x - mu), axis=-1, keepdims=True)
            return (x - mu) * jax.lax.rsqrt(var + EPS) * g + b
        key = jax.random.key(seed)
        ks = jax.random.split(key, 12)
        B, L1, L2 = (8, 1024, 1024)
        D1, D2, E = (512, 384, 512)
        s1, s2, se = (D1 ** (-0.5), D2 ** (-0.5), E ** (-0.5))
        return {'modality1': jax.random.normal(ks[0], (B, L1, D1), jnp.float32), 'modality2': jax.random.normal(ks[1], (B, L2, D2), jnp.float32), 'ln1_g': jnp.ones((D1,), jnp.float32), 'ln1_b': jnp.zeros((D1,), jnp.float32), 'ln2_g': jnp.ones((D2,), jnp.float32), 'ln2_b': jnp.zeros((D2,), jnp.float32), 'Wq': jax.random.normal(ks[2], (D1, E), jnp.float32) * s1, 'bq': jax.random.normal(ks[3], (E,), jnp.float32) * 0.01, 'Wk': jax.random.normal(ks[4], (D2, E), jnp.float32) * s2, 'bk': jax.random.normal(ks[5], (E,), jnp.float32) * 0.01, 'Wv': jax.random.normal(ks[6], (D2, E), jnp.float32) * s2, 'bv': jax.random.normal(ks[7], (E,), jnp.float32) * 0.01, 'Wo': jax.random.normal(ks[8], (E, D1), jnp.float32) * se, 'bo': jax.random.normal(ks[9], (D1,), jnp.float32) * 0.01}
    _L0_xattn_all = _L0_xattn_setup()
    _L0_xattn_in = {k: v for k, v in _L0_xattn_all.items() if k in ('ln1_g', 'ln1_b', 'ln2_g', 'ln2_b', 'Wq', 'bq', 'Wk', 'bk', 'Wv', 'bv', 'Wo', 'bo')}
    del _L0_xattn_all

    def _L0_ffn_setup():
        import jax, jax.numpy as jnp
        import numpy as np
        LATENT = 512
        LEAF_W = 64
        DEPTH = 4
        N_LEAVES = 2 ** DEPTH
        N_NODES = 2 ** DEPTH - 1
        B, S = (4, 1024)

        def _fff_params(key, prefix):
            ks = jax.random.split(key, 4)
            d, h, l, n = (LATENT, LEAF_W, N_LEAVES, N_NODES)
            s_in = 1.0 / np.sqrt(d).astype(np.float32)
            s_h = 1.0 / np.sqrt(h).astype(np.float32)
            return {f'{prefix}_node_w': jax.random.normal(ks[0], (n, d), jnp.float32) * s_in, f'{prefix}_node_b': jax.random.normal(ks[1], (n,), jnp.float32) * s_in, f'{prefix}_w1': jax.random.normal(ks[2], (l, d, h), jnp.float32) * s_in, f'{prefix}_b1': jnp.zeros((l, h), jnp.float32), f'{prefix}_w2': jax.random.normal(ks[3], (l, h, d), jnp.float32) * s_h, f'{prefix}_b2': jnp.zeros((l, d), jnp.float32)}

        def _fff(x, node_w, node_b, w1, b1, w2, b2):
            Bx, Sx, D = x.shape
            xf = x.reshape(-1, D)
            N = xf.shape[0]
            cur = jnp.zeros((N,), jnp.int32)
            for _ in range(DEPTH):
                pw = node_w[cur]
                score = jnp.einsum('nd,nd->n', xf, pw) + node_b[cur]
                cur = 2 * cur + 1 + (score >= 0).astype(jnp.int32)
            leaf = cur - N_NODES
            sel = jax.nn.one_hot(leaf, N_LEAVES, dtype=xf.dtype)
            hidden_all = jax.nn.relu(jnp.einsum('nd,ldh->lnh', xf, w1) + b1[:, None, :])
            hidden = hidden_all * sel.T[:, :, None]
            out = jnp.einsum('lnh,lho->no', hidden, w2) + sel @ b2
            return out.reshape(Bx, Sx, D)
        key = jax.random.key(seed)
        kx, kq, kk, kv = jax.random.split(key, 4)
        inp = {'x': jax.random.normal(kx, (B, S, LATENT), jnp.float32)}
        inp.update(_fff_params(kq, 'q'))
        inp.update(_fff_params(kk, 'k'))
        inp.update(_fff_params(kv, 'v'))
        return inp
    _L0_ffn_all = _L0_ffn_setup()
    _L0_ffn_in = {k: v for k, v in _L0_ffn_all.items() if k in ('q_node_w', 'q_node_b', 'q_w1', 'q_b1', 'q_w2', 'q_b2', 'k_node_w', 'k_node_b', 'k_w1', 'k_b1', 'k_w2', 'k_b2', 'v_node_w', 'v_node_b', 'v_w1', 'v_b1', 'v_w2', 'v_b2')}
    del _L0_ffn_all
    return {'x': x, 'ctx_768': ctx_768, 'L0_xattn_ln1_g': _L0_xattn_in['ln1_g'], 'L0_xattn_ln1_b': _L0_xattn_in['ln1_b'], 'L0_xattn_ln2_g': _L0_xattn_in['ln2_g'], 'L0_xattn_ln2_b': _L0_xattn_in['ln2_b'], 'L0_xattn_Wq': _L0_xattn_in['Wq'], 'L0_xattn_bq': _L0_xattn_in['bq'], 'L0_xattn_Wk': _L0_xattn_in['Wk'], 'L0_xattn_bk': _L0_xattn_in['bk'], 'L0_xattn_Wv': _L0_xattn_in['Wv'], 'L0_xattn_bv': _L0_xattn_in['bv'], 'L0_xattn_Wo': _L0_xattn_in['Wo'], 'L0_xattn_bo': _L0_xattn_in['bo'], 'L0_ffn_q_node_w': _L0_ffn_in['q_node_w'], 'L0_ffn_q_node_b': _L0_ffn_in['q_node_b'], 'L0_ffn_q_w1': _L0_ffn_in['q_w1'], 'L0_ffn_q_b1': _L0_ffn_in['q_b1'], 'L0_ffn_q_w2': _L0_ffn_in['q_w2'], 'L0_ffn_q_b2': _L0_ffn_in['q_b2'], 'L0_ffn_k_node_w': _L0_ffn_in['k_node_w'], 'L0_ffn_k_node_b': _L0_ffn_in['k_node_b'], 'L0_ffn_k_w1': _L0_ffn_in['k_w1'], 'L0_ffn_k_b1': _L0_ffn_in['k_b1'], 'L0_ffn_k_w2': _L0_ffn_in['k_w2'], 'L0_ffn_k_b2': _L0_ffn_in['k_b2'], 'L0_ffn_v_node_w': _L0_ffn_in['v_node_w'], 'L0_ffn_v_node_b': _L0_ffn_in['v_node_b'], 'L0_ffn_v_w1': _L0_ffn_in['v_w1'], 'L0_ffn_v_b1': _L0_ffn_in['v_b1'], 'L0_ffn_v_w2': _L0_ffn_in['v_w2'], 'L0_ffn_v_b2': _L0_ffn_in['v_b2']}

def reference(x, ctx_768, L0_xattn_ln1_g, L0_xattn_ln1_b, L0_xattn_ln2_g, L0_xattn_ln2_b, L0_xattn_Wq, L0_xattn_bq, L0_xattn_Wk, L0_xattn_bk, L0_xattn_Wv, L0_xattn_bv, L0_xattn_Wo, L0_xattn_bo, L0_ffn_q_node_w, L0_ffn_q_node_b, L0_ffn_q_w1, L0_ffn_q_b1, L0_ffn_q_w2, L0_ffn_q_b2, L0_ffn_k_node_w, L0_ffn_k_node_b, L0_ffn_k_w1, L0_ffn_k_b1, L0_ffn_k_w2, L0_ffn_k_b2, L0_ffn_v_node_w, L0_ffn_v_node_b, L0_ffn_v_w1, L0_ffn_v_b1, L0_ffn_v_w2, L0_ffn_v_b2):
    import jax
    import jax.numpy as jnp

    def _L0_xattn_ref(modality1, modality2, ln1_g, ln1_b, ln2_g, ln2_b, Wq, bq, Wk, bk, Wv, bv, Wo, bo):
        import jax, jax.numpy as jnp
        import numpy as np
        EPS = 1e-05

        def layernorm(x, g, b):
            mu = jnp.mean(x, axis=-1, keepdims=True)
            var = jnp.mean(jnp.square(x - mu), axis=-1, keepdims=True)
            return (x - mu) * jax.lax.rsqrt(var + EPS) * g + b
        E = Wq.shape[1]
        scaling = E ** (-0.5)
        x1 = layernorm(modality1, ln1_g, ln1_b)
        x2 = layernorm(modality2, ln2_g, ln2_b)
        q = x1 @ Wq + bq
        k = x2 @ Wk + bk
        v = x2 @ Wv + bv
        scores = jnp.einsum('bqe,bke->bqk', q, k) * scaling
        attn = jax.nn.softmax(scores, axis=-1)
        ctx = jnp.einsum('bqk,bke->bqe', attn, v)
        return ctx @ Wo + bo

    def _L0_ffn_ref(x, q_node_w, q_node_b, q_w1, q_b1, q_w2, q_b2, k_node_w, k_node_b, k_w1, k_b1, k_w2, k_b2, v_node_w, v_node_b, v_w1, v_b1, v_w2, v_b2):
        import jax, jax.numpy as jnp
        import numpy as np
        LATENT = 512
        LEAF_W = 64
        DEPTH = 4
        N_LEAVES = 2 ** DEPTH
        N_NODES = 2 ** DEPTH - 1
        B, S = (4, 1024)

        def _fff_params(key, prefix):
            ks = jax.random.split(key, 4)
            d, h, l, n = (LATENT, LEAF_W, N_LEAVES, N_NODES)
            s_in = 1.0 / np.sqrt(d).astype(np.float32)
            s_h = 1.0 / np.sqrt(h).astype(np.float32)
            return {f'{prefix}_node_w': jax.random.normal(ks[0], (n, d), jnp.float32) * s_in, f'{prefix}_node_b': jax.random.normal(ks[1], (n,), jnp.float32) * s_in, f'{prefix}_w1': jax.random.normal(ks[2], (l, d, h), jnp.float32) * s_in, f'{prefix}_b1': jnp.zeros((l, h), jnp.float32), f'{prefix}_w2': jax.random.normal(ks[3], (l, h, d), jnp.float32) * s_h, f'{prefix}_b2': jnp.zeros((l, d), jnp.float32)}

        def _fff(x, node_w, node_b, w1, b1, w2, b2):
            Bx, Sx, D = x.shape
            xf = x.reshape(-1, D)
            N = xf.shape[0]
            cur = jnp.zeros((N,), jnp.int32)
            for _ in range(DEPTH):
                pw = node_w[cur]
                score = jnp.einsum('nd,nd->n', xf, pw) + node_b[cur]
                cur = 2 * cur + 1 + (score >= 0).astype(jnp.int32)
            leaf = cur - N_NODES
            sel = jax.nn.one_hot(leaf, N_LEAVES, dtype=xf.dtype)
            hidden_all = jax.nn.relu(jnp.einsum('nd,ldh->lnh', xf, w1) + b1[:, None, :])
            hidden = hidden_all * sel.T[:, :, None]
            out = jnp.einsum('lnh,lho->no', hidden, w2) + sel @ b2
            return out.reshape(Bx, Sx, D)
        q = _fff(x, q_node_w, q_node_b, q_w1, q_b1, q_w2, q_b2)
        k = _fff(x, k_node_w, k_node_b, k_w1, k_b1, k_w2, k_b2)
        v = _fff(x, v_node_w, v_node_b, v_w1, v_b1, v_w2, v_b2)
        scale = 1.0 / np.sqrt(LATENT).astype(np.float32)
        attn = jax.nn.softmax(jnp.einsum('bqd,bkd->bqk', q, k) * scale, axis=-1)
        return jnp.einsum('bqk,bkd->bqd', attn, v)
    x = x + _L0_xattn_ref(_layernorm(x, axis=-1), ctx_768, L0_xattn_ln1_g, L0_xattn_ln1_b, L0_xattn_ln2_g, L0_xattn_ln2_b, L0_xattn_Wq, L0_xattn_bq, L0_xattn_Wk, L0_xattn_bk, L0_xattn_Wv, L0_xattn_bv, L0_xattn_Wo, L0_xattn_bo)
    x = x + _L0_ffn_ref(_layernorm(x, axis=-1), L0_ffn_q_node_w, L0_ffn_q_node_b, L0_ffn_q_w1, L0_ffn_q_b1, L0_ffn_q_w2, L0_ffn_q_b2, L0_ffn_k_node_w, L0_ffn_k_node_b, L0_ffn_k_w1, L0_ffn_k_b1, L0_ffn_k_w2, L0_ffn_k_b2, L0_ffn_v_node_w, L0_ffn_v_node_b, L0_ffn_v_w1, L0_ffn_v_b1, L0_ffn_v_w2, L0_ffn_v_b2)
    return x

_drawn_inputs = setup_inputs


def setup_inputs(seed=0):
    import zlib

    import numpy as np

    out = dict(_drawn_inputs(seed))
    spreads = {'L0_xattn_ln1_g': (1.0, 0.2),
     'L0_xattn_ln1_b': (0.0, 0.45),
     'L0_xattn_ln2_g': (1.0, 0.2),
     'L0_xattn_ln2_b': (0.0, 0.1),
     'L0_ffn_q_b1': (0.0, 0.8),
     'L0_ffn_q_b2': (0.0, 0.8),
     'L0_ffn_k_b1': (0.0, 0.8),
     'L0_ffn_k_b2': (0.0, 0.8),
     'L0_ffn_v_b1': (0.0, 0.505),
     'L0_ffn_v_b2': (0.0, 0.292)}
    factors = {'L0_xattn_bq': 8.0,
     'L0_xattn_bk': 8.0,
     'L0_xattn_bv': 6.339,
     'L0_xattn_bo': 6.204,
     'L0_ffn_q_node_w': 5.588,
     'L0_ffn_q_node_b': 8.0,
     'L0_ffn_q_w1': 6.487,
     'L0_ffn_q_w2': 5.464,
     'L0_ffn_k_node_w': 5.581,
     'L0_ffn_k_node_b': 8.0,
     'L0_ffn_k_w1': 6.37,
     'L0_ffn_k_w2': 5.561,
     'L0_ffn_v_node_b': 5.607}
    for name, (base, spread) in spreads.items():
        noise = np.random.default_rng([zlib.crc32(name.encode()), seed]).standard_normal(out[name].shape)
        drawn = base * np.exp(spread * noise) if base else spread * noise
        out[name] = jnp.asarray(drawn.astype(out[name].dtype))
    for name, factor in factors.items():
        out[name] = (out[name] * factor).astype(out[name].dtype)
    return out
```

```python
from contextlib import ExitStack

import numpy as np
import concourse.bass as bass
from concourse import mybir

F32 = mybir.dt.float32
F32R = mybir.dt.float32r
F16 = mybir.dt.float16
I32 = mybir.dt.int32
ALU = mybir.AluOpType
ACT = mybir.ActivationFunctionType
AX = mybir.AxisListType
ds = bass.ds

P = 128
BANK = 512
EPS = 1e-5


def build(nc, x, ctx, ln1_g, ln1_b, ln2_g, ln2_b, Wq, bq, Wk, bk, Wv, bv, Wo, bo, trees, out):
    B, SQ, D = x.shape
    SC, DC = ctx.shape[1:]
    E = Wq.shape[1]
    KD, KC, KE = D // P, DC // P, E // P
    TQ, TC = SQ // P, SC // P
    NT = B * TQ
    NODES, _ = trees[0]["node_w"].shape
    LEAVES, _, HID = trees[0]["w1"].shape
    F = len(trees)
    SLOT_TILES = NT + LEAVES - 1
    HI_PAD = 32
    CROSS_SCALE = float(E) ** -0.5
    SELF_SCALE = float(D) ** -0.5
    XQ_TILES = BANK // P
    HALVES = SQ // BANK
    SBANKS = SC // BANK
    KBANKS = SQ // BANK

    x_rows = x.rearrange("b s d -> (b s) d")
    out_rows = out.rearrange("b s d -> (b s) d")
    ctx_rows = ctx.rearrange("b s d -> (b s) d")
    mid_rows = nc.dram_tensor("mid_rows", [B * SQ, D], F32, kind="Internal").ap()
    norm_rows = nc.dram_tensor("norm_rows", [B * SQ, D], F32, kind="Internal").ap()
    slot_rows = [nc.dram_tensor(f"slot_rows{f}", [SLOT_TILES * P, D], F32, kind="Internal").ap() for f in range(F)]

    top = ExitStack()
    scope = top

    def sb(name, shape, dt=F32):
        return scope.enter_context(nc.sbuf_tensor(name, shape, dt))

    def sem(name):
        return top.enter_context(nc.semaphore(name))

    with top:
        pS = top.enter_context(nc.psum_tensor("pS", [P, 4 * BANK], F32))
        pT = [top.enter_context(nc.psum_tensor(f"pT{i}", [P, BANK], F32)) for i in range(2)]
        pZ = top.enter_context(nc.psum_tensor("pZ", [P, BANK], F32))
        pE = top.enter_context(nc.psum_tensor("pE", [P, BANK], F32))

        def bank(i):
            return pS[:, i * BANK:(i + 1) * BANK]

        ident = sb("ident", [P, P])
        node_scores = sb("node_scores", [P, NT, F * NODES])
        scope = cross_scope = ExitStack()
        ctxT_hi = sb("ctxT_hi", [P, KC, SC], F32R)
        ctxT_lo = sb("ctxT_lo", [P, KC, SC], F32R)
        ctx_hi = sb("ctx_hi", [P, TC, DC], F32R)
        ctx_lo = sb("ctx_lo", [P, TC, DC], F32R)
        M_hi = sb("M_hi", [P, KD, DC], F32R)
        M_lo = sb("M_lo", [P, KD, DC], F32R)
        N_hi = sb("N_hi", [P, KC, D], F32R)
        N_lo = sb("N_lo", [P, KC, D], F32R)
        vectors = ((ln1_g, KD), (ln1_b, KD), (ln2_g, KC), (ln2_b, KC), (bq, KE), (bv, KE))
        NV = sum(k for _, k in vectors)
        columns = sb("columns", [P, NV])
        g1c, b1c, g2c, b2c, bqc, bvc = (
            columns[:, sum(k for _, k in vectors[:i]):sum(k for _, k in vectors[:i + 1])] for i in range(len(vectors)))
        u_col = sb("u_col", [P, KC])
        out_bias = sb("out_bias", [P, D])
        nodeT = sb("nodeT", [P, KD, F * NODES])
        node_bias = sb("node_bias", [P, F * NODES])
        c_raw = [sb(f"c_raw{i}", [P, DC]) for i in range(2)]
        c_norm = [sb(f"c_norm{i}", [P, DC]) for i in range(2)]
        x_raw = [sb(f"x_raw{i}", [P, D]) for i in range(2)]
        x_once = sb("x_once", [P, D])
        x_twice = [sb(f"x_twice{i}", [P, D]) for i in range(2)]
        ln_stats = sb("ln_stats", [P, 6])
        ln_mv = sb("ln_mv", [P, 2])
        ln_var = sb("ln_var", [P, 1])
        ln_rstd = sb("ln_rstd", [P, 1])
        minus_half = sb("minus_half", [P, 1])
        scope = fold_scope = ExitStack()
        wq_raw = sb("wq_raw", [P, KD, E])
        wk_raw = sb("wk_raw", [P, KC, E])
        wv_raw = sb("wv_raw", [P, KC, E])
        wo_raw = sb("wo_raw", [P, KE, D])
        wqT = sb("wqT", [P, KE, D])
        wkT = sb("wkT", [P, KE, DC])
        wvT = sb("wvT", [P, KE, DC])
        M_full = sb("M_full", [P, KD, DC])
        M_gain = sb("M_gain", [P, KD, DC])
        bvB = sb("bvB", [P, KE, P])
        vector_rows = sb("vector_rows", [NV, P])
        node_raw = sb("node_raw", [F * NODES, D])
        fold_scope.close()
        scope = cross_scope
        q_full = sb("q_full", [P, KC, SQ])
        q_hi = sb("q_hi", [P, KC, P], F32R)
        q_lo = sb("q_lo", [P, KC, P], F32R)
        PT_hi = sb("PT_hi", [P, TC * P], F32R)
        PT_lo = sb("PT_lo", [P, TC * P], F32R)
        probs = sb("probs", [P, SC])
        raw_max = sb("raw_max", [P, 1])
        neg_max = sb("neg_max", [P, 1])
        row_sum = sb("row_sum", [P, NT])
        inv_sum = sb("inv_sum", [P, 1])
        z_tile = sb("z_tile", [P, DC])
        zT = sb("zT", [P, DC])
        zT_hi = sb("zT_hi", [P, DC], F32R)
        zT_lo = sb("zT_lo", [P, DC], F32R)
        x_res = sb("x_res", [P, D])
        x_resb = sb("x_resb", [P, D])
        x_mid = sb("x_mid", [P, D])
        x_norm = sb("x_norm", [P, D])
        x_normT = sb("x_normT", [P, D])
        cross_scope.close()
        scope = top
        slot_index = sb("slot_index", [P, F * HI_PAD], I32)
        token_slot = sb("token_slot", [P, F * NT], I32)
        tile_leaf = sb("tile_leaf", [P, F * HI_PAD], I32)
        scope = leaf_scope = ExitStack()
        w1, b1B, w2_hi, w2_lo = [], [], [], []

        def leaf_set(i):
            w1.append(sb(f"w1_{i}", [P, KD, LEAVES * HID]))
            b1B.append(sb(f"b1B{i}", [P, LEAVES * HID]))
            w2_hi.append(sb(f"w2_hi{i}", [P, LEAVES, D], F32R))
            w2_lo.append(sb(f"w2_lo{i}", [P, LEAVES, D], F32R))

        leaf_set(0)
        w2_raw = [sb(f"w2_raw{i}", [P, D]) for i in range(2)]
        b2_raw = sb("b2_raw", [LEAVES, D])
        b2_hi = sb("b2_hi", [LEAVES, D], F32R)
        b2_lo = sb("b2_lo", [LEAVES, D], F32R)
        set0_words = KD * LEAVES * HID + LEAVES * HID + 2 * LEAVES * D + 2 * D + 3 * D
        leaf_set(1)
        row_index = [sb(f"row_index{i}", [P, 1], I32) for i in range(2)]
        x_slot = [sb(f"x_slot{i}", [P, D]) for i in range(2)]
        x_slotT = [sb(f"x_slotT{i}", [P, D]) for i in range(2)]
        hid = [sb(f"hid{i}", [P, HID]) for i in range(2)]
        hid_parts = [sb(f"hid_parts{i}", [P, 2 * HID], F32R) for i in range(2)]
        hT = [sb(f"hT{i}", [P, P], F32R) for i in range(2)]
        hT_one = [sb(f"hT_one{i}", [P, P], F32R) for i in range(2)]
        y_slot = [sb(f"y_slot{i}", [P, D]) for i in range(2)]
        leaf_scope.close()
        scope = route_scope = ExitStack()
        below_route = sb("below_route", [P, set0_words])
        FT = F * NT
        right = sb("right", [P, FT, NODES])
        reach = [sb(f"reach{k}", [P, FT, 2 ** k]) for k in range(1, 5)]
        onehot = reach[3]
        onehot_h = sb("onehot_h", [P, FT * LEAVES], F16)
        before = sb("before", [P, P], F16)
        ones_h = sb("ones_h", [P, P], F16)
        n_leaf = sb("n_leaf", [P, F * LEAVES], I32)
        n_tiles_i = sb("n_tiles_i", [P, F * LEAVES], I32)
        scan = [sb(f"scan{i}", [P, F, LEAVES]) for i in range(5)]
        n_tiles = sb("n_tiles", [P, F, LEAVES])
        base = sb("base", [P, F, LEAVES])
        place = sb("place", [P, FT, LEAVES])
        pos = sb("pos", [P, FT])
        part_i = sb("part_i", [P, 2 * FT], I32)
        part = sb("part", [P, 2 * FT])
        iota_i = sb("iota_i", [P, P], I32)
        iota_f = sb("iota_f", [P, P])
        token_i = sb("token_i", [P, NT], I32)
        token_f = sb("token_f", [P, NT])
        lo_hot = sb("lo_hot", [P, FT, P], F16)
        hi_hot = sb("hi_hot", [P, FT, HI_PAD])
        hi_tok = sb("hi_tok", [P, FT, HI_PAD], F16)
        leaf_cmp = sb("leaf_cmp", [P, F * HI_PAD, LEAVES])
        leaf_f = sb("leaf_f", [P, F * HI_PAD])
        leaf_m = sb("leaf_m", [P, F * HI_PAD])
        route_scope.close()
        scope = self_scope = ExitStack()
        kT_hi = [sb(f"kT_hi{i}", [P, KD, SQ], F32R) for i in range(B)]
        kT_lo = [sb(f"kT_lo{i}", [P, KD, SQ], F32R) for i in range(B)]
        v_hi = [sb(f"v_hi{i}", [P, TQ, D], F32R) for i in range(B)]
        v_lo = [sb(f"v_lo{i}", [P, TQ, D], F32R) for i in range(B)]
        kv_index = [sb(f"kv_index{i}", [P, 1], I32) for i in range(3)]
        k_rows = sb("k_rows", [P, D])
        v_rows = sb("v_rows", [P, D])
        q_rows = sb("q_rows", [P, D])
        sq_hi = sb("sq_hi", [P, D], F32R)
        sq_lo = sb("sq_lo", [P, D], F32R)
        sPT_hi = sb("sPT_hi", [P, SQ], F32R)
        sPT_lo = sb("sPT_lo", [P, SQ], F32R)
        sprobs = sb("sprobs", [P, SQ])
        sraw_max = sb("sraw_max", [P, 1])
        sneg_max = sb("sneg_max", [P, 1])
        srow_sum = sb("srow_sum", [P, NT])
        sinv_sum = sb("sinv_sum", [P, 1])
        mid_tile = sb("mid_tile", [P, D])
        out_tile = sb("out_tile", [P, D])
        self_scope.close()

        ident_zero = sem("ident_zero")
        ident_ready = sem("ident_ready")
        wq_in = sem("wq_in")
        wk_in = sem("wk_in")
        wv_in = sem("wv_in")
        wo_in = sem("wo_in")
        cols_in = sem("cols_in")
        cols_filled = sem("cols_filled")
        columns_ready = sem("columns_ready")
        node_in = sem("node_in")
        wT_filled = sem("wT_filled")
        wqT_ready = sem("wqT_ready")
        wkT_ready = sem("wkT_ready")
        wvT_ready = sem("wvT_ready")
        node_filled = sem("node_filled")
        nodeT_ready = sem("nodeT_ready")
        M_filled = sem("M_filled")
        M_full_ready = sem("M_full_ready")
        M_gained = sem("M_gained")
        M_hi_ready = sem("M_hi_ready")
        M_ready = sem("M_ready")
        N_filled = sem("N_filled")
        N_hi_ready = sem("N_hi_ready")
        N_ready = sem("N_ready")
        bvB_ready = sem("bvB_ready")
        bias_filled = sem("bias_filled")
        bias_ready = sem("bias_ready")
        c_in0 = sem("c_in0")
        c_in1 = sem("c_in1")
        c_norm_step = sem("c_norm_step")
        c_rooted = sem("c_rooted")
        x_rooted = sem("x_rooted")
        mid_rooted = sem("mid_rooted")
        half_ready = sem("half_ready")
        c_normed = sem("c_normed")
        c_hi_ready = sem("c_hi_ready")
        c_lo_ready = sem("c_lo_ready")
        c_turned = sem("c_turned")
        cT_hi_ready = sem("cT_hi_ready")
        cT_lo_ready = sem("cT_lo_ready")
        x_in0 = sem("x_in0")
        x_in1 = sem("x_in1")
        x_norm_step = sem("x_norm_step")
        x_normed = sem("x_normed")
        x_turned = sem("x_turned")
        xT_hi_ready = sem("xT_hi_ready")
        xT_lo_ready = sem("xT_lo_ready")
        q_filled = sem("q_filled")
        q_full_ready = sem("q_full_ready")
        q_hi_ready = sem("q_hi_ready")
        q_ready = sem("q_ready")
        scored = sem("scored")
        raw_max_ready = sem("raw_max_ready")
        max_ready = sem("max_ready")
        exp_ready = sem("exp_ready")
        probs_turned = sem("probs_turned")
        PT_hi_ready = sem("PT_hi_ready")
        PT_ready = sem("PT_ready")
        z_filled = sem("z_filled")
        inv_ready = sem("inv_ready")
        z_ready = sem("z_ready")
        z_turned = sem("z_turned")
        zT_ready = sem("zT_ready")
        zT_hi_ready = sem("zT_hi_ready")
        zT_lo_ready = sem("zT_lo_ready")
        res_in = sem("res_in")
        res_ready = sem("res_ready")
        o_filled = sem("o_filled")
        mid_ready = sem("mid_ready")
        mid_norm_step = sem("mid_norm_step")
        mid_normed = sem("mid_normed")
        mid_stored = sem("mid_stored")
        norm_stored = sem("norm_stored")
        n_turned = sem("n_turned")
        nT_ready = sem("nT_ready")
        nodes_filled = sem("nodes_filled")
        nodes_ready = sem("nodes_ready")
        route_consts = sem("route_consts")
        route_step = sem("route_step")
        onehots_ready = sem("onehots_ready")
        ranks_filled = sem("ranks_filled")
        split_ready = sem("split_ready")
        slots_filled = sem("slots_filled")
        tables_ready = sem("tables_ready")
        w1_in = sem("w1_in")
        b1_in = sem("b1_in")
        b2_in = sem("b2_in")
        w2_in0 = sem("w2_in0")
        w2_in1 = sem("w2_in1")
        w2_hi_ready = sem("w2_hi_ready")
        w2_lo_ready = sem("w2_lo_ready")
        b2_hi_ready = sem("b2_hi_ready")
        b2_ready = sem("b2_ready")
        b2_placed = sem("b2_placed")
        w2_zeroed = sem("w2_zeroed")
        hT_ones = sem("hT_ones")
        index_ready = sem("index_ready")
        slot_in0 = sem("slot_in0")
        slot_in1 = sem("slot_in1")
        slot_turned = sem("slot_turned")
        slotT_ready = sem("slotT_ready")
        h_filled = sem("h_filled")
        hid_step = sem("hid_step")
        hid_ready = sem("hid_ready")
        h_turned = sem("h_turned")
        hT_ready = sem("hT_ready")
        hT_one_ready = sem("hT_one_ready")
        y_filled = sem("y_filled")
        y_ready = sem("y_ready")
        y_stored0 = sem("y_stored0")
        y_stored1 = sem("y_stored1")
        kv_index_ready = sem("kv_index_ready")
        k_in = sem("k_in")
        v_in = sem("v_in")
        sk_turned = sem("sk_turned")
        kT_hi_ready = sem("kT_hi_ready")
        kT_ready = sem("kT_ready")
        v_hi_ready = sem("v_hi_ready")
        v_ready = sem("v_ready")
        q_index_ready = sem("q_index_ready")
        sq_in = sem("sq_in")
        sq_turned = sem("sq_turned")
        sq_hi_ready = sem("sq_hi_ready")
        sq_ready = sem("sq_ready")
        s_scored = sem("s_scored")
        s_raw_max_ready = sem("s_raw_max_ready")
        s_max_ready = sem("s_max_ready")
        s_exp_ready = sem("s_exp_ready")
        s_turned = sem("s_turned")
        sPT_hi_ready = sem("sPT_hi_ready")
        sPT_ready = sem("sPT_ready")
        sz_filled = sem("sz_filled")
        s_inv_ready = sem("s_inv_ready")
        mid_in = sem("mid_in")
        out_ready = sem("out_ready")
        out_stored = sem("out_stored")
        passed = {nc.vector.engine: sem("vector_passed"), nc.gpsimd.engine: sem("gpsimd_passed")}

        def split_product(pe, dst, left, right, first=True, last=True):
            pe.matmul(dst, left[0], right[0], start=first, stop=False)
            pe.matmul(dst, left[0], right[1], start=False, stop=False)
            return pe.matmul(dst, left[1], right[0], start=False, stop=last)

        def at_least(engine, semaphore, value):
            if not (isinstance(value, int) and value <= 0):
                engine.wait_ge(semaphore, value)

        def wait_apart(engine, semaphore, value):
            engine.wait_ge(semaphore, value)
            if not isinstance(value, int):
                engine.sem_inc(passed[engine.engine], 1)

        def layer_norm(dve, dst, src, step, at, rooted, done):
            nc.vector.bn_stats(ln_stats[:, :], src).then_inc(step, 1)
            wait_apart(dve, step, at + 1)
            nc.vector.bn_aggr(ln_mv[:, :], ln_stats[:, :]).then_inc(step, 1)
            dve.wait_ge(step, at + 2)
            nc.vector.tensor_scalar(ln_var[:, :], ln_mv[:, 1:2], EPS, None, ALU.add).then_inc(step, 1)
            dve.wait_ge(rooted, done)
            return nc.vector.tensor_scalar(dst, src, ln_mv[:, 0:1], ln_rstd[:, 0:1], ALU.subtract, ALU.mult)

        def root(pool, step, at, rooted):
            pool.wait_ge(step, at + 3)
            nc.gpsimd.tensor_tensor(ln_rstd[:, :], ln_var[:, :], minus_half[:, :], ALU.pow).then_inc(rooted, 1)

        def walk(engine, step, odd, split_leaf=None):

            def turn(i):
                for k in range(4):
                    step(i * 4 + (k + 3), (k + 3 + odd) % 2)
                    if split_leaf and k % 2:
                        split_leaf(i * 2 + k // 2, k // 2)

            for m in range(3):
                step(m, (m + odd) % 2)
            turn(0)
            with engine.Fori(1, (SLOT_TILES - 3) // 4) as i:
                turn(i)
            for m in range(SLOT_TILES, SLOT_TILES + 3):
                step(m, (m + odd) % 2)
                if split_leaf and m < SLOT_TILES + 2:
                    l = LEAVES - 2 + m - SLOT_TILES
                    split_leaf(l, l % 2)

        assert (SLOT_TILES - 3) % 4 == 0 and (SLOT_TILES - 3) // 2 == LEAVES - 2
        block = top.enter_context(nc.Block())

        @block.sync
        def _(sp):
            blocks = "(k p) n -> p k n"
            sp.dma_start(wq_raw[:, :, :], Wq.rearrange(blocks, p=P)).then_inc(wq_in, 16)
            sp.dma_start(wk_raw[:, :, :], Wk.rearrange(blocks, p=P)).then_inc(wk_in, 16)
            row = 0
            for src, k in vectors:
                sp.dma_start(vector_rows[row:row + k, :], src.rearrange("(k p) -> k p", p=P)).then_inc(cols_in, 16)
                row += k
            sp.dma_start(out_bias[:, :], bo.rearrange("(a n) -> a n", a=1).broadcast_to([P, D])).then_inc(cols_in, 16)
            for f, tree in enumerate(trees):
                own = slice(f * NODES, (f + 1) * NODES)
                sp.dma_start(node_raw[own, :], tree["node_w"]).then_inc(node_in, 16)
                sp.dma_start(node_bias[:, own], tree["node_b"].rearrange("(a n) -> a n", a=1).broadcast_to([P, NODES])
                             ).then_inc(node_in, 16)
            sp.dma_start(wv_raw[:, :, :], Wv.rearrange(blocks, p=P)).then_inc(wv_in, 16)
            sp.dma_start(wo_raw[:, :, :], Wo.rearrange(blocks, p=P)).then_inc(wo_in, 16)

            def context_in(b):
                c_in = [c_in0, c_in1]

                def load(t, slot):
                    at_least(sp, c_normed, t + (b * TC - 1))
                    sp.dma_start(c_raw[slot][:, :], ctx_rows[ds((t + b * TC) * P, P), :]).then_inc(c_in[slot], 16)

                load(0, 0)
                load(1, 1)
                with sp.Fori(1, TC // 2) as i:
                    load(i * 2, 0)
                    load(i * 2 + 1, 1)

            def query_in(b):
                x_in = [x_in0, x_in1]

                def load(t, slot):
                    at_least(sp, x_normed, t + (b * TQ - 1))
                    sp.dma_start(x_raw[slot][:, :], x_rows[ds((t + b * TQ) * P, P), :]).then_inc(x_in[slot], 16)
                load(0, 0)
                load(1, 1)
                with sp.Fori(1, TQ // 2) as i:
                    load(i * 2, 0)
                    load(i * 2 + 1, 1)

            def cross_tail(b):
                sp.wait_ge(M_ready, 1)
                sp.wait_ge(N_ready, 1)
                sp.wait_ge(bias_ready, 1)
                with sp.Fori(b * TQ, (b + 1) * TQ) as n:
                    sp.dma_start(x_res[:, :], x_rows[ds(n * P, P), :]).then_inc(res_in, 16)
                    sp.wait_ge(mid_ready, n + 1)
                    sp.dma_start(mid_rows[ds(n * P, P), :], x_mid[:, :]).then_inc(mid_stored, 16)
                    sp.wait_ge(mid_normed, n + 1)
                    sp.dma_start(norm_rows[ds(n * P, P), :], x_norm[:, :]).then_inc(norm_stored, 16)

            for b in range(B):
                context_in(b)
                query_in(b)
                cross_tail(b)

            w2_in = [w2_in0, w2_in1]

            def leaf_weights(f):
                tree = trees[f]
                if f == 0:
                    sp.wait_ge(nodes_ready, NT)
                    sp.wait_ge(norm_stored, 16 * NT)
                    sp.wait_ge(mid_stored, 16 * NT)
                else:
                    sp.wait_ge(tables_ready, 1)
                    sp.wait_ge(b2_placed, 32 * f)
                if f >= 2:
                    sp.wait_ge(y_filled, SLOT_TILES * (f - 1))
                    sp.wait_ge(hid_ready, SLOT_TILES * (f - 1))
                for k in range(KD):
                    sp.dma_start(w1[f % 2][:, k, :].rearrange("p (l h) -> p l h", l=LEAVES),
                                 tree["w1"][:, k * P:(k + 1) * P, :].rearrange("l p h -> p l h")).then_inc(w1_in, 16)
                sp.dma_start(b1B[f % 2][:, :], tree["b1"].rearrange("(a l) h -> a (l h)", a=1)
                             .broadcast_to([P, LEAVES * HID])).then_inc(b1_in, 16)
                sp.dma_start(b2_raw[:, :], tree["b2"]).then_inc(b2_in, 16)
                leaf_w2(f, 0, 0)
                leaf_w2(f, 1, 1)
                sp.wait_ge(b2_ready, f + 1)
                sp.wait_ge(w2_zeroed, min(f + 1, 2))
                for row, src in ((HID, b2_hi), (HID + 32, b2_lo)):
                    sp.dma_start(w2_lo[f % 2][row:row + 1, :, :].rearrange("a l n -> a (l n)").bitcast(F32),
                                 src[:, :].bitcast(F32)).then_inc(b2_placed, 16)

            def leaf_w2(f, l, slot):
                at_least(sp, w2_lo_ready, l + (f * LEAVES - 1))
                for half in range(2):
                    sp.dma_start(w2_raw[slot][half * HID:(half + 1) * HID, :],
                                 trees[f]["w2"][ds(l, 1), :, :].rearrange("a h n -> (a h) n")).then_inc(w2_in[slot], 16)

            leaf_weights(0)
            for l in range(2, LEAVES):
                leaf_w2(0, l, l % 2)
            y_stored = [y_stored0, y_stored1]
            for f in range(F):
                odd = SLOT_TILES * f % 2

                def store(j, slot):
                    sp.wait_ge(y_ready, j + (SLOT_TILES * f + 1))
                    sp.dma_start(slot_rows[f][ds(j * P, P), :], y_slot[slot][:, :]).then_inc(y_stored[slot], 16)

                if f + 1 < F:
                    leaf_weights(f + 1)
                store(0, odd)
                store(1, 1 - odd)
                with sp.Fori(0, (SLOT_TILES - 7) // 4) as i:
                    for k in range(2):
                        store(i * 4 + (2 * k + 2), odd)
                        store(i * 4 + (2 * k + 3), 1 - odd)
                        if f + 1 < F:
                            leaf_w2(f + 1, i * 2 + (2 + k), k)
                for j in range(SLOT_TILES - 5, SLOT_TILES):
                    store(j, (j + odd) % 2)
                    l = LEAVES - 2 + (j - (SLOT_TILES - 5)) // 2
                    if f + 1 < F and (j - (SLOT_TILES - 5)) % 2 and l < LEAVES:
                        leaf_w2(f + 1, l, l % 2)

            for q in range(2):
                sp.wait_ge(y_stored[q], 16 * ((F * SLOT_TILES + 1 - q) // 2))
            with sp.Fori(0, NT) as n:
                sp.dma_start(mid_tile[:, :], mid_rows[ds(n * P, P), :]).then_inc(mid_in, 16)
                sp.wait_ge(out_ready, n + 1)
                sp.dma_start(out_rows[ds(n * P, P), :], out_tile[:, :]).then_inc(out_stored, 16)
            sp.wait_ge(out_stored, 16 * NT)
            sp.wait_ge(mid_stored, 16 * NT)
            sp.wait_ge(norm_stored, 16 * NT)

        @block.tensor
        def _(pe):
            pe.wait_ge(ident_ready, 1)

            def turn_weights(raw, kin, dst_bank):
                for e in range(KE):
                    for k in range(kin):
                        last = pe.transpose(dst_bank(e)[:, k * P:(k + 1) * P], raw[:, k, e * P:(e + 1) * P], ident[:, :])
                    last.then_inc(wT_filled, 1)

            pe.wait_ge(wq_in, 16)
            turn_weights(wq_raw, KD, bank)
            pe.wait_ge(cols_in, 16 * (len(vectors) + 1))
            pe.transpose(pE[:, 0:NV], vector_rows[:, :], ident[0:NV, 0:NV]).then_inc(cols_filled, 1)
            pe.wait_ge(wk_in, 16)
            pe.wait_ge(columns_ready, 1)
            turn_weights(wk_raw, KC, lambda e: (pT[0], pT[1], pZ, pE)[e])
            pe.wait_ge(wv_in, 16)
            pe.wait_ge(wqT_ready, KE)
            turn_weights(wv_raw, KC, bank)
            pe.wait_ge(wkT_ready, KE)
            pe.wait_ge(node_in, 16 * 2 * F)
            for k in range(KD):
                last = pe.transpose(pE[:, k * F * NODES:(k + 1) * F * NODES], node_raw[:, k * P:(k + 1) * P],
                                    ident[0:F * NODES, 0:F * NODES])
            last.then_inc(node_filled, 1)
            m_bank = (pT[0], pT[1], pZ, pT[0])
            for k in range(KD):
                if k == 3:
                    pe.wait_ge(M_full_ready, 1)
                for e in range(KE):
                    last = pe.matmul(m_bank[k][:, 0:DC], wqT[:, e, k * P:(k + 1) * P], wkT[:, e, :],
                                     start=e == 0, stop=e == KE - 1)
                last.then_inc(M_filled, 1)
            pe.wait_ge(wvT_ready, KE)
            pe.wait_ge(wo_in, 16)
            for c in range(KC):
                for e in range(KE):
                    last = pe.matmul(bank(c), wvT[:, e, c * P:(c + 1) * P], wo_raw[:, e, :], start=e == 0, stop=e == KE - 1)
                last.then_inc(N_filled, 1)
            pe.wait_ge(bvB_ready, 1)
            for e in range(KE):
                pe.matmul(bank(3), bvB[:, e, :], wo_raw[:, e, :], start=e == 0, stop=e == KE - 1)
            pe.wait_ge(nodeT_ready, 1)
            pe.wait_ge(M_full_ready, KD)
            for c in range(KC):
                for e in range(KE):
                    pe.matmul(pE[:, c:c + 1], wkT[:, e, c * P:(c + 1) * P], bqc[:, e:e + 1], start=e == 0, stop=False)
                for k in range(KD):
                    last = pe.matmul(pE[:, c:c + 1], M_full[:, k, c * P:(c + 1) * P], b1c[:, k:k + 1],
                                     start=False, stop=k == KD - 1)
            last.then_inc(bias_filled, 1)

            def turn_context(b):
                if b:
                    pe.wait_ge(PT_ready, SBANKS * TQ * b)
                def turn(t, slot):
                    pe.wait_ge(c_normed, t + (TC * b + 1))
                    at_least(pe, cT_lo_ready, t + (TC * b - 1))
                    for k in range(KC):
                        last = pe.transpose(pT[slot][:, k * P:(k + 1) * P], c_norm[slot][:, k * P:(k + 1) * P], ident[:, :])
                    last.then_inc(c_turned, 1)
                turn(0, 0)
                turn(1, 1)
                with pe.Fori(1, TC // 2) as i:
                    turn(i * 2, 0)
                    turn(i * 2 + 1, 1)

            def project_queries(b):
                pe.wait_ge(cT_lo_ready, TC * (b + 1))
                pe.wait_ge(M_ready, 1)
                pe.wait_ge(N_ready, 1)
                pe.wait_ge(bias_ready, 1)
                for h in range(HALVES):
                    for tt in range(XQ_TILES):
                        n = b * TQ + h * XQ_TILES + tt
                        pe.wait_ge(x_normed, n + 1)
                        if n % TQ >= 2:
                            pe.wait_ge(xT_lo_ready, n - 1)
                        for k in range(KD):
                            last = pe.transpose(pT[tt % 2][:, k * P:(k + 1) * P], x_twice[tt % 2][:, k * P:(k + 1) * P],
                                                ident[:, :])
                        last.then_inc(x_turned, 1)
                    pe.wait_ge(xT_lo_ready, b * TQ + (h + 1) * XQ_TILES)
                    if h:
                        pe.wait_ge(q_full_ready, KC * (b * HALVES + h))
                    xT_hi = PT_hi[:, :].rearrange("p (k n) -> p k n", k=KD)
                    xT_lo = PT_lo[:, :].rearrange("p (k n) -> p k n", k=KD)
                    for c in range(KC):
                        cols = slice(c * P, (c + 1) * P)
                        for k in range(KD):
                            last = split_product(pe, bank(c), (M_hi[:, k, cols], M_lo[:, k, cols]),
                                                 (xT_hi[:, k, :], xT_lo[:, k, :]), k == 0, k == KD - 1)
                        last.then_inc(q_filled, 1)

            def cross(b):
                n0 = b * TQ

                def turn_probs(n, j):
                    pe.wait_ge(exp_ready, n + 1)
                    at_least(pe, PT_ready, n * SBANKS + (j - 1))
                    for k in range(4):
                        blk = (4 * j + k) * P
                        last = pe.transpose(pT[j % 2][:, k * P:(k + 1) * P], probs[:, blk:blk + P], ident[:, :])
                    last.then_inc(probs_turned, 1)

                def score(n, j):
                    if j == 0:
                        pe.wait_ge(q_ready, n + 1)
                    for c in range(KC):
                        last = split_product(pe, bank(j), (q_hi[:, c, :], q_lo[:, c, :]),
                                             (ctxT_hi[:, c, j * BANK:(j + 1) * BANK], ctxT_lo[:, c, j * BANK:(j + 1) * BANK]),
                                             c == 0, c == KC - 1)
                    if j == SBANKS - 1:
                        last.then_inc(scored, 1)

                def weigh(n, part, parts=4):
                    if part == 0:
                        pe.wait_ge(PT_ready, n * SBANKS + SBANKS)
                        at_least(pe, z_ready, n)
                    for t in range(part * TC // parts, (part + 1) * TC // parts):
                        last = split_product(pe, pZ[:, 0:DC], (PT_hi[:, t * P:(t + 1) * P], PT_lo[:, t * P:(t + 1) * P]),
                                             (ctx_hi[:, t, :], ctx_lo[:, t, :]), t == 0, t == TC - 1)
                    if part == parts - 1:
                        last.then_inc(z_filled, 1)

                def turn_z(e):
                    pe.wait_ge(z_ready, e + 1)
                    at_least(pe, nodes_ready, e)
                    for c in range(KC):
                        last = pe.transpose(pE[:, c * P:(c + 1) * P], z_tile[:, c * P:(c + 1) * P], ident[:, :])
                    last.then_inc(z_turned, 1)

                def project_out(e):
                    pe.wait_ge(zT_lo_ready, e + 1)
                    for c in range(KC):
                        cols = slice(c * P, (c + 1) * P)
                        last = split_product(pe, pE[:, :], (zT_hi[:, cols], zT_lo[:, cols]), (N_hi[:, c, :], N_lo[:, c, :]),
                                             c == 0, c == KC - 1)
                    last.then_inc(o_filled, 1)

                def turn_norm(e):
                    pe.wait_ge(mid_normed, e + 1)
                    for k in range(KD):
                        last = pe.transpose(pE[:, k * P:(k + 1) * P], x_norm[:, k * P:(k + 1) * P], ident[:, :])
                    last.then_inc(n_turned, 1)

                def score_nodes(e):
                    pe.wait_ge(nT_ready, e + 1)
                    for k in range(KD):
                        last = pe.matmul(pE[:, 0:F * NODES], x_normT[:, k * P:(k + 1) * P], nodeT[:, k, :],
                                         start=k == 0, stop=k == KD - 1)
                    last.then_inc(nodes_filled, 1)

                def step(n, front, back, tail):
                    for j in range(SBANKS):
                        if back:
                            turn_probs(n - 1, j)
                        if tail and j == 3:
                            project_out(n - 2)
                        if front:
                            score(n, j)
                        if tail and j == 0:
                            turn_z(n - 2)
                    for part in range(4):
                        if back:
                            weigh(n - 1, part)
                        if tail and part == 1:
                            turn_norm(n - 2)
                        if tail and part == 2:
                            score_nodes(n - 2)

                step(n0, True, False, False)
                step(n0 + 1, True, True, False)
                with pe.Fori(n0 + 2, n0 + TQ) as n:
                    step(n, True, True, True)
                step(n0 + TQ, False, True, True)
                step(n0 + TQ + 1, False, False, True)

            for b in range(B):
                turn_context(b)
                project_queries(b)
                cross(b)

            pe.wait_ge(route_consts, 3)
            W = NT * LEAVES
            for f in range(F):
                pe.wait_ge(onehots_ready, 1)
                oh = onehot_h[:, f * W:(f + 1) * W]
                for back in range(1, NT):
                    pe.matmul(bank(f)[:, back * LEAVES:W], ones_h[:, :], oh[:, 0:W - back * LEAVES],
                              start=back == 1, stop=False, skip_group_check=True)
                pe.matmul(bank(f)[:, 0:W], before[:, :], oh, start=False, stop=True, skip_group_check=True)
                for t in range(NT):
                    last = pe.matmul(pT[0][:, f * LEAVES:(f + 1) * LEAVES], ones_h[:, :],
                                     oh[:, t * LEAVES:(t + 1) * LEAVES], start=t == 0, stop=t == NT - 1)
            last.then_inc(ranks_filled, 1)
            for f in range(F):
                pe.wait_ge(split_ready, 1)
                for t in range(NT):
                    last = pe.matmul(pT[1][:, f * HI_PAD:(f + 1) * HI_PAD], lo_hot[:, f * NT + t, :],
                                     hi_tok[:, f * NT + t, :], start=t == 0, stop=t == NT - 1)
            last.then_inc(slots_filled, 1)
            pe.wait_ge(tables_ready, 1)

            for f in range(F):
                n0 = SLOT_TILES * f
                slot_in = [slot_in0, slot_in1]
                pe.wait_ge(w1_in, 16 * KD * (f + 1))

                def turn_rows(j, q):
                    pe.wait_ge(slot_in[q], (j + (n0 + 2 - q)) * 8)
                    at_least(pe, slotT_ready, j + (n0 - 1))
                    for k in range(KD):
                        last = pe.transpose(bank(q)[:, k * P:(k + 1) * P], x_slot[q][:, k * P:(k + 1) * P], ident[:, :])
                    last.then_inc(slot_turned, 1)

                def first_layer(j, q):
                    leaf = pe.value_load(tile_leaf[0:1, ds(j + f * HI_PAD, 1)], min_val=0, max_val=LEAVES - 1)
                    pe.wait_ge(slotT_ready, j + (n0 + 1))
                    at_least(pe, hid_ready, j + (n0 - 1))
                    for k in range(KD):
                        last = pe.matmul(pT[q][:, 0:HID], x_slotT[q][:, k * P:(k + 1) * P],
                                         w1[f % 2][:, k, ds(leaf * HID, HID)], start=k == 0, stop=k == KD - 1)
                    last.then_inc(h_filled, 1)

                def turn_hidden(j, q):
                    pe.wait_ge(hid_ready, j + (n0 + 1))
                    at_least(pe, hT_ready, j + (n0 - 1))
                    pe.transpose((pZ, pE)[q][:, 0:P], hid_parts[q][:, :].bitcast(F32), ident[:, :]).then_inc(h_turned, 1)

                def second_layer(j, q):
                    leaf = pe.value_load(tile_leaf[0:1, ds(j + f * HI_PAD, 1)], min_val=0, max_val=LEAVES - 1)
                    pe.wait_ge(hT_ready, j + (n0 + 1))
                    pe.wait_ge(hT_one_ready, j + (n0 + 1))
                    at_least(pe, y_ready, j + (n0 - 1))
                    pe.matmul(bank(2 + q), hT[q][:, :], w2_hi[f % 2][:, ds(leaf, 1), :], start=True, stop=False)
                    pe.matmul(bank(2 + q), hT_one[q][:, :], w2_lo[f % 2][:, ds(leaf, 1), :], start=False, stop=True
                              ).then_inc(y_filled, 1)

                def step(m, q):
                    edge = isinstance(m, int)
                    if not edge or m < SLOT_TILES:
                        turn_rows(m, q)
                    if not edge or 1 <= m <= SLOT_TILES:
                        first_layer(m - 1, 1 - q)
                    if not edge or 2 <= m <= SLOT_TILES + 1:
                        turn_hidden(m - 2, q)
                    if edge and m == 2:
                        pe.wait_ge(w2_lo_ready, LEAVES * (f + 1))
                        pe.wait_ge(b2_placed, 32 * (f + 1))
                        pe.wait_ge(hT_ones, 2)
                    if not edge or 3 <= m:
                        second_layer(m - 3, 1 - q)

                walk(pe, step, n0 % 2)

            for b in range(B):
                n0 = b * TQ

                def turn_keys(t):
                    pe.wait_ge(k_in, (t + (n0 + 1)) * 16)
                    at_least(pe, kT_ready, t + n0)
                    for k in range(KD):
                        last = pe.transpose(pE[:, k * P:(k + 1) * P], k_rows[:, k * P:(k + 1) * P], ident[:, :])
                    last.then_inc(sk_turned, 1)

                if b:
                    pe.wait_ge(sq_ready, n0)
                turn_keys(0)
                with pe.Fori(1, TQ) as t:
                    turn_keys(t)
                pe.wait_ge(kT_ready, n0 + TQ)
                pe.wait_ge(v_ready, n0 + TQ)

                def turn_query(n):
                    pe.wait_ge(sq_in, (n + 1) * 16)
                    at_least(pe, sq_ready, n)
                    for k in range(KD):
                        last = pe.transpose(pE[:, k * P:(k + 1) * P], q_rows[:, k * P:(k + 1) * P], ident[:, :])
                    last.then_inc(sq_turned, 1)

                def sturn(n, j):
                    pe.wait_ge(s_exp_ready, n + 1)
                    at_least(pe, sPT_ready, n * KBANKS + (j - 1))
                    for k in range(4):
                        blk = (4 * j + k) * P
                        last = pe.transpose(pT[j % 2][:, k * P:(k + 1) * P], sprobs[:, blk:blk + P], ident[:, :])
                    last.then_inc(s_turned, 1)

                def sscore(n, j):
                    if j == 0:
                        pe.wait_ge(sq_ready, n + 1)
                    for k in range(KD):
                        cols = slice(k * P, (k + 1) * P)
                        keys = slice(j * BANK, (j + 1) * BANK)
                        last = split_product(pe, bank(j), (sq_hi[:, cols], sq_lo[:, cols]),
                                             (kT_hi[b][:, k, keys], kT_lo[b][:, k, keys]), k == 0, k == KD - 1)
                    if j == KBANKS - 1:
                        last.then_inc(s_scored, 1)

                def sweigh(n):
                    pe.wait_ge(sPT_ready, n * KBANKS + KBANKS)
                    at_least(pe, out_ready, n)
                    for t in range(TQ):
                        last = split_product(pe, pZ[:, :], (sPT_hi[:, t * P:(t + 1) * P], sPT_lo[:, t * P:(t + 1) * P]),
                                             (v_hi[b][:, t, :], v_lo[b][:, t, :]), t == 0, t == TQ - 1)
                    last.then_inc(sz_filled, 1)

                def step(n, front, back, more=True):
                    for j in range(KBANKS):
                        if back:
                            sturn(n - 1, j)
                        if front:
                            sscore(n, j)
                    if front and more:
                        turn_query(n + 1)
                    if back:
                        sweigh(n - 1)

                turn_query(n0)
                step(n0, True, False)
                step(n0 + 1, True, True)
                with pe.Fori(n0 + 2, n0 + TQ - 1) as n:
                    step(n, True, True)
                step(n0 + TQ - 1, True, True, more=False)
                step(n0 + TQ, False, True)

        @block.scalar
        def _(act):
            for e in range(KE):
                act.wait_ge(wT_filled, e + 1)
                nc.scalar.copy(wqT[:, e, :], bank(e)).then_inc(wqT_ready, 1)
            for e in range(KE):
                act.wait_ge(wT_filled, 2 * KE + e + 1)
                nc.scalar.copy(wvT[:, e, :], bank(e)[:, 0:DC]).then_inc(wvT_ready, 1)
            m_bank = (pT[0], pT[1], pZ, pT[0])
            for k in range(KD):
                act.wait_ge(M_filled, k + 1)
                nc.scalar.copy(M_full[:, k, :], m_bank[k][:, 0:DC]).then_inc(M_full_ready, 1)
            for c in range(KC):
                act.wait_ge(N_filled, c + 1)
                nc.scalar.copy(N_hi[:, c, :], bank(c)).then_inc(N_hi_ready, 1)
            act.wait_ge(M_gained, KD)
            nc.scalar.copy(M_hi[:, :, :], M_gain[:, :, :]).then_inc(M_hi_ready, 1)

            def context(b):
                if b:
                    act.wait_ge(z_filled, TQ * b)

                def split(t, slot):
                    act.wait_ge(c_normed, t + (TC * b + 1))
                    nc.scalar.copy(ctx_hi[:, ds(t, 1), :], c_norm[slot][:, :]).then_inc(c_hi_ready, 1)
                    act.wait_ge(c_turned, t + (TC * b + 1))
                    nc.scalar.copy(ctxT_hi[:, :, ds(t * P, P)], pT[slot][:, 0:DC].rearrange("p (k n) -> p k n", k=KC)
                                   ).then_inc(cT_hi_ready, 1)

                with act.Fori(0, TC // 2) as i:
                    split(i * 2, 0)
                    split(i * 2 + 1, 1)

            def queries(b):
                for h in range(HALVES):
                    if h:
                        act.wait_ge(q_filled, KC * (b * HALVES + h))
                    xT_hi = PT_hi[:, :].rearrange("p (k n) -> p k n", k=KD)
                    for tt in range(XQ_TILES):
                        n = b * TQ + h * XQ_TILES + tt
                        act.wait_ge(x_turned, n + 1)
                        if n == 0:
                            act.wait_ge(M_ready, 1)
                            act.wait_ge(N_ready, 1)
                            act.wait_ge(bias_ready, 1)
                        nc.scalar.copy(xT_hi[:, :, tt * P:(tt + 1) * P], pT[tt % 2][:, :].rearrange("p (k n) -> p k n", k=KD)
                                       ).then_inc(xT_hi_ready, 1)

            def cross(b):
                n0 = b * TQ

                def probs_hi(n, j, first=False):
                    act.wait_ge(probs_turned, n * SBANKS + (j + 1))
                    if j == 0:
                        if first:
                            act.wait_ge(q_filled, KC * HALVES * (b + 1))
                        else:
                            act.wait_ge(z_filled, n)
                    nc.scalar.copy(PT_hi[:, j * BANK:(j + 1) * BANK], pT[j % 2][:, :]).then_inc(PT_hi_ready, 1)

                def exp(n):
                    act.wait_ge(max_ready, n + 1)
                    at_least(act, probs_turned, n * SBANKS)
                    nc.scalar.activation(probs[:, :], pS[:, 0:SC], ACT.Exp, bias=neg_max[:, 0:1], scale=CROSS_SCALE,
                                         accum_out=row_sum[:, ds(n, 1)]).then_inc(exp_ready, 1)

                def z_hi(e):
                    act.wait_ge(zT_ready, (e + 1) * KC)
                    nc.scalar.copy(zT_hi[:, :], zT[:, :]).then_inc(zT_hi_ready, 1)

                def norm_T(e):
                    act.wait_ge(n_turned, e + 1)
                    nc.scalar.copy(x_normT[:, :], pE[:, :]).then_inc(nT_ready, 1)

                def step(n, front, back, tail, first=False):
                    for j in range(SBANKS):
                        if back:
                            probs_hi(n - 1, j, first)
                        if tail and j == 1:
                            z_hi(n - 2)
                    if front:
                        exp(n)
                    if tail:
                        norm_T(n - 2)

                step(n0, True, False, False)
                step(n0 + 1, True, True, False, first=True)
                with act.Fori(n0 + 2, n0 + TQ) as n:
                    step(n, True, True, True)
                step(n0 + TQ, False, True, True)
                step(n0 + TQ + 1, False, False, True)

            for b in range(B):
                context(b)
                queries(b)
                cross(b)

            w2_in = [w2_in0, w2_in1]

            def b2_high(f):
                act.wait_ge(b2_in, 16 * (f + 1))
                nc.scalar.copy(b2_hi[:, :], b2_raw[:, :]).then_inc(b2_hi_ready, 1)

            def w2_high(f, l, slot):
                act.wait_ge(w2_in[slot], (l + (f * LEAVES + 2 - slot)) * 16)
                nc.scalar.copy(w2_hi[f % 2][:, ds(l, 1), :], w2_raw[slot][:, :]).then_inc(w2_hi_ready, 1)

            b2_high(0)
            with act.Fori(0, LEAVES // 2) as i:
                w2_high(0, i * 2, 0)
                w2_high(0, i * 2 + 1, 1)
            for f in range(F):
                n0 = SLOT_TILES * f

                def rows_T(j, q):
                    act.wait_ge(slot_turned, j + (n0 + 1))
                    at_least(act, h_filled, j + (n0 - 1))
                    nc.scalar.copy(x_slotT[q][:, :], bank(q)).then_inc(slotT_ready, 1)

                def hidden_T(j, q):
                    act.wait_ge(h_turned, j + (n0 + 1))
                    at_least(act, y_filled, j + (n0 - 1))
                    nc.scalar.copy(hT[q][:, :], (pZ, pE)[q][:, 0:P]).then_inc(hT_ready, 1)

                def step(m, q):
                    edge = isinstance(m, int)
                    if not edge or m < SLOT_TILES:
                        rows_T(m, q)
                    if not edge or 2 <= m <= SLOT_TILES + 1:
                        hidden_T(m - 2, q)

                odd = n0 % 2
                if f + 1 < F:
                    b2_high(f + 1)
                walk(act, step, odd, (lambda l, slot: w2_high(f + 1, l, slot)) if f + 1 < F else None)

            for b in range(B):
                n0 = b * TQ

                def keys(t):
                    act.wait_ge(sk_turned, t + (n0 + 1))
                    nc.scalar.copy(kT_hi[b][:, :, ds(t * P, P)], pE[:, :].rearrange("p (k n) -> p k n", k=KD)
                                   ).then_inc(kT_hi_ready, 1)
                    act.wait_ge(v_in, (t + (n0 + 1)) * 16)
                    nc.scalar.copy(v_hi[b][:, ds(t, 1), :], v_rows[:, :]).then_inc(v_hi_ready, 1)

                with act.Fori(0, TQ) as t:
                    keys(t)

                def query(n):
                    act.wait_ge(sq_turned, n + 1)
                    at_least(act, s_scored, n)
                    nc.scalar.copy(sq_hi[:, :], pE[:, :]).then_inc(sq_hi_ready, 1)

                def sprobs_hi(n, j):
                    act.wait_ge(s_turned, n * KBANKS + (j + 1))
                    if j == 0 and not (isinstance(n, int) and n == 0):
                        act.wait_ge(sz_filled, n)
                    nc.scalar.copy(sPT_hi[:, j * BANK:(j + 1) * BANK], pT[j % 2][:, :]).then_inc(sPT_hi_ready, 1)

                def sexp(n):
                    act.wait_ge(s_max_ready, n + 1)
                    at_least(act, s_turned, n * KBANKS)
                    nc.scalar.activation(sprobs[:, :], pS[:, 0:SQ], ACT.Exp, bias=sneg_max[:, 0:1], scale=SELF_SCALE,
                                         accum_out=srow_sum[:, ds(n, 1)]).then_inc(s_exp_ready, 1)

                def step(n, front, back, more=True):
                    for j in range(KBANKS):
                        if back:
                            sprobs_hi(n - 1, j)
                    if front:
                        sexp(n)
                        if more:
                            query(n + 1)

                query(n0)
                step(n0, True, False)
                step(n0 + 1, True, True)
                with act.Fori(n0 + 2, n0 + TQ - 1) as n:
                    step(n, True, True)
                step(n0 + TQ - 1, True, True, more=False)
                step(n0 + TQ, False, True)

        @block.vector
        def _(dve):
            dve.wait_ge(cols_filled, 1)
            nc.vector.tensor_copy(columns[:, :], pE[:, 0:NV]).then_inc(columns_ready, 1)
            dve.wait_ge(columns_ready, 1)
            for e in range(KE):
                last = nc.vector.tensor_copy(bvB[:, e, :], bvc[:, e:e + 1].broadcast_to([P, P]))
            last.then_inc(bvB_ready, 1)
            for e in range(KE):
                dve.wait_ge(wT_filled, KE + e + 1)
                nc.vector.tensor_copy(wkT[:, e, :], (pT[0], pT[1], pZ, pE)[e][:, 0:DC]).then_inc(wkT_ready, 1)
            dve.wait_ge(node_filled, 1)
            nc.vector.tensor_copy(nodeT[:, :, :].rearrange("p k n -> p (k n)"), pE[:, 0:KD * F * NODES]).then_inc(nodeT_ready, 1)
            for k in range(KD):
                dve.wait_ge(M_full_ready, k + 1)
                nc.vector.tensor_scalar(M_gain[:, k, :], M_full[:, k, :], g1c[:, k:k + 1], None, ALU.mult).then_inc(M_gained, 1)
            dve.wait_ge(M_hi_ready, 1)
            nc.vector.tensor_tensor(M_lo[:, :, :], M_gain[:, :, :], M_hi[:, :, :].bitcast(F32), ALU.subtract).then_inc(M_ready, 1)
            for c in range(KC):
                dve.wait_ge(N_hi_ready, c + 1)
                last = nc.vector.tensor_tensor(N_lo[:, c, :], bank(c), N_hi[:, c, :].bitcast(F32), ALU.subtract)
            last.then_inc(N_ready, 1)
            dve.wait_ge(bias_filled, 1)
            nc.vector.tensor_copy(u_col[:, :], pE[:, 0:KC])
            nc.vector.tensor_tensor(out_bias[:, :], bank(3), out_bias[:, :], ALU.add).then_inc(bias_ready, 1)

            def context(b):
                c_in = [c_in0, c_in1]
                n0 = TC * b

                def norm(t, slot):
                    dve.wait_ge(c_in[slot], (t + (n0 + 2 - slot)) * 8)
                    at_least(dve, c_lo_ready, t + (n0 - 1))
                    at_least(dve, c_turned, t + (n0 - 1))
                    layer_norm(dve, c_norm[slot][:, :], c_raw[slot][:, :], c_norm_step, (t + n0) * 3,
                               c_rooted, t + (n0 + 1)).then_inc(c_normed, 1)

                def low(t, slot):
                    dve.wait_ge(cT_hi_ready, t + (n0 + 1))
                    nc.vector.tensor_tensor(ctxT_lo[:, :, ds(t * P, P)], pT[slot][:, 0:DC].rearrange("p (k n) -> p k n", k=KC),
                                            ctxT_hi[:, :, ds(t * P, P)].bitcast(F32), ALU.subtract).then_inc(cT_lo_ready, 1)

                norm(0, 0)
                norm(1, 1)
                low(0, 0)
                with dve.Fori(1, TC // 2) as i:
                    norm(i * 2, 0)
                    low(i * 2 - 1, 1)
                    norm(i * 2 + 1, 1)
                    low(i * 2, 0)
                low(TC - 1, 1)

            def queries(b):
                x_in = [x_in0, x_in1]
                xT_hi = PT_hi[:, :].rearrange("p (k n) -> p k n", k=KD)
                xT_lo = PT_lo[:, :].rearrange("p (k n) -> p k n", k=KD)

                def low(n):
                    q, cols = n % 2, slice(n % XQ_TILES * P, (n % XQ_TILES + 1) * P)
                    dve.wait_ge(xT_hi_ready, n + 1)
                    nc.vector.tensor_tensor(xT_lo[:, :, cols], pT[q][:, :].rearrange("p (k n) -> p k n", k=KD),
                                            xT_hi[:, :, cols].bitcast(F32), ALU.subtract).then_inc(xT_lo_ready, 1)

                for h in range(HALVES):
                    for tt in range(XQ_TILES):
                        n = b * TQ + h * XQ_TILES + tt
                        q = n % 2
                        dve.wait_ge(x_in[q], 16 * (n // 2 + 1))
                        layer_norm(dve, x_once[:, :], x_raw[q][:, :], x_norm_step, 7 * n,
                                   x_rooted, 2 * n + 1).then_inc(x_norm_step, 1)
                        dve.wait_ge(x_norm_step, 7 * n + 4)
                        at_least(dve, x_turned, n - 1)
                        layer_norm(dve, x_twice[q][:, :], x_once[:, :], x_norm_step, 7 * n + 4,
                                   x_rooted, 2 * n + 2).then_inc(x_normed, 1)
                        if tt:
                            low(n - 1)
                    low(n)
                    for c in range(KC):
                        dve.wait_ge(q_filled, KC * (b * HALVES + h) + c + 1)
                        if b and c == h == 0:
                            dve.wait_ge(q_ready, TQ * b)
                        nc.vector.tensor_scalar(q_full[:, c, h * BANK:(h + 1) * BANK], bank(c), u_col[:, c:c + 1],
                                                g2c[:, c:c + 1], ALU.add, ALU.mult).then_inc(q_full_ready, 1)

            def cross(b):
                n0 = b * TQ

                def probs_lo(n, j):
                    dve.wait_ge(PT_hi_ready, n * SBANKS + (j + 1))
                    cols = slice(j * BANK, (j + 1) * BANK)
                    nc.vector.tensor_tensor(PT_lo[:, cols], pT[j % 2][:, :], PT_hi[:, cols].bitcast(F32), ALU.subtract
                                            ).then_inc(PT_ready, 1)

                def row_max(n):
                    dve.wait_ge(scored, n + 1)
                    nc.vector.tensor_reduce(raw_max[:, :], pS[:, 0:SC], AX.X, ALU.max).then_inc(raw_max_ready, 1)
                    dve.wait_ge(raw_max_ready, n + 1)
                    nc.vector.tensor_scalar(neg_max[:, :], raw_max[:, :], -CROSS_SCALE, None, ALU.mult).then_inc(max_ready, 1)

                def normalise(n):
                    dve.wait_ge(exp_ready, n + 1)
                    nc.vector.reciprocal(inv_sum[:, :], row_sum[:, ds(n, 1)]).then_inc(inv_ready, 1)
                    dve.wait_ge(inv_ready, n + 1)
                    dve.wait_ge(z_filled, n + 1)
                    at_least(dve, z_turned, n)
                    nc.vector.tensor_scalar(z_tile[:, :], pZ[:, 0:DC], inv_sum[:, 0:1], None, ALU.mult).then_inc(z_ready, 1)

                def affine(e):
                    dve.wait_ge(z_turned, e + 1)
                    at_least(dve, zT_lo_ready, e)
                    for c in range(KC):
                        cols = slice(c * P, (c + 1) * P)
                        nc.vector.tensor_scalar(zT[:, cols], pE[:, cols], g2c[:, c:c + 1], b2c[:, c:c + 1],
                                                ALU.mult, ALU.add).then_inc(zT_ready, 1)

                def residual(e):
                    dve.wait_ge(o_filled, e + 1)
                    dve.wait_ge(res_ready, e + 1)
                    at_least(dve, mid_stored, e * 16)
                    nc.vector.tensor_tensor(x_mid[:, :], pE[:, :], x_resb[:, :], ALU.add).then_inc(mid_ready, 1)

                def norm_mid(e):
                    dve.wait_ge(mid_ready, e + 1)
                    at_least(dve, norm_stored, e * 16)
                    at_least(dve, n_turned, e)
                    layer_norm(dve, x_norm[:, :], x_mid[:, :], mid_norm_step, e * 3,
                               mid_rooted, e + 1).then_inc(mid_normed, 1)

                def nodes(e):
                    dve.wait_ge(nodes_filled, e + 1)
                    nc.vector.tensor_tensor(node_scores[:, ds(e, 1), :], pE[:, 0:F * NODES], node_bias[:, :], ALU.add
                                            ).then_inc(nodes_ready, 1)

                def step(n, front, back, tail):
                    for j in range(SBANKS):
                        if back:
                            probs_lo(n - 1, j)
                        if tail and j == 1:
                            affine(n - 2)
                    if tail:
                        residual(n - 2)
                    if front:
                        row_max(n)
                    if tail:
                        norm_mid(n - 2)
                        nodes(n - 2)
                    if back:
                        normalise(n - 1)

                step(n0, True, False, False)
                step(n0 + 1, True, True, False)
                with dve.Fori(n0 + 2, n0 + TQ) as n:
                    step(n, True, True, True)
                step(n0 + TQ, False, True, True)
                step(n0 + TQ + 1, False, False, True)

            for b in range(B):
                context(b)
                queries(b)
                cross(b)

            count = [0]

            def then(instruction):
                count[0] += 1
                instruction.then_inc(route_step, 1)
                dve.wait_ge(route_step, count[0])

            v = nc.vector
            dve.wait_ge(norm_stored, 16 * NT)
            dve.wait_ge(mid_stored, 16 * NT)
            dve.wait_ge(nodes_ready, NT)
            then(v.tensor_scalar(right[:, :, :].rearrange("p (f t) n -> p t f n", f=F),
                                 node_scores[:, :, :].rearrange("p t (f n) -> p t f n", f=F), 0.0, None, ALU.is_ge))
            for k in range(len(reach)):
                wide = reach[k][:, :, :].rearrange("p t (n side) -> p t n side", side=2)
                own = right[:, :, 2 ** k - 1:2 ** (k + 1) - 1]
                if k == 0:
                    v.tensor_copy(wide[:, :, :, 1], own)
                    then(v.tensor_scalar(wide[:, :, :, 0], own, -1.0, 1.0, ALU.mult, ALU.add))
                else:
                    then(v.tensor_tensor(wide[:, :, :, 1], reach[k - 1][:, :, :], own, ALU.mult))
                    then(v.tensor_tensor(wide[:, :, :, 0], reach[k - 1][:, :, :], wide[:, :, :, 1], ALU.subtract))
            v.tensor_copy(onehot_h[:, :], onehot[:, :, :].rearrange("p t l -> p (t l)")).then_inc(onehots_ready, 1)
            dve.wait_ge(route_consts, 5)
            v.tensor_copy(iota_f[:, :], iota_i[:, :])
            then(v.tensor_copy(token_f[:, :], token_i[:, :]))
            dve.wait_ge(ranks_filled, 1)
            then(v.tensor_scalar(n_leaf[:, :], pT[0][:, 0:F * LEAVES], float(P - 1), None, ALU.add))
            then(v.tensor_single_scalar(n_tiles_i[:, :], n_leaf[:, :], P.bit_length() - 1, ALU.arith_shift_right))
            then(v.tensor_copy(n_tiles[:, :, :].rearrange("p f l -> p (f l)"), n_tiles_i[:, :]))
            src = n_tiles
            for k in range(4):
                d = 2 ** k
                v.tensor_copy(scan[k][:, :, 0:d], src[:, :, 0:d])
                then(v.tensor_tensor(scan[k][:, :, d:], src[:, :, d:], src[:, :, 0:LEAVES - d], ALU.add))
                src = scan[k]
            ends = src
            then(v.tensor_tensor(scan[4][:, :, :], ends[:, :, :], n_tiles[:, :, :], ALU.subtract))
            then(v.tensor_scalar(base[:, :, :], scan[4][:, :, :], float(P), None, ALU.mult))
            for f in range(F):
                own = place[:, f * NT:(f + 1) * NT, :]
                last = v.tensor_tensor(own, bank(f)[:, 0:NT * LEAVES].rearrange("p (t l) -> p t l", t=NT),
                                       base[:, f:f + 1, :].broadcast_to([P, NT, LEAVES]), ALU.add)
            then(last)
            then(v.tensor_tensor(place[:, :, :], place[:, :, :], onehot[:, :, :], ALU.mult))
            then(v.tensor_reduce(pos[:, :], place[:, :, :], AX.X, ALU.add))
            then(v.tensor_copy(token_slot[:, :], pos[:, :]))
            v.tensor_single_scalar(part_i[:, 0:FT], token_slot[:, :], P.bit_length() - 1, ALU.arith_shift_right)
            then(v.tensor_single_scalar(part_i[:, FT:2 * FT], token_slot[:, :], P - 1, ALU.bitwise_and))
            then(v.tensor_copy(part[:, :], part_i[:, :]))
            wide = [P, FT, HI_PAD]
            then(v.tensor_tensor(hi_hot[:, :, :], iota_f[:, 0:HI_PAD].rearrange("p (a n) -> p a n", a=1).broadcast_to(wide),
                                 part[:, 0:FT].rearrange("p (t a) -> p t a", a=1).broadcast_to(wide), ALU.is_equal))
            for f in range(F):
                v.tensor_tensor(hi_tok[:, f * NT:(f + 1) * NT, :], hi_hot[:, f * NT:(f + 1) * NT, :],
                                token_f[:, :].rearrange("p (t a) -> p t a", a=1).broadcast_to([P, NT, HI_PAD]), ALU.mult)
            wide = [P, FT, P]
            v.tensor_tensor(lo_hot[:, :, :], iota_f[:, :].rearrange("p (a n) -> p a n", a=1).broadcast_to(wide),
                            part[:, FT:2 * FT].rearrange("p (t a) -> p t a", a=1).broadcast_to(wide), ALU.is_equal
                            ).then_inc(split_ready, 1)
            for f in range(F):
                wide = [P, HI_PAD, LEAVES]
                last = v.tensor_tensor(leaf_cmp[:, f * HI_PAD:(f + 1) * HI_PAD, :],
                                       iota_f[:, 0:HI_PAD].rearrange("p (n a) -> p n a", a=1).broadcast_to(wide),
                                       ends[:, f:f + 1, :].broadcast_to(wide), ALU.is_ge)
            then(last)
            then(v.tensor_reduce(leaf_f[:, :], leaf_cmp[:, :, :], AX.X, ALU.add))
            then(v.tensor_scalar(leaf_m[:, :], leaf_f[:, :], float(LEAVES - 1), None, ALU.min))
            then(v.tensor_copy(tile_leaf[:, :], leaf_m[:, :]))
            dve.wait_ge(slots_filled, 1)
            v.tensor_copy(slot_index[:, :], pT[1][:, 0:F * HI_PAD]).then_inc(tables_ready, 1)
            dve.wait_ge(tables_ready, 1)

            y_stored = [y_stored0, y_stored1]
            for f in range(F):
                n0 = SLOT_TILES * f
                dve.wait_ge(b1_in, 16 * (f + 1))

                def hidden(j, q):
                    leaf = dve.value_load(tile_leaf[0:1, ds(j + f * HI_PAD, 1)], min_val=0, max_val=LEAVES - 1)
                    dve.wait_ge(h_filled, j + (n0 + 1))
                    v.tensor_tensor(hid[q][:, :], pT[q][:, 0:HID], b1B[f % 2][:, ds(leaf * HID, HID)], ALU.add
                                    ).then_inc(hid_step, 1)
                    dve.wait_ge(hid_step, (j + n0) * 2 + 1)
                    at_least(dve, h_turned, j + (n0 - 1))
                    v.tensor_scalar(hid_parts[q][:, 0:HID], hid[q][:, :], 0.0, None, ALU.max).then_inc(hid_step, 1)
                    dve.wait_ge(hid_step, (j + n0) * 2 + 2)
                    v.scalar_tensor_tensor(hid_parts[q][:, HID:2 * HID], hid[q][:, :], 0.0,
                                           hid_parts[q][:, 0:HID].bitcast(F32), ALU.max, ALU.subtract).then_inc(hid_ready, 1)

                def hidden_one(j, q):
                    dve.wait_ge(hT_ready, j + (n0 + 1))
                    at_least(dve, y_filled, j + (n0 - 1))
                    if isinstance(j, int) and j + n0 == 0:
                        dve.wait_ge(hT_ones, 2)
                    v.tensor_copy(hT_one[q][0:HID, :], hT[q][0:HID, :].bitcast(F32)).then_inc(hT_one_ready, 1)

                def result(j, q):
                    dve.wait_ge(y_filled, j + (n0 + 1))
                    at_least(dve, y_stored[q], (j + (n0 - q)) * 8)
                    v.tensor_copy(y_slot[q][:, :], bank(2 + q)).then_inc(y_ready, 1)

                def step(m, q):
                    edge = isinstance(m, int)
                    if not edge or 1 <= m <= SLOT_TILES:
                        hidden(m - 1, 1 - q)
                    if not edge or 2 <= m <= SLOT_TILES + 1:
                        hidden_one(m - 2, q)
                    if not edge or 3 <= m:
                        result(m - 3, 1 - q)

                walk(dve, step, n0 % 2)

            for b in range(B):
                n0 = b * TQ
                if b == 0:
                    for q in range(2):
                        dve.wait_ge(y_stored[q], 16 * ((F * SLOT_TILES + 1 - q) // 2))

                with dve.Fori(0, TQ) as t:
                    dve.wait_ge(kT_hi_ready, t + (n0 + 1))
                    v.tensor_tensor(kT_lo[b][:, :, ds(t * P, P)], pE[:, :].rearrange("p (k n) -> p k n", k=KD),
                                    kT_hi[b][:, :, ds(t * P, P)].bitcast(F32), ALU.subtract).then_inc(kT_ready, 1)

                def query(n):
                    dve.wait_ge(sq_hi_ready, n + 1)
                    v.tensor_tensor(sq_lo[:, :], pE[:, :], sq_hi[:, :].bitcast(F32), ALU.subtract).then_inc(sq_ready, 1)

                def sprobs_lo(n, j):
                    dve.wait_ge(sPT_hi_ready, n * KBANKS + (j + 1))
                    cols = slice(j * BANK, (j + 1) * BANK)
                    v.tensor_tensor(sPT_lo[:, cols], pT[j % 2][:, :], sPT_hi[:, cols].bitcast(F32), ALU.subtract
                                    ).then_inc(sPT_ready, 1)

                def srow_max(n):
                    dve.wait_ge(s_scored, n + 1)
                    v.tensor_reduce(sraw_max[:, :], pS[:, 0:SQ], AX.X, ALU.max).then_inc(s_raw_max_ready, 1)
                    dve.wait_ge(s_raw_max_ready, n + 1)
                    v.tensor_scalar(sneg_max[:, :], sraw_max[:, :], -SELF_SCALE, None, ALU.mult).then_inc(s_max_ready, 1)

                def result(n):
                    dve.wait_ge(s_exp_ready, n + 1)
                    at_least(dve, out_ready, n)
                    v.reciprocal(sinv_sum[:, :], srow_sum[:, ds(n, 1)]).then_inc(s_inv_ready, 1)
                    dve.wait_ge(s_inv_ready, n + 1)
                    dve.wait_ge(sz_filled, n + 1)
                    dve.wait_ge(mid_in, (n + 1) * 16)
                    at_least(dve, out_stored, n * 16)
                    v.scalar_tensor_tensor(out_tile[:, :], pZ[:, :], sinv_sum[:, 0:1], mid_tile[:, :], ALU.mult, ALU.add
                                           ).then_inc(out_ready, 1)

                def step(n, front, back, more=True):
                    for j in range(KBANKS):
                        if back:
                            sprobs_lo(n - 1, j)
                    if front:
                        srow_max(n)
                        if more:
                            query(n + 1)
                    if back:
                        result(n - 1)

                query(n0)
                step(n0, True, False)
                step(n0 + 1, True, True)
                with dve.Fori(n0 + 2, n0 + TQ - 1) as n:
                    step(n, True, True)
                step(n0 + TQ - 1, True, True, more=False)
                step(n0 + TQ, False, True)

        @block.gpsimd
        def _(pool):
            g = nc.gpsimd
            g.memset(ident[:, :], 0.0).then_inc(ident_zero, 1)
            pool.wait_ge(ident_zero, 1)
            g.affine_select(out=ident[:, :], in_=ident[:, :], compare_op=ALU.not_equal, fill=1.0, base=0,
                            pattern=[[-1, P]], channel_multiplier=1).then_inc(ident_ready, 1)

            g.memset(minus_half[:, :], -0.5).then_inc(half_ready, 1)
            pool.wait_ge(half_ready, 1)

            for b in range(B):
                def context_root(t):
                    root(pool, c_norm_step, (t + TC * b) * 3, c_rooted)

                def low(t, slot):
                    wait_apart(pool, c_hi_ready, t + (TC * b + 1))
                    g.tensor_tensor(ctx_lo[:, ds(t, 1), :], c_norm[slot][:, :], ctx_hi[:, ds(t, 1), :].bitcast(F32),
                                    ALU.subtract).then_inc(c_lo_ready, 1)

                context_root(0)
                context_root(1)
                low(0, 0)
                with pool.Fori(1, TC // 2) as i:
                    context_root(i * 2)
                    low(i * 2 - 1, 1)
                    context_root(i * 2 + 1)
                    low(i * 2, 0)
                low(TC - 1, 1)
                with pool.Fori(b * TQ, (b + 1) * TQ) as n:
                    root(pool, x_norm_step, n * 7, x_rooted)
                    root(pool, x_norm_step, n * 7 + 4, x_rooted)

                def take_query(n, t):
                    at_least(pool, scored, n)
                    g.tensor_copy(q_hi[:, :, :], q_full[:, :, ds(t * P, P)]).then_inc(q_hi_ready, 1)
                    wait_apart(pool, q_hi_ready, n + 1)
                    g.tensor_tensor(q_lo[:, :, :], q_full[:, :, ds(t * P, P)], q_hi[:, :, :].bitcast(F32), ALU.subtract
                                    ).then_inc(q_ready, 1)

                def tail(e):
                    pool.wait_ge(res_in, (e + 1) * 16)
                    at_least(pool, mid_ready, e)
                    g.tensor_tensor(x_resb[:, :], x_res[:, :], out_bias[:, :], ALU.add).then_inc(res_ready, 1)
                    pool.wait_ge(zT_hi_ready, e + 1)
                    g.tensor_tensor(zT_lo[:, :], zT[:, :], zT_hi[:, :].bitcast(F32), ALU.subtract).then_inc(zT_lo_ready, 1)

                def mid_root(e):
                    root(pool, mid_norm_step, e * 3, mid_rooted)

                n0 = b * TQ
                pool.wait_ge(q_full_ready, KC * HALVES * (b + 1))
                take_query(n0, 0)
                take_query(n0 + 1, 1)
                take_query(n0 + 2, 2)
                with pool.Fori(0, TQ - 3) as t:
                    tail(t + n0)
                    take_query(t + (n0 + 3), t + 3)
                    mid_root(t + n0)
                for e in range(n0 + TQ - 3, n0 + TQ):
                    tail(e)
                    mid_root(e)

            pool.wait_ge(nodes_ready, NT)
            pool.wait_ge(norm_stored, 16 * NT)
            pool.wait_ge(mid_stored, 16 * NT)
            g.memset(ones_h[:, :], 1.0).then_inc(route_consts, 1)
            g.memset(before[:, :], 1.0).then_inc(route_consts, 1)
            pool.wait_ge(route_consts, 2)
            g.affine_select(out=before[:, :], in_=before[:, :], compare_op=ALU.is_gt, fill=0.0, base=0,
                            pattern=[[1, P]], channel_multiplier=-1).then_inc(route_consts, 1)
            g.iota(iota_i[:, :], pattern=[[1, P]], base=0, channel_multiplier=0).then_inc(route_consts, 1)
            g.iota(token_i[:, :], pattern=[[P, NT]], base=0, channel_multiplier=1).then_inc(route_consts, 1)

            w2_in = [w2_in0, w2_in1]

            def b2_low(f):
                pool.wait_ge(b2_hi_ready, f + 1)
                g.tensor_tensor(b2_lo[:, :], b2_raw[:, :], b2_hi[:, :].bitcast(F32), ALU.subtract).then_inc(b2_ready, 1)

            def w2_low(f, l, slot):
                wait_apart(pool, w2_hi_ready, l + (f * LEAVES + 1))
                g.tensor_tensor(w2_lo[f % 2][0:HID, ds(l, 1), :], w2_raw[slot][0:HID, :],
                                w2_hi[f % 2][0:HID, ds(l, 1), :].bitcast(F32), ALU.subtract).then_inc(w2_lo_ready, 1)

            pool.wait_ge(route_consts, 5)
            g.memset(w2_lo[0][HID:P, :, :].bitcast(F32), 0.0).then_inc(w2_zeroed, 1)
            pool.wait_ge(w2_zeroed, 1)
            b2_low(0)
            with pool.Fori(0, LEAVES // 2) as i:
                w2_low(0, i * 2, 0)
                w2_low(0, i * 2 + 1, 1)
            pool.wait_ge(tables_ready, 1)
            pool.wait_ge(w2_lo_ready, LEAVES)
            for q in range(2):
                g.memset(hT_one[q][HID:P, :].bitcast(F32), 1.0).then_inc(hT_ones, 1)
                pool.wait_ge(hT_ones, q + 1)
            g.memset(w2_lo[1][HID:P, :, :].bitcast(F32), 0.0).then_inc(w2_zeroed, 1)
            pool.wait_ge(w2_zeroed, 2)
            slot_in = [slot_in0, slot_in1]
            for f in range(F):
                n0 = SLOT_TILES * f

                def gather(j, q):
                    at_least(pool, slot_turned, j + (n0 - 1))
                    at_least(pool, slot_in[q], (j + (n0 - q)) * 8)
                    g.tensor_copy(row_index[q][:, :], slot_index[:, ds(j + f * HI_PAD, 1)]).then_inc(index_ready, 1)
                    wait_apart(pool, index_ready, j + (n0 + 1))
                    g.indirect_dma_start(out=x_slot[q][:, :], out_offset=None, in_=norm_rows,
                                         in_offset=bass.IndirectOffsetOnAxis(ap=row_index[q][:, 0:1], axis=0)
                                         ).then_inc(slot_in[q], 16)

                def step(m, q):
                    if not isinstance(m, int) or m < SLOT_TILES:
                        gather(m, q)

                if f + 1 < F:
                    b2_low(f + 1)
                walk(pool, step, n0 % 2, (lambda l, slot: w2_low(f + 1, l, slot)) if f + 1 < F else None)

            for q, stored in enumerate((y_stored0, y_stored1)):
                pool.wait_ge(stored, 16 * ((F * SLOT_TILES + 1 - q) // 2))

            def rows_of(f, index, rows, index_ready, n, n_index, landed):
                g.tensor_copy(index[:, :], token_slot[:, ds(n + f * NT, 1)]).then_inc(index_ready, 1)
                wait_apart(pool, index_ready, n_index)
                g.indirect_dma_start(out=rows[:, :], out_offset=None, in_=slot_rows[f],
                                     in_offset=bass.IndirectOffsetOnAxis(ap=index[:, 0:1], axis=0)).then_inc(landed, 16)

            for b in range(B):
                n0 = b * TQ

                def keys(t):
                    n = t + n0
                    at_least(pool, sk_turned, n)
                    rows_of(1, kv_index[0], k_rows, kv_index_ready, n, n * 2 + 1, k_in)
                    rows_of(2, kv_index[1], v_rows, kv_index_ready, n, n * 2 + 2, v_in)
                    wait_apart(pool, v_hi_ready, n + 1)
                    g.tensor_tensor(v_lo[b][:, ds(t, 1), :], v_rows[:, :], v_hi[b][:, ds(t, 1), :].bitcast(F32),
                                    ALU.subtract).then_inc(v_ready, 1)
                    pool.wait_ge(v_ready, n + 1)

                def query(n):
                    at_least(pool, sq_turned, n)
                    rows_of(0, kv_index[2], q_rows, q_index_ready, n, n + 1, sq_in)

                keys(0)
                with pool.Fori(1, TQ) as t:
                    keys(t)
                query(n0)
                with pool.Fori(n0 + 1, n0 + TQ) as n:
                    query(n)


_TREES = ["q", "k", "v"]
_LEAF = ["node_w", "node_b", "w1", "b1", "w2", "b2"]
_XATTN = ["ln1_g", "ln1_b", "ln2_g", "ln2_b", "Wq", "bq", "Wk", "bk", "Wv", "bv", "Wo", "bo"]
_INS = ["x", "ctx_768"] + ["L0_xattn_" + n for n in _XATTN] + [f"L0_ffn_{t}_{n}" for t in _TREES for n in _LEAF]
_OUT = ((2, 1024, 512), "float32")


def kernel(**inputs):
    import concourse.bacc as _bacc
    from concourse.bass_utils import run_bass_kernel_spmd as _run

    nc = _bacc.Bacc("TRN2", target_bir_lowering=False, num_devices=1)
    arrays, aps = {}, {}
    for name in _INS:
        a = np.ascontiguousarray(inputs[name])
        arrays[f"in_{name}_dram"] = a
        aps[name] = nc.dram_tensor(f"in_{name}_dram", a.shape, mybir.dt.from_np(a.dtype), kind="ExternalInput").ap()
    out = nc.dram_tensor("out_0_dram", _OUT[0], mybir.dt.from_np(np.dtype(_OUT[1])), kind="ExternalOutput").ap()
    trees = [{n: aps[f"L0_ffn_{t}_{n}"] for n in _LEAF} for t in _TREES]
    build(nc, aps["x"], aps["ctx_768"], *[aps["L0_xattn_" + n] for n in _XATTN], trees, out)
    r = _run(nc, [arrays], core_ids=[0])
    return r.results[0]["out_0_dram"]
```

```python
from contextlib import ExitStack

import numpy as np
import concourse.bass as bass
from concourse import mybir

F32 = mybir.dt.float32
F32R = mybir.dt.float32r
F16 = mybir.dt.float16
I32 = mybir.dt.int32
ALU = mybir.AluOpType
ACT = mybir.ActivationFunctionType
AX = mybir.AxisListType
ds = bass.ds

P = 128
BANK = 512
EPS = 1e-5


def build(nc, x, ctx, ln1_g, ln1_b, ln2_g, ln2_b, Wq, bq, Wk, bk, Wv, bv, Wo, bo, trees, out):
    B, SQ, D = x.shape
    SC, DC = ctx.shape[1:]
    E = Wq.shape[1]
    KD, KC, KE = D // P, DC // P, E // P
    TQ, TC = SQ // P, SC // P
    NT = B * TQ
    NODES, _ = trees[0]["node_w"].shape
    LEAVES, _, HID = trees[0]["w1"].shape
    F = len(trees)
    SLOT_TILES = NT + LEAVES - 1
    HI_PAD = 32
    CROSS_SCALE = float(E) ** -0.5
    SELF_SCALE = float(D) ** -0.5
    XQ_TILES = BANK // P
    HALVES = SQ // BANK
    SBANKS = SC // BANK
    KBANKS = SQ // BANK

    x_rows = x.rearrange("b s d -> (b s) d")
    out_rows = out.rearrange("b s d -> (b s) d")
    ctx_rows = ctx.rearrange("b s d -> (b s) d")
    mid_rows = nc.dram_tensor("mid_rows", [B * SQ, D], F32, kind="Internal").ap()
    norm_rows = nc.dram_tensor("norm_rows", [B * SQ, D], F32, kind="Internal").ap()
    slot_rows = [nc.dram_tensor(f"slot_rows{f}", [SLOT_TILES * P, D], F32, kind="Internal").ap() for f in range(F)]

    top = ExitStack()
    scope = top

    def sb(name, shape, dt=F32):
        return scope.enter_context(nc.sbuf_tensor(name, shape, dt))

    def sem(name):
        return top.enter_context(nc.semaphore(name))

    with top:
        pS = top.enter_context(nc.psum_tensor("pS", [P, 4 * BANK], F32))
        pT = [top.enter_context(nc.psum_tensor(f"pT{i}", [P, BANK], F32)) for i in range(2)]
        pZ = top.enter_context(nc.psum_tensor("pZ", [P, BANK], F32))
        pE = top.enter_context(nc.psum_tensor("pE", [P, BANK], F32))

        def bank(i):
            return pS[:, i * BANK:(i + 1) * BANK]

        ident = sb("ident", [P, P])
        node_scores = sb("node_scores", [P, NT, F * NODES])
        scope = cross_scope = ExitStack()
        ctxT_hi = sb("ctxT_hi", [P, KC, SC], F32R)
        ctxT_lo = sb("ctxT_lo", [P, KC, SC], F32R)
        ctx_hi = sb("ctx_hi", [P, TC, DC], F32R)
        ctx_lo = sb("ctx_lo", [P, TC, DC], F32R)
        M_hi = sb("M_hi", [P, KD, DC], F32R)
        M_lo = sb("M_lo", [P, KD, DC], F32R)
        N_hi = sb("N_hi", [P, KC, D], F32R)
        N_lo = sb("N_lo", [P, KC, D], F32R)
        vectors = ((ln1_g, KD), (ln1_b, KD), (ln2_g, KC), (ln2_b, KC), (bq, KE), (bv, KE))
        NV = sum(k for _, k in vectors)
        columns = sb("columns", [P, NV])
        g1c, b1c, g2c, b2c, bqc, bvc = (
            columns[:, sum(k for _, k in vectors[:i]):sum(k for _, k in vectors[:i + 1])] for i in range(len(vectors)))
        u_col = sb("u_col", [P, KC])
        out_bias = sb("out_bias", [P, D])
        nodeT = sb("nodeT", [P, KD, F * NODES])
        node_bias = sb("node_bias", [P, F * NODES])
        c_raw = [sb(f"c_raw{i}", [P, DC]) for i in range(2)]
        c_norm = [sb(f"c_norm{i}", [P, DC]) for i in range(2)]
        x_raw = [sb(f"x_raw{i}", [P, D]) for i in range(2)]
        x_once = sb("x_once", [P, D])
        x_twice = [sb(f"x_twice{i}", [P, D]) for i in range(2)]
        ln_stats = sb("ln_stats", [P, 6])
        ln_mv = sb("ln_mv", [P, 2])
        ln_var = sb("ln_var", [P, 1])
        ln_rstd = sb("ln_rstd", [P, 1])
        minus_half = sb("minus_half", [P, 1])
        scope = fold_scope = ExitStack()
        wq_raw = sb("wq_raw", [P, KD, E])
        wk_raw = sb("wk_raw", [P, KC, E])
        wv_raw = sb("wv_raw", [P, KC, E])
        wo_raw = sb("wo_raw", [P, KE, D])
        wqT = sb("wqT", [P, KE, D])
        wkT = sb("wkT", [P, KE, DC])
        wvT = sb("wvT", [P, KE, DC])
        M_full = sb("M_full", [P, KD, DC])
        M_gain = sb("M_gain", [P, KD, DC])
        bvB = sb("bvB", [P, KE, P])
        vector_rows = sb("vector_rows", [NV, P])
        node_raw = sb("node_raw", [F * NODES, D])
        fold_scope.close()
        scope = cross_scope
        q_full = sb("q_full", [P, KC, SQ])
        q_hi = sb("q_hi", [P, KC, P], F32R)
        q_lo = sb("q_lo", [P, KC, P], F32R)
        PT_hi = sb("PT_hi", [P, TC * P], F32R)
        PT_lo = sb("PT_lo", [P, TC * P], F32R)
        probs = sb("probs", [P, SC])
        raw_max = sb("raw_max", [P, 1])
        neg_max = sb("neg_max", [P, 1])
        row_sum = sb("row_sum", [P, NT])
        inv_sum = sb("inv_sum", [P, 1])
        z_tile = sb("z_tile", [P, DC])
        zT = sb("zT", [P, DC])
        zT_hi = sb("zT_hi", [P, DC], F32R)
        zT_lo = sb("zT_lo", [P, DC], F32R)
        x_res = sb("x_res", [P, D])
        x_resb = sb("x_resb", [P, D])
        x_mid = sb("x_mid", [P, D])
        x_norm = sb("x_norm", [P, D])
        x_normT = sb("x_normT", [P, D])
        cross_scope.close()
        scope = top
        slot_index = sb("slot_index", [P, F * HI_PAD], I32)
        token_slot = sb("token_slot", [P, F * NT], I32)
        tile_leaf = sb("tile_leaf", [P, F * HI_PAD], I32)
        scope = leaf_scope = ExitStack()
        W1 = KD * HID + 1
        w1, w2_hi, w2_lo, w2_wide, w2_once = [], [], [], [], []

        def leaf_set(i):
            nonlocal scope
            w1.append(sb(f"w1_{i}", [P, LEAVES, W1]))
            scope = incoming_scope = ExitStack()
            w2_wide.append(sb(f"w2_wide{i}", [P, LEAVES, D]))
            w2_once.append(sb(f"w2_once{i}", [P, LEAVES, D]))
            incoming_scope.close()
            scope = leaf_scope
            w2_hi.append(sb(f"w2_hi{i}", [P, LEAVES, D], F32R))
            w2_lo.append(sb(f"w2_lo{i}", [P, LEAVES, D], F32R))

        leaf_set(0)
        b2_raw = sb("b2_raw", [LEAVES, D])
        b2_hi = sb("b2_hi", [LEAVES, D], F32R)
        b2_lo = sb("b2_lo", [LEAVES, D], F32R)
        b1_rows = sb("b1_rows", [LEAVES, 2 * HID])
        set0_words = LEAVES * W1 + 2 * LEAVES * D + 3 * D + 2 * HID
        leaf_set(1)
        row_index = [sb(f"row_index{i}", [P, 1], I32) for i in range(4)]
        x_slot = [sb(f"x_slot{i}", [P, D]) for i in range(4)]
        x_slotT = [sb(f"x_slotT{i}", [P, D]) for i in range(2)]
        w1_leaf = [sb(f"w1_leaf{i}", [P, W1]) for i in range(2)]
        hidden_T = [sb(f"hidden_T{i}", [HID, P]) for i in range(2)]
        hT = [sb(f"hT{i}", [P, P], F32R) for i in range(2)]
        hT_one = [sb(f"hT_one{i}", [P, P], F32R) for i in range(2)]
        y_slot = [sb(f"y_slot{i}", [P, D]) for i in range(2)]
        leaf_scope.close()
        scope = route_scope = ExitStack()
        below_route = sb("below_route", [P, set0_words])
        FT = F * NT
        right = sb("right", [P, FT, NODES])
        reach = [sb(f"reach{k}", [P, FT, 2 ** k]) for k in range(1, 5)]
        onehot = reach[3]
        onehot_h = sb("onehot_h", [P, FT * LEAVES], F16)
        before = sb("before", [P, P], F16)
        ones_h = sb("ones_h", [P, P], F16)
        n_leaf = sb("n_leaf", [P, F * LEAVES], I32)
        n_tiles_i = sb("n_tiles_i", [P, F * LEAVES], I32)
        scan = [sb(f"scan{i}", [P, F, LEAVES]) for i in range(5)]
        n_tiles = sb("n_tiles", [P, F, LEAVES])
        base = sb("base", [P, F, LEAVES])
        place = sb("place", [P, FT, LEAVES])
        pos = sb("pos", [P, FT])
        part_i = sb("part_i", [P, 2 * FT], I32)
        part = sb("part", [P, 2 * FT])
        iota_i = sb("iota_i", [P, P], I32)
        iota_f = sb("iota_f", [P, P])
        token_i = sb("token_i", [P, NT], I32)
        token_f = sb("token_f", [P, NT])
        lo_hot = sb("lo_hot", [P, FT, P], F16)
        hi_hot = sb("hi_hot", [P, FT, HI_PAD])
        hi_tok = sb("hi_tok", [P, FT, HI_PAD], F16)
        leaf_cmp = sb("leaf_cmp", [P, F * HI_PAD, LEAVES])
        leaf_f = sb("leaf_f", [P, F * HI_PAD])
        leaf_m = sb("leaf_m", [P, F * HI_PAD])
        route_scope.close()
        scope = self_scope = ExitStack()
        kT_hi, kT_lo, v_hi, v_lo = [None] * B, [None] * B, [None] * B, [None] * B

        def key_buffers(b):
            kT_hi[b] = sb(f"kT_hi{b}", [P, KD, SQ], F32R)
            kT_lo[b] = sb(f"kT_lo{b}", [P, KD, SQ], F32R)
            v_hi[b] = sb(f"v_hi{b}", [P, TQ, D], F32R)
            v_lo[b] = sb(f"v_lo{b}", [P, TQ, D], F32R)

        key_buffers(1)
        q_rows = sb("q_rows", [P, D])
        sq_hi = sb("sq_hi", [P, D], F32R)
        sq_lo = sb("sq_lo", [P, D], F32R)
        sPT_hi = sb("sPT_hi", [P, SQ], F32R)
        sPT_lo = sb("sPT_lo", [P, SQ], F32R)
        sprobs = sb("sprobs", [P, SQ])
        above_queries = sb("above_queries", [P, set0_words - (2 * KD * SQ + 2 * TQ * D + 3 * D + 3 * SQ)])
        key_buffers(0)
        k_rows = sb("k_rows", [P, D])
        v_rows = sb("v_rows", [P, D])
        kv_index = [sb(f"kv_index{i}", [P, 1], I32) for i in range(2)]
        q_index = sb("q_index", [P, 1], I32)
        sraw_max = sb("sraw_max", [P, 1])
        sneg_max = sb("sneg_max", [P, 1])
        srow_sum = sb("srow_sum", [P, NT])
        sinv_sum = sb("sinv_sum", [P, 1])
        mid_tile = sb("mid_tile", [P, D])
        out_tile = sb("out_tile", [P, D])
        self_scope.close()

        ident_zero = sem("ident_zero")
        ident_ready = sem("ident_ready")
        wq_in = sem("wq_in")
        wk_in = sem("wk_in")
        wv_in = sem("wv_in")
        wo_in = sem("wo_in")
        cols_in = sem("cols_in")
        cols_filled = sem("cols_filled")
        columns_ready = sem("columns_ready")
        node_in = sem("node_in")
        wT_filled = sem("wT_filled")
        wqT_ready = sem("wqT_ready")
        wkT_ready = sem("wkT_ready")
        wvT_ready = sem("wvT_ready")
        node_filled = sem("node_filled")
        nodeT_ready = sem("nodeT_ready")
        M_filled = sem("M_filled")
        M_full_ready = sem("M_full_ready")
        M_gained = sem("M_gained")
        M_hi_ready = sem("M_hi_ready")
        M_ready = sem("M_ready")
        N_filled = sem("N_filled")
        N_hi_ready = sem("N_hi_ready")
        N_ready = sem("N_ready")
        bvB_ready = sem("bvB_ready")
        bias_filled = sem("bias_filled")
        bias_ready = sem("bias_ready")
        c_in0 = sem("c_in0")
        c_in1 = sem("c_in1")
        c_norm_step = sem("c_norm_step")
        c_rooted = sem("c_rooted")
        x_rooted = sem("x_rooted")
        mid_rooted = sem("mid_rooted")
        half_ready = sem("half_ready")
        c_normed = sem("c_normed")
        c_hi_ready = sem("c_hi_ready")
        c_lo_ready = sem("c_lo_ready")
        c_turned = sem("c_turned")
        cT_hi_ready = sem("cT_hi_ready")
        cT_lo_ready = sem("cT_lo_ready")
        x_in0 = sem("x_in0")
        x_in1 = sem("x_in1")
        x_norm_step = sem("x_norm_step")
        x_normed = sem("x_normed")
        x_turned = sem("x_turned")
        xT_hi_ready = sem("xT_hi_ready")
        xT_lo_ready = sem("xT_lo_ready")
        q_filled = sem("q_filled")
        q_full_ready = sem("q_full_ready")
        q_hi_ready = sem("q_hi_ready")
        q_ready = sem("q_ready")
        scored = sem("scored")
        raw_max_ready = sem("raw_max_ready")
        max_ready = sem("max_ready")
        exp_ready = sem("exp_ready")
        probs_turned = sem("probs_turned")
        PT_hi_ready = sem("PT_hi_ready")
        PT_ready = sem("PT_ready")
        z_filled = sem("z_filled")
        inv_ready = sem("inv_ready")
        z_ready = sem("z_ready")
        z_turned = sem("z_turned")
        zT_ready = sem("zT_ready")
        zT_hi_ready = sem("zT_hi_ready")
        zT_lo_ready = sem("zT_lo_ready")
        res_in = sem("res_in")
        res_ready = sem("res_ready")
        o_filled = sem("o_filled")
        mid_ready = sem("mid_ready")
        mid_norm_step = sem("mid_norm_step")
        mid_normed = sem("mid_normed")
        mid_stored = sem("mid_stored")
        norm_stored = sem("norm_stored")
        n_turned = sem("n_turned")
        nT_ready = sem("nT_ready")
        nodes_filled = sem("nodes_filled")
        nodes_ready = sem("nodes_ready")
        route_consts = sem("route_consts")
        route_step = sem("route_step")
        onehots_ready = sem("onehots_ready")
        ranks_filled = sem("ranks_filled")
        split_ready = sem("split_ready")
        slots_filled = sem("slots_filled")
        tables_ready = sem("tables_ready")
        w1_in = sem("w1_in")
        b1_in = sem("b1_in")
        b2_in = sem("b2_in")
        w2_in = sem("w2_in")
        w2_hi_ready = sem("w2_hi_ready")
        w2_lo_ready = sem("w2_lo_ready")
        b2_hi_ready = sem("b2_hi_ready")
        b2_ready = sem("b2_ready")
        b2_placed = sem("b2_placed")
        hT_ones = sem("hT_ones")
        index_ready = sem("index_ready")
        slot_in0 = sem("slot_in0")
        slot_in1 = sem("slot_in1")
        slot_in2 = sem("slot_in2")
        slot_in3 = sem("slot_in3")
        slot_turned = sem("slot_turned")
        slotT_ready = sem("slotT_ready")
        w1_leaf_ready = sem("w1_leaf_ready")
        b1_turned = sem("b1_turned")
        b1_placed = sem("b1_placed")
        h_filled = sem("h_filled")
        hidden_ready = sem("hidden_ready")
        hT_hi_ready = sem("hT_hi_ready")
        hT_ready = sem("hT_ready")
        hT_one_ready = sem("hT_one_ready")
        y_filled = sem("y_filled")
        y_ready = sem("y_ready")
        y_stored0 = sem("y_stored0")
        y_stored1 = sem("y_stored1")
        kv_index_ready = sem("kv_index_ready")
        k_in = sem("k_in")
        v_in = sem("v_in")
        sk_turned = sem("sk_turned")
        kT_hi_ready = sem("kT_hi_ready")
        kT_ready = sem("kT_ready")
        v_hi_ready = sem("v_hi_ready")
        v_ready = sem("v_ready")
        q_index_ready = sem("q_index_ready")
        sq_in = sem("sq_in")
        sq_turned = sem("sq_turned")
        sq_hi_ready = sem("sq_hi_ready")
        sq_ready = sem("sq_ready")
        s_scored = sem("s_scored")
        s_raw_max_ready = sem("s_raw_max_ready")
        s_max_ready = sem("s_max_ready")
        s_exp_ready = sem("s_exp_ready")
        s_turned = sem("s_turned")
        sPT_hi_ready = sem("sPT_hi_ready")
        sPT_ready = sem("sPT_ready")
        sz_filled = sem("sz_filled")
        s_inv_ready = sem("s_inv_ready")
        mid_in = sem("mid_in")
        out_ready = sem("out_ready")
        out_stored = sem("out_stored")
        passed = {nc.vector.engine: sem("vector_passed"), nc.gpsimd.engine: sem("gpsimd_passed")}

        def split_product(pe, dst, left, right, first=True, last=True):
            pe.matmul(dst, left[0], right[0], start=first, stop=False)
            pe.matmul(dst, left[0], right[1], start=False, stop=False)
            return pe.matmul(dst, left[1], right[0], start=False, stop=last)

        def at_least(engine, semaphore, value):
            if not (isinstance(value, int) and value <= 0):
                engine.wait_ge(semaphore, value)

        def wait_apart(engine, semaphore, value):
            engine.wait_ge(semaphore, value)
            if not isinstance(value, int):
                engine.sem_inc(passed[engine.engine], 1)

        def layer_norm(dve, dst, src, step, at, rooted, done):
            nc.vector.bn_stats(ln_stats[:, :], src).then_inc(step, 1)
            wait_apart(dve, step, at + 1)
            nc.vector.bn_aggr(ln_mv[:, :], ln_stats[:, :]).then_inc(step, 1)
            dve.wait_ge(step, at + 2)
            nc.vector.tensor_scalar(ln_var[:, :], ln_mv[:, 1:2], EPS, None, ALU.add).then_inc(step, 1)
            dve.wait_ge(rooted, done)
            return nc.vector.tensor_scalar(dst, src, ln_mv[:, 0:1], ln_rstd[:, 0:1], ALU.subtract, ALU.mult)

        def root(pool, step, at, rooted):
            pool.wait_ge(step, at + 3)
            nc.gpsimd.tensor_tensor(ln_rstd[:, :], ln_var[:, :], minus_half[:, :], ALU.pow).then_inc(rooted, 1)

        def walk(engine, step, n0, split_leaf=None, key_tile=None):

            def turn(i):
                for k in range(4):
                    step(i * 4 + (k + 3), (k + 3 + n0) % 4)
                    if split_leaf and k % 2:
                        split_leaf(i * 2 + k // 2, i)
                    if key_tile and k == 3:
                        key_tile(i)

            for m in range(3):
                step(m, (m + n0) % 4)
            turn(0)
            with engine.Fori(1, TQ - 1) as i:
                turn(i)
            for m in range(SLOT_TILES, SLOT_TILES + 2):
                step(m, (m + n0) % 4)
                if split_leaf:
                    split_leaf(LEAVES - 2 + m - SLOT_TILES, LEAVES // 2 - 1)
                if key_tile and m == SLOT_TILES:
                    key_tile(TQ - 1)

        W2_IN = 3 * 16
        W2_QUADS = LEAVES // 4

        def w2_in_before(f):
            return W2_IN * (W2_QUADS + (f - 1) * (LEAVES // 2 - 1))

        assert SLOT_TILES == 4 * (TQ - 1) + 3 and LEAVES == 2 * TQ and B == 2

        def self_steps(engine, step):
            step(0, 0, None, True)
            step(1, 0, 0, True)
            with engine.Fori(2, TQ) as n:
                step(n, 0, 0, True)
            step(TQ, 1, 0, False)
            with engine.Fori(TQ + 1, NT - 1) as n:
                step(n, 1, 1, False)
            step(NT - 1, 1, 1, False)
            step(NT, None, 1, False)

        block = top.enter_context(nc.Block())

        @block.sync
        def _(sp):
            blocks = "(k p) n -> p k n"
            sp.dma_start(wq_raw[:, :, :], Wq.rearrange(blocks, p=P)).then_inc(wq_in, 16)
            sp.dma_start(wk_raw[:, :, :], Wk.rearrange(blocks, p=P)).then_inc(wk_in, 16)
            row = 0
            for src, k in vectors:
                sp.dma_start(vector_rows[row:row + k, :], src.rearrange("(k p) -> k p", p=P)).then_inc(cols_in, 16)
                row += k
            sp.dma_start(out_bias[:, :], bo.rearrange("(a n) -> a n", a=1).broadcast_to([P, D])).then_inc(cols_in, 16)
            for f, tree in enumerate(trees):
                own = slice(f * NODES, (f + 1) * NODES)
                sp.dma_start(node_raw[own, :], tree["node_w"]).then_inc(node_in, 16)
                sp.dma_start(node_bias[:, own], tree["node_b"].rearrange("(a n) -> a n", a=1).broadcast_to([P, NODES])
                             ).then_inc(node_in, 16)
            sp.dma_start(wv_raw[:, :, :], Wv.rearrange(blocks, p=P)).then_inc(wv_in, 16)
            sp.dma_start(wo_raw[:, :, :], Wo.rearrange(blocks, p=P)).then_inc(wo_in, 16)

            def context_in(b):
                c_in = [c_in0, c_in1]

                def load(t, slot):
                    at_least(sp, c_normed, t + (b * TC - 1))
                    sp.dma_start(c_raw[slot][:, :], ctx_rows[ds((t + b * TC) * P, P), :]).then_inc(c_in[slot], 16)

                load(0, 0)
                load(1, 1)
                with sp.Fori(1, TC // 2) as i:
                    load(i * 2, 0)
                    load(i * 2 + 1, 1)

            def query_in(b):
                x_in = [x_in0, x_in1]

                def load(t, slot):
                    at_least(sp, x_normed, t + (b * TQ - 1))
                    sp.dma_start(x_raw[slot][:, :], x_rows[ds((t + b * TQ) * P, P), :]).then_inc(x_in[slot], 16)
                load(0, 0)
                load(1, 1)
                with sp.Fori(1, TQ // 2) as i:
                    load(i * 2, 0)
                    load(i * 2 + 1, 1)

            def cross_tail(b):
                sp.wait_ge(M_ready, 1)
                sp.wait_ge(N_ready, 1)
                sp.wait_ge(bias_ready, 1)
                with sp.Fori(b * TQ, (b + 1) * TQ) as n:
                    sp.dma_start(x_res[:, :], x_rows[ds(n * P, P), :]).then_inc(res_in, 16)
                    sp.wait_ge(mid_ready, n + 1)
                    sp.dma_start(mid_rows[ds(n * P, P), :], x_mid[:, :]).then_inc(mid_stored, 16)
                    sp.wait_ge(mid_normed, n + 1)
                    sp.dma_start(norm_rows[ds(n * P, P), :], x_norm[:, :]).then_inc(norm_stored, 16)

            for b in range(B):
                context_in(b)
                query_in(b)
                cross_tail(b)

            def leaf_w2(f, l, n):
                src = trees[f]["w2"][ds(l, n), :, :].rearrange("l h n -> h l n")
                for dst in (w2_wide[f % 2][0:HID], w2_wide[f % 2][HID:P], w2_once[f % 2][0:HID]):
                    sp.dma_start(dst[:, ds(l, n), :], src).then_inc(w2_in, 16)

            def leaf_weights(f):
                tree = trees[f]
                if f == 0:
                    sp.wait_ge(nodes_ready, NT)
                    sp.wait_ge(norm_stored, 16 * NT)
                    sp.wait_ge(mid_stored, 16 * NT)
                else:
                    sp.wait_ge(tables_ready, 1)
                    sp.wait_ge(b2_placed, 32 * f)
                    sp.wait_ge(w2_lo_ready, LEAVES * f)
                    sp.wait_ge(b1_placed, f)
                if f >= 2:
                    sp.wait_ge(y_filled, SLOT_TILES * (f - 1))
                    sp.wait_ge(w1_leaf_ready, SLOT_TILES * (f - 1))
                sp.dma_start(b2_raw[:, :], tree["b2"]).then_inc(b2_in, 16)
                leaf_w2(f, 0, 4)
                for k in range(KD):
                    sp.dma_start(w1[f % 2][:, :, k * HID:(k + 1) * HID],
                                 tree["w1"][:, k * P:(k + 1) * P, :].rearrange("l p h -> p l h")).then_inc(w1_in, 16)
                for half in range(2):
                    sp.dma_start(b1_rows[:, half * HID:(half + 1) * HID], tree["b1"]).then_inc(b1_in, 16)
                if f == 0:
                    for quad in range(1, W2_QUADS):
                        sp.wait_ge(w2_in, W2_IN * quad)
                        leaf_w2(0, quad * 4, 4)
                sp.wait_ge(b2_ready, f + 1)
                for row, src in ((HID, b2_hi), (HID + 1, b2_lo)):
                    sp.dma_start(w2_lo[f % 2][row:row + 1, :, :].rearrange("a l n -> a (l n)").bitcast(F32),
                                 src[:, :].bitcast(F32)).then_inc(b2_placed, 16)

            leaf_weights(0)
            y_stored = [y_stored0, y_stored1]
            for f in range(F):
                odd = SLOT_TILES * f % 2

                def store(j, slot):
                    sp.wait_ge(y_ready, j + (SLOT_TILES * f + 1))
                    sp.dma_start(slot_rows[f][ds(j * P, P), :], y_slot[slot][:, :]).then_inc(y_stored[slot], 16)

                if f + 1 < F:
                    leaf_weights(f + 1)
                store(0, odd)
                store(1, 1 - odd)
                with sp.Fori(0, LEAVES // 2 - 2) as i:
                    for k in range(2):
                        store(i * 4 + (2 * k + 2), odd)
                        store(i * 4 + (2 * k + 3), 1 - odd)
                    if f + 1 < F:
                        sp.wait_ge(w2_in, i * W2_IN + (w2_in_before(f + 1) + W2_IN))
                        leaf_w2(f + 1, i * 2 + 4, 2)
                for j in range((LEAVES // 2 - 2) * 4 + 2, SLOT_TILES):
                    store(j, (j + odd) % 2)

            for q in range(2):
                sp.wait_ge(y_stored[q], 16 * ((F * SLOT_TILES + 1 - q) // 2))
            with sp.Fori(0, NT) as n:
                sp.dma_start(mid_tile[:, :], mid_rows[ds(n * P, P), :]).then_inc(mid_in, 16)
                sp.wait_ge(out_ready, n + 1)
                sp.dma_start(out_rows[ds(n * P, P), :], out_tile[:, :]).then_inc(out_stored, 16)
            sp.wait_ge(out_stored, 16 * NT)
            sp.wait_ge(mid_stored, 16 * NT)
            sp.wait_ge(norm_stored, 16 * NT)

        @block.tensor
        def _(pe):
            pe.wait_ge(ident_ready, 1)

            def turn_weights(raw, kin, dst_bank):
                for e in range(KE):
                    for k in range(kin):
                        last = pe.transpose(dst_bank(e)[:, k * P:(k + 1) * P], raw[:, k, e * P:(e + 1) * P], ident[:, :])
                    last.then_inc(wT_filled, 1)

            pe.wait_ge(wq_in, 16)
            turn_weights(wq_raw, KD, bank)
            pe.wait_ge(cols_in, 16 * (len(vectors) + 1))
            pe.transpose(pE[:, 0:NV], vector_rows[:, :], ident[0:NV, 0:NV]).then_inc(cols_filled, 1)
            pe.wait_ge(wk_in, 16)
            pe.wait_ge(columns_ready, 1)
            turn_weights(wk_raw, KC, lambda e: (pT[0], pT[1], pZ, pE)[e])
            pe.wait_ge(wv_in, 16)
            pe.wait_ge(wqT_ready, KE)
            turn_weights(wv_raw, KC, bank)
            pe.wait_ge(wkT_ready, KE)
            pe.wait_ge(node_in, 16 * 2 * F)
            for k in range(KD):
                last = pe.transpose(pE[:, k * F * NODES:(k + 1) * F * NODES], node_raw[:, k * P:(k + 1) * P],
                                    ident[0:F * NODES, 0:F * NODES])
            last.then_inc(node_filled, 1)
            m_bank = (pT[0], pT[1], pZ, pT[0])
            for k in range(KD):
                if k == 3:
                    pe.wait_ge(M_full_ready, 1)
                for e in range(KE):
                    last = pe.matmul(m_bank[k][:, 0:DC], wqT[:, e, k * P:(k + 1) * P], wkT[:, e, :],
                                     start=e == 0, stop=e == KE - 1)
                last.then_inc(M_filled, 1)
            pe.wait_ge(wvT_ready, KE)
            pe.wait_ge(wo_in, 16)
            for c in range(KC):
                for e in range(KE):
                    last = pe.matmul(bank(c), wvT[:, e, c * P:(c + 1) * P], wo_raw[:, e, :], start=e == 0, stop=e == KE - 1)
                last.then_inc(N_filled, 1)
            pe.wait_ge(bvB_ready, 1)
            for e in range(KE):
                pe.matmul(bank(3), bvB[:, e, :], wo_raw[:, e, :], start=e == 0, stop=e == KE - 1)
            pe.wait_ge(nodeT_ready, 1)
            pe.wait_ge(M_full_ready, KD)
            for c in range(KC):
                for e in range(KE):
                    pe.matmul(pE[:, c:c + 1], wkT[:, e, c * P:(c + 1) * P], bqc[:, e:e + 1], start=e == 0, stop=False)
                for k in range(KD):
                    last = pe.matmul(pE[:, c:c + 1], M_full[:, k, c * P:(c + 1) * P], b1c[:, k:k + 1],
                                     start=False, stop=k == KD - 1)
            last.then_inc(bias_filled, 1)

            def turn_context(b):
                if b:
                    pe.wait_ge(PT_ready, SBANKS * TQ * b)
                def turn(t, slot):
                    pe.wait_ge(c_normed, t + (TC * b + 1))
                    at_least(pe, cT_lo_ready, t + (TC * b - 1))
                    for k in range(KC):
                        last = pe.transpose(pT[slot][:, k * P:(k + 1) * P], c_norm[slot][:, k * P:(k + 1) * P], ident[:, :])
                    last.then_inc(c_turned, 1)
                turn(0, 0)
                turn(1, 1)
                with pe.Fori(1, TC // 2) as i:
                    turn(i * 2, 0)
                    turn(i * 2 + 1, 1)

            def project_queries(b):
                pe.wait_ge(cT_lo_ready, TC * (b + 1))
                pe.wait_ge(M_ready, 1)
                pe.wait_ge(N_ready, 1)
                pe.wait_ge(bias_ready, 1)
                for h in range(HALVES):
                    for tt in range(XQ_TILES):
                        n = b * TQ + h * XQ_TILES + tt
                        pe.wait_ge(x_normed, n + 1)
                        if n % TQ >= 2:
                            pe.wait_ge(xT_lo_ready, n - 1)
                        for k in range(KD):
                            last = pe.transpose(pT[tt % 2][:, k * P:(k + 1) * P], x_twice[tt % 2][:, k * P:(k + 1) * P],
                                                ident[:, :])
                        last.then_inc(x_turned, 1)
                    pe.wait_ge(xT_lo_ready, b * TQ + (h + 1) * XQ_TILES)
                    if h:
                        pe.wait_ge(q_full_ready, KC * (b * HALVES + h))
                    xT_hi = PT_hi[:, :].rearrange("p (k n) -> p k n", k=KD)
                    xT_lo = PT_lo[:, :].rearrange("p (k n) -> p k n", k=KD)
                    for c in range(KC):
                        cols = slice(c * P, (c + 1) * P)
                        for k in range(KD):
                            last = split_product(pe, bank(c), (M_hi[:, k, cols], M_lo[:, k, cols]),
                                                 (xT_hi[:, k, :], xT_lo[:, k, :]), k == 0, k == KD - 1)
                        last.then_inc(q_filled, 1)

            def cross(b):
                n0 = b * TQ

                def turn_probs(n, j):
                    pe.wait_ge(exp_ready, n + 1)
                    at_least(pe, PT_ready, n * SBANKS + (j - 1))
                    for k in range(4):
                        blk = (4 * j + k) * P
                        last = pe.transpose(pT[j % 2][:, k * P:(k + 1) * P], probs[:, blk:blk + P], ident[:, :])
                    last.then_inc(probs_turned, 1)

                def score(n, j):
                    if j == 0:
                        pe.wait_ge(q_ready, n + 1)
                    for c in range(KC):
                        last = split_product(pe, bank(j), (q_hi[:, c, :], q_lo[:, c, :]),
                                             (ctxT_hi[:, c, j * BANK:(j + 1) * BANK], ctxT_lo[:, c, j * BANK:(j + 1) * BANK]),
                                             c == 0, c == KC - 1)
                    if j == SBANKS - 1:
                        last.then_inc(scored, 1)

                def weigh(n, part, parts=4):
                    if part == 0:
                        pe.wait_ge(PT_ready, n * SBANKS + SBANKS)
                        at_least(pe, z_ready, n)
                    for t in range(part * TC // parts, (part + 1) * TC // parts):
                        last = split_product(pe, pZ[:, 0:DC], (PT_hi[:, t * P:(t + 1) * P], PT_lo[:, t * P:(t + 1) * P]),
                                             (ctx_hi[:, t, :], ctx_lo[:, t, :]), t == 0, t == TC - 1)
                    if part == parts - 1:
                        last.then_inc(z_filled, 1)

                def turn_z(e):
                    pe.wait_ge(z_ready, e + 1)
                    at_least(pe, nodes_ready, e)
                    for c in range(KC):
                        last = pe.transpose(pE[:, c * P:(c + 1) * P], z_tile[:, c * P:(c + 1) * P], ident[:, :])
                    last.then_inc(z_turned, 1)

                def project_out(e):
                    pe.wait_ge(zT_lo_ready, e + 1)
                    for c in range(KC):
                        cols = slice(c * P, (c + 1) * P)
                        last = split_product(pe, pE[:, :], (zT_hi[:, cols], zT_lo[:, cols]), (N_hi[:, c, :], N_lo[:, c, :]),
                                             c == 0, c == KC - 1)
                    last.then_inc(o_filled, 1)

                def turn_norm(e):
                    pe.wait_ge(mid_normed, e + 1)
                    for k in range(KD):
                        last = pe.transpose(pE[:, k * P:(k + 1) * P], x_norm[:, k * P:(k + 1) * P], ident[:, :])
                    last.then_inc(n_turned, 1)

                def score_nodes(e):
                    pe.wait_ge(nT_ready, e + 1)
                    for k in range(KD):
                        last = pe.matmul(pE[:, 0:F * NODES], x_normT[:, k * P:(k + 1) * P], nodeT[:, k, :],
                                         start=k == 0, stop=k == KD - 1)
                    last.then_inc(nodes_filled, 1)

                def step(n, front, back, tail):
                    for j in range(SBANKS):
                        if back:
                            turn_probs(n - 1, j)
                        if tail and j == 3:
                            project_out(n - 2)
                        if front:
                            score(n, j)
                        if tail and j == 0:
                            turn_z(n - 2)
                    for part in range(4):
                        if back:
                            weigh(n - 1, part)
                        if tail and part == 1:
                            turn_norm(n - 2)
                        if tail and part == 2:
                            score_nodes(n - 2)

                step(n0, True, False, False)
                step(n0 + 1, True, True, False)
                with pe.Fori(n0 + 2, n0 + TQ) as n:
                    step(n, True, True, True)
                step(n0 + TQ, False, True, True)
                step(n0 + TQ + 1, False, False, True)

            for b in range(B):
                turn_context(b)
                project_queries(b)
                cross(b)

            pe.wait_ge(route_consts, 3)
            W = NT * LEAVES
            for f in range(F):
                pe.wait_ge(onehots_ready, 1)
                oh = onehot_h[:, f * W:(f + 1) * W]
                for back in range(1, NT):
                    pe.matmul(bank(f)[:, back * LEAVES:W], ones_h[:, :], oh[:, 0:W - back * LEAVES],
                              start=back == 1, stop=False, skip_group_check=True)
                pe.matmul(bank(f)[:, 0:W], before[:, :], oh, start=False, stop=True, skip_group_check=True)
                for t in range(NT):
                    last = pe.matmul(pT[0][:, f * LEAVES:(f + 1) * LEAVES], ones_h[:, :],
                                     oh[:, t * LEAVES:(t + 1) * LEAVES], start=t == 0, stop=t == NT - 1)
            last.then_inc(ranks_filled, 1)
            for f in range(F):
                pe.wait_ge(split_ready, 1)
                for t in range(NT):
                    last = pe.matmul(pT[1][:, f * HI_PAD:(f + 1) * HI_PAD], lo_hot[:, f * NT + t, :],
                                     hi_tok[:, f * NT + t, :], start=t == 0, stop=t == NT - 1)
            last.then_inc(slots_filled, 1)
            pe.wait_ge(tables_ready, 1)

            for f in range(F):
                n0 = SLOT_TILES * f
                slot_in = [slot_in0, slot_in1, slot_in2, slot_in3]
                pe.wait_ge(b1_in, 32 * (f + 1))
                pe.transpose(pE[:, 0:LEAVES], b1_rows[:, :], ident[0:LEAVES, 0:LEAVES]).then_inc(b1_turned, 1)

                def turn_rows(j, q):
                    pe.wait_ge(slot_in[q], (j + (n0 + 4 - q)) * 4)
                    at_least(pe, slotT_ready, j + (n0 - 1))
                    for k in range(KD):
                        last = pe.transpose(bank(q % 2)[:, k * P:(k + 1) * P], x_slot[q][:, k * P:(k + 1) * P], ident[:, :])
                    last.then_inc(slot_turned, 1)

                def first_layer(j, q):
                    pe.wait_ge(slotT_ready, j + (n0 + 1))
                    pe.wait_ge(w1_leaf_ready, j + (n0 + 1))
                    at_least(pe, hidden_ready, j + (n0 - 1))
                    for k in range(KD):
                        last = pe.matmul(pT[q][0:HID, 0:P], w1_leaf[q][:, k * HID:(k + 1) * HID],
                                         x_slotT[q][:, k * P:(k + 1) * P], start=k == 0, stop=k == KD - 1)
                    last.then_inc(h_filled, 1)

                def second_layer(j, q):
                    leaf = pe.value_load(tile_leaf[0:1, ds(j + f * HI_PAD, 1)], min_val=0, max_val=LEAVES - 1)
                    pe.wait_ge(hT_ready, j + (n0 + 1))
                    pe.wait_ge(hT_one_ready, j + (n0 + 1))
                    at_least(pe, y_ready, j + (n0 - 1))
                    pe.matmul(bank(2 + q), hT[q][:, :], w2_hi[f % 2][:, ds(leaf, 1), :], start=True, stop=False)
                    pe.matmul(bank(2 + q), hT_one[q][0:HID + 2, :], w2_lo[f % 2][0:HID + 2, ds(leaf, 1), :],
                              start=False, stop=True).then_inc(y_filled, 1)

                def step(m, q):
                    edge = isinstance(m, int)
                    if not edge or m < SLOT_TILES:
                        turn_rows(m, q)
                    if not edge or 1 <= m <= SLOT_TILES:
                        first_layer(m - 1, (q + 1) % 2)
                    if edge and m == 2:
                        pe.wait_ge(w2_lo_ready, LEAVES * (f + 1))
                        pe.wait_ge(b2_placed, 32 * (f + 1))
                        pe.wait_ge(hT_ones, 2)
                    if not edge or 2 <= m:
                        second_layer(m - 2, q % 2)

                def turn_keys(t):
                    pe.wait_ge(k_in, (t + 1) * 16)
                    if isinstance(t, int) and t == 0:
                        pe.wait_ge(b1_placed, F)
                    at_least(pe, kT_ready, t)
                    for k in range(KD):
                        last = pe.transpose(pE[:, k * P:(k + 1) * P], k_rows[:, k * P:(k + 1) * P], ident[:, :])
                    last.then_inc(sk_turned, 1)

                walk(pe, step, n0, key_tile=turn_keys if f == F - 1 else None)

            def turn_query(n):
                pe.wait_ge(sq_in, (n + 1) * 16)
                for k in range(KD):
                    last = pe.transpose(pE[:, k * P:(k + 1) * P], q_rows[:, k * P:(k + 1) * P], ident[:, :])
                last.then_inc(sq_turned, 1)

            def sturn(n, j):
                pe.wait_ge(s_exp_ready, n + 1)
                at_least(pe, sPT_ready, n * KBANKS + (j - 1))
                for k in range(4):
                    blk = (4 * j + k) * P
                    last = pe.transpose(pT[j % 2][:, k * P:(k + 1) * P], sprobs[:, blk:blk + P], ident[:, :])
                last.then_inc(s_turned, 1)

            def sscore(n, j, b):
                if j == 0:
                    pe.wait_ge(sq_ready, n + 1)
                for k in range(KD):
                    cols = slice(k * P, (k + 1) * P)
                    keys = slice(j * BANK, (j + 1) * BANK)
                    last = split_product(pe, bank(j), (sq_hi[:, cols], sq_lo[:, cols]),
                                         (kT_hi[b][:, k, keys], kT_lo[b][:, k, keys]), k == 0, k == KD - 1)
                if j == KBANKS - 1:
                    last.then_inc(s_scored, 1)

            def sweigh(n, half, b):
                if half == 0:
                    pe.wait_ge(sPT_ready, n * KBANKS + KBANKS)
                    at_least(pe, out_ready, n)
                for t in range(half * TQ // 2, (half + 1) * TQ // 2):
                    last = split_product(pe, pZ[:, :], (sPT_hi[:, t * P:(t + 1) * P], sPT_lo[:, t * P:(t + 1) * P]),
                                         (v_hi[b][:, t, :], v_lo[b][:, t, :]), t == 0, t == TQ - 1)
                if half:
                    last.then_inc(sz_filled, 1)

            def step(n, front, back, key):
                if isinstance(n, int) and n in (0, TQ):
                    pe.wait_ge(kT_ready, n + TQ)
                    pe.wait_ge(v_ready, n + TQ)
                for j in range(KBANKS):
                    if back is not None:
                        sturn(n - 1, j)
                    if front is not None:
                        sscore(n, j, front)
                if not isinstance(n, int) or n + 1 < NT:
                    if key:
                        pe.wait_ge(kT_ready, n + TQ)
                    pe.wait_ge(sq_ready, n + 1)
                    turn_query(n + 1)
                if back is not None:
                    sweigh(n - 1, 0, back)
                if key:
                    pe.wait_ge(sq_ready, n + 2)
                    turn_keys(n + TQ)
                if back is not None:
                    sweigh(n - 1, 1, back)

            pe.wait_ge(kT_ready, TQ)
            turn_query(0)
            pe.wait_ge(sq_ready, 1)
            self_steps(pe, step)

        @block.scalar
        def _(act):
            for e in range(KE):
                act.wait_ge(wT_filled, e + 1)
                nc.scalar.copy(wqT[:, e, :], bank(e)).then_inc(wqT_ready, 1)
            for e in range(KE):
                act.wait_ge(wT_filled, 2 * KE + e + 1)
                nc.scalar.copy(wvT[:, e, :], bank(e)[:, 0:DC]).then_inc(wvT_ready, 1)
            m_bank = (pT[0], pT[1], pZ, pT[0])
            for k in range(KD):
                act.wait_ge(M_filled, k + 1)
                nc.scalar.copy(M_full[:, k, :], m_bank[k][:, 0:DC]).then_inc(M_full_ready, 1)
            for c in range(KC):
                act.wait_ge(N_filled, c + 1)
                nc.scalar.copy(N_hi[:, c, :], bank(c)).then_inc(N_hi_ready, 1)
            act.wait_ge(M_gained, KD)
            nc.scalar.copy(M_hi[:, :, :], M_gain[:, :, :]).then_inc(M_hi_ready, 1)

            def context(b):
                if b:
                    act.wait_ge(z_filled, TQ * b)

                def split(t, slot):
                    act.wait_ge(c_normed, t + (TC * b + 1))
                    nc.scalar.copy(ctx_hi[:, ds(t, 1), :], c_norm[slot][:, :]).then_inc(c_hi_ready, 1)
                    act.wait_ge(c_turned, t + (TC * b + 1))
                    nc.scalar.copy(ctxT_hi[:, :, ds(t * P, P)], pT[slot][:, 0:DC].rearrange("p (k n) -> p k n", k=KC)
                                   ).then_inc(cT_hi_ready, 1)

                with act.Fori(0, TC // 2) as i:
                    split(i * 2, 0)
                    split(i * 2 + 1, 1)

            def queries(b):
                for h in range(HALVES):
                    if h:
                        act.wait_ge(q_filled, KC * (b * HALVES + h))
                    xT_hi = PT_hi[:, :].rearrange("p (k n) -> p k n", k=KD)
                    for tt in range(XQ_TILES):
                        n = b * TQ + h * XQ_TILES + tt
                        act.wait_ge(x_turned, n + 1)
                        if n == 0:
                            act.wait_ge(M_ready, 1)
                            act.wait_ge(N_ready, 1)
                            act.wait_ge(bias_ready, 1)
                        nc.scalar.copy(xT_hi[:, :, tt * P:(tt + 1) * P], pT[tt % 2][:, :].rearrange("p (k n) -> p k n", k=KD)
                                       ).then_inc(xT_hi_ready, 1)

            def cross(b):
                n0 = b * TQ

                def probs_hi(n, j, first=False):
                    act.wait_ge(probs_turned, n * SBANKS + (j + 1))
                    if j == 0:
                        if first:
                            act.wait_ge(q_filled, KC * HALVES * (b + 1))
                        else:
                            act.wait_ge(z_filled, n)
                    nc.scalar.copy(PT_hi[:, j * BANK:(j + 1) * BANK], pT[j % 2][:, :]).then_inc(PT_hi_ready, 1)

                def exp(n):
                    act.wait_ge(max_ready, n + 1)
                    at_least(act, probs_turned, n * SBANKS)
                    nc.scalar.activation(probs[:, :], pS[:, 0:SC], ACT.Exp, bias=neg_max[:, 0:1], scale=CROSS_SCALE,
                                         accum_out=row_sum[:, ds(n, 1)]).then_inc(exp_ready, 1)

                def z_hi(e):
                    act.wait_ge(zT_ready, (e + 1) * KC)
                    nc.scalar.copy(zT_hi[:, :], zT[:, :]).then_inc(zT_hi_ready, 1)

                def norm_T(e):
                    act.wait_ge(n_turned, e + 1)
                    nc.scalar.copy(x_normT[:, :], pE[:, :]).then_inc(nT_ready, 1)

                def step(n, front, back, tail, first=False):
                    for j in range(SBANKS):
                        if back:
                            probs_hi(n - 1, j, first)
                        if tail and j == 1:
                            z_hi(n - 2)
                    if front:
                        exp(n)
                    if tail:
                        norm_T(n - 2)

                step(n0, True, False, False)
                step(n0 + 1, True, True, False, first=True)
                with act.Fori(n0 + 2, n0 + TQ) as n:
                    step(n, True, True, True)
                step(n0 + TQ, False, True, True)
                step(n0 + TQ + 1, False, False, True)

            for b in range(B):
                context(b)
                queries(b)
                cross(b)

            def b2_high(f):
                act.wait_ge(b2_in, 16 * (f + 1))
                nc.scalar.copy(b2_hi[:, :], b2_raw[:, :]).then_inc(b2_hi_ready, 1)

            def w2_high(f, l, i):
                landed = W2_IN if isinstance(i, int) and i == 0 else i * W2_IN
                act.wait_ge(w2_in, landed + w2_in_before(f))
                nc.scalar.copy(w2_hi[f % 2][:, ds(l, 1), :], w2_wide[f % 2][:, ds(l, 1), :]).then_inc(w2_hi_ready, 1)

            def key_high(t, t0=0):
                b = t0 // TQ
                act.wait_ge(sk_turned, t + (t0 + 1))
                nc.scalar.copy(kT_hi[b][:, :, ds(t * P, P)], pE[:, :].rearrange("p (k n) -> p k n", k=KD)
                               ).then_inc(kT_hi_ready, 1)
                act.wait_ge(v_in, (t + (t0 + 1)) * 16)
                nc.scalar.copy(v_hi[b][:, ds(t, 1), :], v_rows[:, :]).then_inc(v_hi_ready, 1)

            b2_high(0)
            for quad in range(W2_QUADS):
                own = slice(quad * 4, quad * 4 + 4)
                act.wait_ge(w2_in, W2_IN * (quad + 1))
                nc.scalar.copy(w2_hi[0][:, own, :], w2_wide[0][:, own, :]).then_inc(w2_hi_ready, 4)
            for f in range(F):
                n0 = SLOT_TILES * f

                def take_w1(j, q):
                    leaf = act.value_load(tile_leaf[0:1, ds(j + f * HI_PAD, 1)], min_val=0, max_val=LEAVES - 1)
                    at_least(act, h_filled, j + (n0 - 1))
                    at_least(act, hidden_ready, j + (n0 - 1))
                    nc.scalar.copy(w1_leaf[q][:, :], w1[f % 2][:, ds(leaf, 1), :]).then_inc(w1_leaf_ready, 1)

                def rows_T(j, q):
                    act.wait_ge(slot_turned, j + (n0 + 1))
                    at_least(act, h_filled, j + (n0 - 1))
                    nc.scalar.copy(x_slotT[q][:, :], bank(q)).then_inc(slotT_ready, 1)

                def hidden_one(j, q):
                    act.wait_ge(hidden_ready, j + (n0 + 1))
                    at_least(act, y_filled, j + (n0 - 1))
                    if isinstance(j, int) and j + n0 == 0:
                        act.wait_ge(hT_ones, 2)
                    nc.scalar.copy(hT_one[q][0:HID, :], hidden_T[q][:, :]).then_inc(hT_one_ready, 1)

                def step(m, q):
                    edge = isinstance(m, int)
                    if not edge or m < SLOT_TILES:
                        take_w1(m, q % 2)
                        rows_T(m, q % 2)
                    if not edge or 1 <= m <= SLOT_TILES:
                        hidden_one(m - 1, (q + 1) % 2)

                act.wait_ge(w1_in, 16 * KD * (f + 1))
                act.wait_ge(b1_placed, f + 1)
                if f == 0:
                    act.wait_ge(tables_ready, 1)
                if f + 1 < F:
                    b2_high(f + 1)
                walk(act, step, n0, (lambda l, i: w2_high(f + 1, l, i)) if f + 1 < F else None,
                     key_high if f == F - 1 else None)

            def query(n):
                act.wait_ge(sq_turned, n + 1)
                at_least(act, s_scored, n)
                nc.scalar.copy(sq_hi[:, :], pE[:, :]).then_inc(sq_hi_ready, 1)

            def sprobs_hi(n, j):
                act.wait_ge(s_turned, n * KBANKS + (j + 1))
                if j == 0:
                    at_least(act, sz_filled, n)
                nc.scalar.copy(sPT_hi[:, j * BANK:(j + 1) * BANK], pT[j % 2][:, :]).then_inc(sPT_hi_ready, 1)

            def sexp(n):
                act.wait_ge(s_max_ready, n + 1)
                at_least(act, s_turned, n * KBANKS)
                nc.scalar.activation(sprobs[:, :], pS[:, 0:SQ], ACT.Exp, bias=sneg_max[:, 0:1], scale=SELF_SCALE,
                                     accum_out=srow_sum[:, ds(n, 1)]).then_inc(s_exp_ready, 1)

            def step(n, front, back, key):
                for j in range(KBANKS):
                    if back is not None:
                        sprobs_hi(n - 1, j)
                if front is not None:
                    sexp(n)
                    if not isinstance(n, int) or n + 1 < NT:
                        query(n + 1)
                if key:
                    key_high(n, TQ)

            query(0)
            self_steps(act, step)

        @block.vector
        def _(dve):
            dve.wait_ge(cols_filled, 1)
            nc.vector.tensor_copy(columns[:, :], pE[:, 0:NV]).then_inc(columns_ready, 1)
            dve.wait_ge(columns_ready, 1)
            for e in range(KE):
                last = nc.vector.tensor_copy(bvB[:, e, :], bvc[:, e:e + 1].broadcast_to([P, P]))
            last.then_inc(bvB_ready, 1)
            for e in range(KE):
                dve.wait_ge(wT_filled, KE + e + 1)
                nc.vector.tensor_copy(wkT[:, e, :], (pT[0], pT[1], pZ, pE)[e][:, 0:DC]).then_inc(wkT_ready, 1)
            dve.wait_ge(node_filled, 1)
            nc.vector.tensor_copy(nodeT[:, :, :].rearrange("p k n -> p (k n)"), pE[:, 0:KD * F * NODES]).then_inc(nodeT_ready, 1)
            for k in range(KD):
                dve.wait_ge(M_full_ready, k + 1)
                nc.vector.tensor_scalar(M_gain[:, k, :], M_full[:, k, :], g1c[:, k:k + 1], None, ALU.mult).then_inc(M_gained, 1)
            dve.wait_ge(M_hi_ready, 1)
            nc.vector.tensor_tensor(M_lo[:, :, :], M_gain[:, :, :], M_hi[:, :, :].bitcast(F32), ALU.subtract).then_inc(M_ready, 1)
            for c in range(KC):
                dve.wait_ge(N_hi_ready, c + 1)
                last = nc.vector.tensor_tensor(N_lo[:, c, :], bank(c), N_hi[:, c, :].bitcast(F32), ALU.subtract)
            last.then_inc(N_ready, 1)
            dve.wait_ge(bias_filled, 1)
            nc.vector.tensor_copy(u_col[:, :], pE[:, 0:KC])
            nc.vector.tensor_tensor(out_bias[:, :], bank(3), out_bias[:, :], ALU.add).then_inc(bias_ready, 1)

            def context(b):
                c_in = [c_in0, c_in1]
                n0 = TC * b

                def norm(t, slot):
                    dve.wait_ge(c_in[slot], (t + (n0 + 2 - slot)) * 8)
                    at_least(dve, c_lo_ready, t + (n0 - 1))
                    at_least(dve, c_turned, t + (n0 - 1))
                    layer_norm(dve, c_norm[slot][:, :], c_raw[slot][:, :], c_norm_step, (t + n0) * 3,
                               c_rooted, t + (n0 + 1)).then_inc(c_normed, 1)

                def low(t, slot):
                    dve.wait_ge(cT_hi_ready, t + (n0 + 1))
                    nc.vector.tensor_tensor(ctxT_lo[:, :, ds(t * P, P)], pT[slot][:, 0:DC].rearrange("p (k n) -> p k n", k=KC),
                                            ctxT_hi[:, :, ds(t * P, P)].bitcast(F32), ALU.subtract).then_inc(cT_lo_ready, 1)

                norm(0, 0)
                norm(1, 1)
                low(0, 0)
                with dve.Fori(1, TC // 2) as i:
                    norm(i * 2, 0)
                    low(i * 2 - 1, 1)
                    norm(i * 2 + 1, 1)
                    low(i * 2, 0)
                low(TC - 1, 1)

            def queries(b):
                x_in = [x_in0, x_in1]
                xT_hi = PT_hi[:, :].rearrange("p (k n) -> p k n", k=KD)
                xT_lo = PT_lo[:, :].rearrange("p (k n) -> p k n", k=KD)

                def low(n):
                    q, cols = n % 2, slice(n % XQ_TILES * P, (n % XQ_TILES + 1) * P)
                    dve.wait_ge(xT_hi_ready, n + 1)
                    nc.vector.tensor_tensor(xT_lo[:, :, cols], pT[q][:, :].rearrange("p (k n) -> p k n", k=KD),
                                            xT_hi[:, :, cols].bitcast(F32), ALU.subtract).then_inc(xT_lo_ready, 1)

                for h in range(HALVES):
                    for tt in range(XQ_TILES):
                        n = b * TQ + h * XQ_TILES + tt
                        q = n % 2
                        dve.wait_ge(x_in[q], 16 * (n // 2 + 1))
                        layer_norm(dve, x_once[:, :], x_raw[q][:, :], x_norm_step, 7 * n,
                                   x_rooted, 2 * n + 1).then_inc(x_norm_step, 1)
                        dve.wait_ge(x_norm_step, 7 * n + 4)
                        at_least(dve, x_turned, n - 1)
                        layer_norm(dve, x_twice[q][:, :], x_once[:, :], x_norm_step, 7 * n + 4,
                                   x_rooted, 2 * n + 2).then_inc(x_normed, 1)
                        if tt:
                            low(n - 1)
                    low(n)
                    for c in range(KC):
                        dve.wait_ge(q_filled, KC * (b * HALVES + h) + c + 1)
                        if b and c == h == 0:
                            dve.wait_ge(q_ready, TQ * b)
                        nc.vector.tensor_scalar(q_full[:, c, h * BANK:(h + 1) * BANK], bank(c), u_col[:, c:c + 1],
                                                g2c[:, c:c + 1], ALU.add, ALU.mult).then_inc(q_full_ready, 1)

            def cross(b):
                n0 = b * TQ

                def probs_lo(n, j):
                    dve.wait_ge(PT_hi_ready, n * SBANKS + (j + 1))
                    cols = slice(j * BANK, (j + 1) * BANK)
                    nc.vector.tensor_tensor(PT_lo[:, cols], pT[j % 2][:, :], PT_hi[:, cols].bitcast(F32), ALU.subtract
                                            ).then_inc(PT_ready, 1)

                def row_max(n):
                    dve.wait_ge(scored, n + 1)
                    nc.vector.tensor_reduce(raw_max[:, :], pS[:, 0:SC], AX.X, ALU.max).then_inc(raw_max_ready, 1)
                    dve.wait_ge(raw_max_ready, n + 1)
                    nc.vector.tensor_scalar(neg_max[:, :], raw_max[:, :], -CROSS_SCALE, None, ALU.mult).then_inc(max_ready, 1)

                def normalise(n):
                    dve.wait_ge(exp_ready, n + 1)
                    nc.vector.reciprocal(inv_sum[:, :], row_sum[:, ds(n, 1)]).then_inc(inv_ready, 1)
                    dve.wait_ge(inv_ready, n + 1)
                    dve.wait_ge(z_filled, n + 1)
                    at_least(dve, z_turned, n)
                    nc.vector.tensor_scalar(z_tile[:, :], pZ[:, 0:DC], inv_sum[:, 0:1], None, ALU.mult).then_inc(z_ready, 1)

                def affine(e):
                    dve.wait_ge(z_turned, e + 1)
                    at_least(dve, zT_lo_ready, e)
                    for c in range(KC):
                        cols = slice(c * P, (c + 1) * P)
                        nc.vector.tensor_scalar(zT[:, cols], pE[:, cols], g2c[:, c:c + 1], b2c[:, c:c + 1],
                                                ALU.mult, ALU.add).then_inc(zT_ready, 1)

                def residual(e):
                    dve.wait_ge(o_filled, e + 1)
                    dve.wait_ge(res_ready, e + 1)
                    at_least(dve, mid_stored, e * 16)
                    nc.vector.tensor_tensor(x_mid[:, :], pE[:, :], x_resb[:, :], ALU.add).then_inc(mid_ready, 1)

                def norm_mid(e):
                    dve.wait_ge(mid_ready, e + 1)
                    at_least(dve, norm_stored, e * 16)
                    at_least(dve, n_turned, e)
                    layer_norm(dve, x_norm[:, :], x_mid[:, :], mid_norm_step, e * 3,
                               mid_rooted, e + 1).then_inc(mid_normed, 1)

                def nodes(e):
                    dve.wait_ge(nodes_filled, e + 1)
                    nc.vector.tensor_tensor(node_scores[:, ds(e, 1), :], pE[:, 0:F * NODES], node_bias[:, :], ALU.add
                                            ).then_inc(nodes_ready, 1)

                def step(n, front, back, tail):
                    for j in range(SBANKS):
                        if back:
                            probs_lo(n - 1, j)
                        if tail and j == 1:
                            affine(n - 2)
                    if tail:
                        residual(n - 2)
                    if front:
                        row_max(n)
                    if tail:
                        norm_mid(n - 2)
                        nodes(n - 2)
                    if back:
                        normalise(n - 1)

                step(n0, True, False, False)
                step(n0 + 1, True, True, False)
                with dve.Fori(n0 + 2, n0 + TQ) as n:
                    step(n, True, True, True)
                step(n0 + TQ, False, True, True)
                step(n0 + TQ + 1, False, False, True)

            for b in range(B):
                context(b)
                queries(b)
                cross(b)

            count = [0]

            def then(instruction):
                count[0] += 1
                instruction.then_inc(route_step, 1)
                dve.wait_ge(route_step, count[0])

            v = nc.vector
            dve.wait_ge(norm_stored, 16 * NT)
            dve.wait_ge(mid_stored, 16 * NT)
            dve.wait_ge(nodes_ready, NT)
            then(v.tensor_scalar(right[:, :, :].rearrange("p (f t) n -> p t f n", f=F),
                                 node_scores[:, :, :].rearrange("p t (f n) -> p t f n", f=F), 0.0, None, ALU.is_ge))
            for k in range(len(reach)):
                wide = reach[k][:, :, :].rearrange("p t (n side) -> p t n side", side=2)
                own = right[:, :, 2 ** k - 1:2 ** (k + 1) - 1]
                if k == 0:
                    v.tensor_copy(wide[:, :, :, 1], own)
                    then(v.tensor_scalar(wide[:, :, :, 0], own, -1.0, 1.0, ALU.mult, ALU.add))
                else:
                    then(v.tensor_tensor(wide[:, :, :, 1], reach[k - 1][:, :, :], own, ALU.mult))
                    then(v.tensor_tensor(wide[:, :, :, 0], reach[k - 1][:, :, :], wide[:, :, :, 1], ALU.subtract))
            v.tensor_copy(onehot_h[:, :], onehot[:, :, :].rearrange("p t l -> p (t l)")).then_inc(onehots_ready, 1)
            dve.wait_ge(route_consts, 5)
            v.tensor_copy(iota_f[:, :], iota_i[:, :])
            then(v.tensor_copy(token_f[:, :], token_i[:, :]))
            dve.wait_ge(ranks_filled, 1)
            then(v.tensor_scalar(n_leaf[:, :], pT[0][:, 0:F * LEAVES], float(P - 1), None, ALU.add))
            then(v.tensor_single_scalar(n_tiles_i[:, :], n_leaf[:, :], P.bit_length() - 1, ALU.arith_shift_right))
            then(v.tensor_copy(n_tiles[:, :, :].rearrange("p f l -> p (f l)"), n_tiles_i[:, :]))
            src = n_tiles
            for k in range(4):
                d = 2 ** k
                v.tensor_copy(scan[k][:, :, 0:d], src[:, :, 0:d])
                then(v.tensor_tensor(scan[k][:, :, d:], src[:, :, d:], src[:, :, 0:LEAVES - d], ALU.add))
                src = scan[k]
            ends = src
            then(v.tensor_tensor(scan[4][:, :, :], ends[:, :, :], n_tiles[:, :, :], ALU.subtract))
            then(v.tensor_scalar(base[:, :, :], scan[4][:, :, :], float(P), None, ALU.mult))
            for f in range(F):
                own = place[:, f * NT:(f + 1) * NT, :]
                last = v.tensor_tensor(own, bank(f)[:, 0:NT * LEAVES].rearrange("p (t l) -> p t l", t=NT),
                                       base[:, f:f + 1, :].broadcast_to([P, NT, LEAVES]), ALU.add)
            then(last)
            then(v.tensor_tensor(place[:, :, :], place[:, :, :], onehot[:, :, :], ALU.mult))
            then(v.tensor_reduce(pos[:, :], place[:, :, :], AX.X, ALU.add))
            then(v.tensor_copy(token_slot[:, :], pos[:, :]))
            v.tensor_single_scalar(part_i[:, 0:FT], token_slot[:, :], P.bit_length() - 1, ALU.arith_shift_right)
            then(v.tensor_single_scalar(part_i[:, FT:2 * FT], token_slot[:, :], P - 1, ALU.bitwise_and))
            then(v.tensor_copy(part[:, :], part_i[:, :]))
            wide = [P, FT, HI_PAD]
            then(v.tensor_tensor(hi_hot[:, :, :], iota_f[:, 0:HI_PAD].rearrange("p (a n) -> p a n", a=1).broadcast_to(wide),
                                 part[:, 0:FT].rearrange("p (t a) -> p t a", a=1).broadcast_to(wide), ALU.is_equal))
            for f in range(F):
                v.tensor_tensor(hi_tok[:, f * NT:(f + 1) * NT, :], hi_hot[:, f * NT:(f + 1) * NT, :],
                                token_f[:, :].rearrange("p (t a) -> p t a", a=1).broadcast_to([P, NT, HI_PAD]), ALU.mult)
            wide = [P, FT, P]
            v.tensor_tensor(lo_hot[:, :, :], iota_f[:, :].rearrange("p (a n) -> p a n", a=1).broadcast_to(wide),
                            part[:, FT:2 * FT].rearrange("p (t a) -> p t a", a=1).broadcast_to(wide), ALU.is_equal
                            ).then_inc(split_ready, 1)
            for f in range(F):
                wide = [P, HI_PAD, LEAVES]
                last = v.tensor_tensor(leaf_cmp[:, f * HI_PAD:(f + 1) * HI_PAD, :],
                                       iota_f[:, 0:HI_PAD].rearrange("p (n a) -> p n a", a=1).broadcast_to(wide),
                                       ends[:, f:f + 1, :].broadcast_to(wide), ALU.is_ge)
            then(last)
            then(v.tensor_reduce(leaf_f[:, :], leaf_cmp[:, :, :], AX.X, ALU.add))
            then(v.tensor_scalar(leaf_m[:, :], leaf_f[:, :], float(LEAVES - 1), None, ALU.min))
            then(v.tensor_copy(tile_leaf[:, :], leaf_m[:, :]))
            dve.wait_ge(slots_filled, 1)
            v.tensor_copy(slot_index[:, :], pT[1][:, 0:F * HI_PAD]).then_inc(tables_ready, 1)
            dve.wait_ge(tables_ready, 1)

            y_stored = [y_stored0, y_stored1]

            def key_low(t, t0=0):
                b = t0 // TQ
                dve.wait_ge(kT_hi_ready, t + (t0 + 1))
                v.tensor_tensor(kT_lo[b][:, :, ds(t * P, P)], pE[:, :].rearrange("p (k n) -> p k n", k=KD),
                                kT_hi[b][:, :, ds(t * P, P)].bitcast(F32), ALU.subtract).then_inc(kT_ready, 1)
                dve.wait_ge(v_hi_ready, t + (t0 + 1))
                v.tensor_tensor(v_lo[b][:, ds(t, 1), :], v_rows[:, :], v_hi[b][:, ds(t, 1), :].bitcast(F32), ALU.subtract
                                ).then_inc(v_ready, 1)

            for f in range(F):
                n0 = SLOT_TILES * f
                dve.wait_ge(b1_turned, f + 1)
                dve.wait_ge(w1_in, 16 * KD * (f + 1))
                v.tensor_copy(w1[f % 2][:, :, KD * HID], pE[:, 0:LEAVES]).then_inc(b1_placed, 1)

                def hidden(j, q):
                    dve.wait_ge(h_filled, j + (n0 + 1))
                    at_least(dve, hT_one_ready, j + (n0 - 1))
                    v.tensor_scalar(hidden_T[q][:, :], pT[q][0:HID, 0:P], w1_leaf[q][0:HID, KD * HID:W1], 0.0,
                                    ALU.add, ALU.max).then_inc(hidden_ready, 1)
                    dve.wait_ge(hidden_ready, j + (n0 + 1))
                    at_least(dve, y_filled, j + (n0 - 1))
                    v.tensor_copy(hT[q][0:HID, :], hidden_T[q][:, :]).then_inc(hT_hi_ready, 1)
                    dve.wait_ge(hT_hi_ready, j + (n0 + 1))
                    v.tensor_tensor(hT[q][HID:P, :], hidden_T[q][:, :], hT[q][0:HID, :].bitcast(F32), ALU.subtract
                                    ).then_inc(hT_ready, 1)

                def result(j, q):
                    dve.wait_ge(y_filled, j + (n0 + 1))
                    at_least(dve, y_stored[q], (j + (n0 - q)) * 8)
                    v.tensor_copy(y_slot[q][:, :], bank(2 + q)).then_inc(y_ready, 1)

                def step(m, q):
                    edge = isinstance(m, int)
                    if not edge or 1 <= m <= SLOT_TILES:
                        hidden(m - 1, (q + 1) % 2)
                    if not edge or 2 <= m:
                        result(m - 2, q % 2)

                def w2_low(l, i):
                    dve.wait_ge(w2_hi_ready, l + ((f + 1) * LEAVES + 1))
                    v.tensor_tensor(w2_lo[(f + 1) % 2][0:HID, ds(l, 1), :], w2_once[(f + 1) % 2][0:HID, ds(l, 1), :],
                                    w2_hi[(f + 1) % 2][0:HID, ds(l, 1), :].bitcast(F32),
                                    ALU.subtract).then_inc(w2_lo_ready, 1)

                if f + 1 < F:
                    dve.wait_ge(b2_hi_ready, f + 2)
                    v.tensor_tensor(b2_lo[:, :], b2_raw[:, :], b2_hi[:, :].bitcast(F32), ALU.subtract).then_inc(b2_ready, 1)
                walk(dve, step, n0, w2_low if f + 1 < F else None, key_low if f == F - 1 else None)

            for q in range(2):
                dve.wait_ge(y_stored[q], 16 * ((F * SLOT_TILES + 1 - q) // 2))

            def query(n):
                dve.wait_ge(sq_hi_ready, n + 1)
                v.tensor_tensor(sq_lo[:, :], pE[:, :], sq_hi[:, :].bitcast(F32), ALU.subtract).then_inc(sq_ready, 1)

            def sprobs_lo(n, j):
                dve.wait_ge(sPT_hi_ready, n * KBANKS + (j + 1))
                cols = slice(j * BANK, (j + 1) * BANK)
                v.tensor_tensor(sPT_lo[:, cols], pT[j % 2][:, :], sPT_hi[:, cols].bitcast(F32), ALU.subtract
                                ).then_inc(sPT_ready, 1)

            def srow_max(n):
                dve.wait_ge(s_scored, n + 1)
                v.tensor_reduce(sraw_max[:, :], pS[:, 0:SQ], AX.X, ALU.max).then_inc(s_raw_max_ready, 1)
                dve.wait_ge(s_raw_max_ready, n + 1)
                v.tensor_scalar(sneg_max[:, :], sraw_max[:, :], -SELF_SCALE, None, ALU.mult).then_inc(s_max_ready, 1)

            def result(n):
                dve.wait_ge(s_exp_ready, n + 1)
                at_least(dve, out_ready, n)
                v.reciprocal(sinv_sum[:, :], srow_sum[:, ds(n, 1)]).then_inc(s_inv_ready, 1)
                dve.wait_ge(s_inv_ready, n + 1)
                dve.wait_ge(sz_filled, n + 1)
                dve.wait_ge(mid_in, (n + 1) * 16)
                at_least(dve, out_stored, n * 16)
                v.scalar_tensor_tensor(out_tile[:, :], pZ[:, :], sinv_sum[:, 0:1], mid_tile[:, :], ALU.mult, ALU.add
                                       ).then_inc(out_ready, 1)

            def step(n, front, back, key):
                for j in range(KBANKS):
                    if back is not None:
                        sprobs_lo(n - 1, j)
                if front is not None:
                    srow_max(n)
                    if not isinstance(n, int) or n + 1 < NT:
                        query(n + 1)
                if key:
                    key_low(n, TQ)
                if back is not None:
                    result(n - 1)

            query(0)
            self_steps(dve, step)

        @block.gpsimd
        def _(pool):
            g = nc.gpsimd
            g.memset(ident[:, :], 0.0).then_inc(ident_zero, 1)
            pool.wait_ge(ident_zero, 1)
            g.affine_select(out=ident[:, :], in_=ident[:, :], compare_op=ALU.not_equal, fill=1.0, base=0,
                            pattern=[[-1, P]], channel_multiplier=1).then_inc(ident_ready, 1)

            g.memset(minus_half[:, :], -0.5).then_inc(half_ready, 1)
            pool.wait_ge(half_ready, 1)

            for b in range(B):
                def context_root(t):
                    root(pool, c_norm_step, (t + TC * b) * 3, c_rooted)

                def low(t, slot):
                    wait_apart(pool, c_hi_ready, t + (TC * b + 1))
                    g.tensor_tensor(ctx_lo[:, ds(t, 1), :], c_norm[slot][:, :], ctx_hi[:, ds(t, 1), :].bitcast(F32),
                                    ALU.subtract).then_inc(c_lo_ready, 1)

                context_root(0)
                context_root(1)
                low(0, 0)
                with pool.Fori(1, TC // 2) as i:
                    context_root(i * 2)
                    low(i * 2 - 1, 1)
                    context_root(i * 2 + 1)
                    low(i * 2, 0)
                low(TC - 1, 1)
                with pool.Fori(b * TQ, (b + 1) * TQ) as n:
                    root(pool, x_norm_step, n * 7, x_rooted)
                    root(pool, x_norm_step, n * 7 + 4, x_rooted)

                def take_query(n, t):
                    at_least(pool, scored, n)
                    g.tensor_copy(q_hi[:, :, :], q_full[:, :, ds(t * P, P)]).then_inc(q_hi_ready, 1)
                    wait_apart(pool, q_hi_ready, n + 1)
                    g.tensor_tensor(q_lo[:, :, :], q_full[:, :, ds(t * P, P)], q_hi[:, :, :].bitcast(F32), ALU.subtract
                                    ).then_inc(q_ready, 1)

                def tail(e):
                    pool.wait_ge(res_in, (e + 1) * 16)
                    at_least(pool, mid_ready, e)
                    g.tensor_tensor(x_resb[:, :], x_res[:, :], out_bias[:, :], ALU.add).then_inc(res_ready, 1)
                    pool.wait_ge(zT_hi_ready, e + 1)
                    g.tensor_tensor(zT_lo[:, :], zT[:, :], zT_hi[:, :].bitcast(F32), ALU.subtract).then_inc(zT_lo_ready, 1)

                def mid_root(e):
                    root(pool, mid_norm_step, e * 3, mid_rooted)

                n0 = b * TQ
                pool.wait_ge(q_full_ready, KC * HALVES * (b + 1))
                take_query(n0, 0)
                take_query(n0 + 1, 1)
                take_query(n0 + 2, 2)
                with pool.Fori(0, TQ - 3) as t:
                    tail(t + n0)
                    take_query(t + (n0 + 3), t + 3)
                    mid_root(t + n0)
                for e in range(n0 + TQ - 3, n0 + TQ):
                    tail(e)
                    mid_root(e)

            pool.wait_ge(nodes_ready, NT)
            pool.wait_ge(norm_stored, 16 * NT)
            pool.wait_ge(mid_stored, 16 * NT)
            g.memset(ones_h[:, :], 1.0).then_inc(route_consts, 1)
            g.memset(before[:, :], 1.0).then_inc(route_consts, 1)
            pool.wait_ge(route_consts, 2)
            g.affine_select(out=before[:, :], in_=before[:, :], compare_op=ALU.is_gt, fill=0.0, base=0,
                            pattern=[[1, P]], channel_multiplier=-1).then_inc(route_consts, 1)
            g.iota(iota_i[:, :], pattern=[[1, P]], base=0, channel_multiplier=0).then_inc(route_consts, 1)
            g.iota(token_i[:, :], pattern=[[P, NT]], base=0, channel_multiplier=1).then_inc(route_consts, 1)

            pool.wait_ge(route_consts, 5)
            pool.wait_ge(b2_hi_ready, 1)
            g.tensor_tensor(b2_lo[:, :], b2_raw[:, :], b2_hi[:, :].bitcast(F32), ALU.subtract).then_inc(b2_ready, 1)
            for quad in range(W2_QUADS):
                own = slice(quad * 4, quad * 4 + 4)
                pool.wait_ge(w2_hi_ready, 4 * (quad + 1))
                g.tensor_tensor(w2_lo[0][0:HID, own, :], w2_once[0][0:HID, own, :], w2_hi[0][0:HID, own, :].bitcast(F32), ALU.subtract
                                ).then_inc(w2_lo_ready, 4)
            pool.wait_ge(tables_ready, 1)
            pool.wait_ge(w2_lo_ready, LEAVES)
            for q in range(2):
                g.memset(hT_one[q][HID:HID + 2, :].bitcast(F32), 1.0).then_inc(hT_ones, 1)
                pool.wait_ge(hT_ones, q + 1)
            slot_in = [slot_in0, slot_in1, slot_in2, slot_in3]

            def rows_of(f, index, rows, index_ready, n, n_index, landed):
                g.tensor_copy(index[:, :], token_slot[:, ds(n + f * NT, 1)]).then_inc(index_ready, 1)
                wait_apart(pool, index_ready, n_index)
                g.indirect_dma_start(out=rows[:, :], out_offset=None, in_=slot_rows[f],
                                     in_offset=bass.IndirectOffsetOnAxis(ap=index[:, 0:1], axis=0)).then_inc(landed, 16)

            def gather_keys(t, t0=0):
                n = t + t0
                if isinstance(n, int) and n == 0:
                    for q, stored in enumerate((y_stored0, y_stored1)):
                        pool.wait_ge(stored, 16 * ((2 * SLOT_TILES + 1 - q) // 2))
                at_least(pool, sk_turned, n)
                rows_of(0, kv_index[0], k_rows, kv_index_ready, n, n * 2 + 1, k_in)
                at_least(pool, v_ready, n)
                rows_of(1, kv_index[1], v_rows, kv_index_ready, n, n * 2 + 2, v_in)

            for f in range(F):
                n0 = SLOT_TILES * f

                def gather(j, q):
                    at_least(pool, slot_turned, j + (n0 - 3))
                    at_least(pool, slot_in[q], (j + (n0 - q)) * 4)
                    g.tensor_copy(row_index[q][:, :], slot_index[:, ds(j + f * HI_PAD, 1)]).then_inc(index_ready, 1)
                    wait_apart(pool, index_ready, j + (n0 + 1))
                    g.indirect_dma_start(out=x_slot[q][:, :], out_offset=None, in_=norm_rows,
                                         in_offset=bass.IndirectOffsetOnAxis(ap=row_index[q][:, 0:1], axis=0)
                                         ).then_inc(slot_in[q], 16)

                def step(m, q):
                    if not isinstance(m, int) or m < SLOT_TILES:
                        gather(m, q)

                walk(pool, step, n0, key_tile=gather_keys if f == F - 1 else None)

            for q, stored in enumerate((y_stored0, y_stored1)):
                pool.wait_ge(stored, 16 * ((F * SLOT_TILES + 1 - q) // 2))

            def gather_query(n):
                at_least(pool, sq_turned, n)
                rows_of(F - 1, q_index, q_rows, q_index_ready, n, n + 1, sq_in)

            gather_query(0)
            with pool.Fori(0, TQ) as n:
                gather_query(n + 1)
                gather_keys(n, TQ)
            with pool.Fori(TQ + 1, NT) as n:
                gather_query(n)


_TREES = ["k", "v", "q"]
_LEAF = ["node_w", "node_b", "w1", "b1", "w2", "b2"]
_XATTN = ["ln1_g", "ln1_b", "ln2_g", "ln2_b", "Wq", "bq", "Wk", "bk", "Wv", "bv", "Wo", "bo"]
_INS = ["x", "ctx_768"] + ["L0_xattn_" + n for n in _XATTN] + [f"L0_ffn_{t}_{n}" for t in _TREES for n in _LEAF]
_OUT = ((2, 1024, 512), "float32")


def kernel(**inputs):
    import concourse.bacc as _bacc
    from concourse.bass_utils import run_bass_kernel_spmd as _run

    nc = _bacc.Bacc("TRN2", target_bir_lowering=False, num_devices=1)
    arrays, aps = {}, {}
    for name in _INS:
        a = np.ascontiguousarray(inputs[name])
        arrays[f"in_{name}_dram"] = a
        aps[name] = nc.dram_tensor(f"in_{name}_dram", a.shape, mybir.dt.from_np(a.dtype), kind="ExternalInput").ap()
    out = nc.dram_tensor("out_0_dram", _OUT[0], mybir.dt.from_np(np.dtype(_OUT[1])), kind="ExternalOutput").ap()
    trees = [{n: aps[f"L0_ffn_{t}_{n}"] for n in _LEAF} for t in _TREES]
    build(nc, aps["x"], aps["ctx_768"], *[aps["L0_xattn_" + n] for n in _XATTN], trees, out)
    r = _run(nc, [arrays], core_ids=[0])
    return r.results[0]["out_0_dram"]
```

```python
from contextlib import ExitStack

import numpy as np
import concourse.bass as bass
from concourse import mybir

F32 = mybir.dt.float32
F32R = mybir.dt.float32r
F16 = mybir.dt.float16
I32 = mybir.dt.int32
ALU = mybir.AluOpType
ACT = mybir.ActivationFunctionType
AX = mybir.AxisListType
ds = bass.ds

P = 128
BANK = 512
EPS = 1e-5


def build(nc, x, ctx, ln1_g, ln1_b, ln2_g, ln2_b, Wq, bq, Wk, bk, Wv, bv, Wo, bo, trees, out):
    B, SQ, D = x.shape
    SC, DC = ctx.shape[1:]
    E = Wq.shape[1]
    KD, KC, KE = D // P, DC // P, E // P
    TQ, TC = SQ // P, SC // P
    NT = B * TQ
    NODES, _ = trees[0]["node_w"].shape
    LEAVES, _, HID = trees[0]["w1"].shape
    F = len(trees)
    SLOT_TILES = NT + LEAVES - 1
    HI_PAD = 32
    CROSS_SCALE = float(E) ** -0.5
    SELF_SCALE = float(D) ** -0.5
    SBANKS = SC // BANK
    KBANKS = SQ // BANK

    x_rows = x.rearrange("b s d -> (b s) d")
    out_rows = out.rearrange("b s d -> (b s) d")
    ctx_rows = ctx.rearrange("b s d -> (b s) d")
    mid_rows = nc.dram_tensor("mid_rows", [B * SQ, D], F32, kind="Internal").ap()
    norm_rows = nc.dram_tensor("norm_rows", [B * SQ, D], F32, kind="Internal").ap()
    slot_rows = [nc.dram_tensor(f"slot_rows{f}", [SLOT_TILES * P, D], F32, kind="Internal").ap() for f in range(F)]

    top = ExitStack()
    scope = top

    def sb(name, shape, dt=F32):
        return scope.enter_context(nc.sbuf_tensor(name, shape, dt))

    def sem(name):
        return top.enter_context(nc.semaphore(name))

    with top:
        pS = top.enter_context(nc.psum_tensor("pS", [P, 4 * BANK], F32))
        pT = [top.enter_context(nc.psum_tensor(f"pT{i}", [P, BANK], F32)) for i in range(2)]
        pZ = top.enter_context(nc.psum_tensor("pZ", [P, BANK], F32))
        pE = top.enter_context(nc.psum_tensor("pE", [P, BANK], F32))

        def bank(i):
            return pS[:, i * BANK:(i + 1) * BANK]

        ident = sb("ident", [P, P])
        node_scores = sb("node_scores", [P, NT, F * NODES])
        slot_index = sb("slot_index", [P, F * HI_PAD], I32)
        token_slot = sb("token_slot", [P, F * NT], I32)
        tile_leaf = sb("tile_leaf", [P, F * HI_PAD], I32)
        W1 = KD * HID + 1
        scope = cross_scope = ExitStack()
        ctxT_hi = sb("ctxT_hi", [P, KC, SC], F32R)
        ctxT_lo = sb("ctxT_lo", [P, KC, SC], F32R)
        past_w2 = sb("past_w2", [P, max(0, LEAVES * (W1 + D) - 2 * KC * SC)])
        ctx_hi = sb("ctx_hi", [P, TC, DC], F32R)
        ctx_lo = sb("ctx_lo", [P, TC, DC], F32R)
        M_hi = sb("M_hi", [P, KD, DC], F32R)
        M_lo = sb("M_lo", [P, KD, DC], F32R)
        N_hi = sb("N_hi", [P, KC, D], F32R)
        N_lo = sb("N_lo", [P, KC, D], F32R)
        vectors = ((ln1_g, KD), (ln1_b, KD), (ln2_g, KC), (ln2_b, KC), (bq, KE), (bv, KE))
        NV = sum(k for _, k in vectors)
        columns = sb("columns", [P, NV])
        g1c, b1c, g2c, b2c, bqc, bvc = (
            columns[:, sum(k for _, k in vectors[:i]):sum(k for _, k in vectors[:i + 1])] for i in range(len(vectors)))
        u_gain = sb("u_gain", [P, DC])
        out_bias = sb("out_bias", [P, D])
        nodeT = sb("nodeT", [P, KD, F * NODES])
        node_bias = sb("node_bias", [P, F * NODES])
        c_raw = [sb(f"c_raw{i}", [P, DC]) for i in range(4)]
        c_stats = [sb(f"c_stats{i}", [P, 6]) for i in range(2)]
        c_moments = [sb(f"c_moments{i}", [P, 2]) for i in range(2)]
        c_mean = sb("c_mean", [P, B * TC])
        c_var = sb("c_var", [P, B * TC])
        c_rstd = sb("c_rstd", [P, B * TC])
        x_raw = sb("x_raw", [P, D])
        x_hat = sb("x_hat", [P, D])
        x_stats, mid_stats = sb("x_stats", [P, 6]), sb("mid_stats", [P, 6])
        x_moments, mid_moments = sb("x_moments", [P, 2]), sb("mid_moments", [P, 2])
        x_var, mid_var = sb("x_var", [P, 1]), sb("mid_var", [P, 1])
        x_rstd, mid_rstd = sb("x_rstd", [P, 1]), sb("mid_rstd", [P, 1])
        minus_half = sb("minus_half", [P, B * TC])
        scope = fold_scope = ExitStack()
        wq_raw = sb("wq_raw", [P, KD, E])
        wk_raw = sb("wk_raw", [P, KC, E])
        wv_raw = sb("wv_raw", [P, KC, E])
        wo_raw = sb("wo_raw", [P, KE, D])
        wqT = sb("wqT", [P, KE, D])
        wkT = sb("wkT", [P, KE, DC])
        wvT = sb("wvT", [P, KE, DC])
        M_full = sb("M_full", [P, KD, DC])
        M_gain = wqT[:, 0:KD, 0:DC]
        bvB = sb("bvB", [P, KE, P])
        bqB = sb("bqB", [P, KE, P])
        b1B = sb("b1B", [P, KD, P])
        g2B = sb("g2B", [P, DC])
        vector_rows = sb("vector_rows", [NV, P])
        node_raw = sb("node_raw", [F * NODES, D])
        fold_scope.close()
        scope = cross_scope
        c_norm = [sb(f"c_norm{i}", [P, DC]) for i in range(4)]
        xT_hi = sb("xT_hi", [P, D], F32R)
        xT_lo = sb("xT_lo", [P, D], F32R)
        q_tile = sb("q_tile", [P, DC])
        q_hi = sb("q_hi", [P, KC, P], F32R)
        q_lo = sb("q_lo", [P, KC, P], F32R)
        PT_hi = sb("PT_hi", [P, TC * P], F32R)
        PT_lo = sb("PT_lo", [P, TC * P], F32R)
        probs = sb("probs", [P, SC])
        raw_max = sb("raw_max", [P, 1])
        part_max = sb("part_max", [P, 2])
        neg_max = sb("neg_max", [P, 1])
        row_sum = sb("row_sum", [P, NT])
        inv_sum = sb("inv_sum", [P, 1])
        z_tile = sb("z_tile", [P, DC])
        zT = sb("zT", [P, DC])
        zT_hi = sb("zT_hi", [P, DC], F32R)
        zT_lo = sb("zT_lo", [P, DC], F32R)
        x_res = sb("x_res", [P, D])
        x_resb = sb("x_resb", [P, D])
        x_mid = sb("x_mid", [P, D])
        x_norm = sb("x_norm", [P, D])
        x_normT = sb("x_normT", [P, D])
        cross_scope.close()
        scope = leaf_scope = ExitStack()
        w1, w2_hi, w2_lo, w2_raw = [], [], [], []

        def leaf_set(i):
            nonlocal scope
            w1.append(sb(f"w1_{i}", [P, LEAVES, W1]))
            scope = incoming_scope = ExitStack()
            w2_raw.append(sb(f"w2_raw{i}", [P, LEAVES, D]))
            incoming_scope.close()
            scope = leaf_scope
            w2_lo.append(sb(f"w2_lo{i}", [P, LEAVES, D], F32R))
            w2_hi.append(sb(f"w2_hi{i}", [P, LEAVES, D], F32R))

        leaf_set(0)
        b2_raw = sb("b2_raw", [LEAVES, D])
        b2_hi = sb("b2_hi", [LEAVES, D], F32R)
        b2_lo = sb("b2_lo", [LEAVES, D], F32R)
        b1_rows = sb("b1_rows", [LEAVES, 2 * HID])
        set0_words = LEAVES * W1 + 2 * LEAVES * D + 3 * D + 2 * HID
        leaf_set(1)
        row_index = [sb(f"row_index{i}", [P, 1], I32) for i in range(4)]
        x_slot = [sb(f"x_slot{i}", [P, D]) for i in range(4)]
        x_slotT = [sb(f"x_slotT{i}", [P, D]) for i in range(2)]
        w1_leaf = [sb(f"w1_leaf{i}", [P, W1]) for i in range(2)]
        hidden_T = [sb(f"hidden_T{i}", [HID, P]) for i in range(2)]
        hT = [sb(f"hT{i}", [P, P], F32R) for i in range(2)]
        hT_one = [sb(f"hT_one{i}", [P, P], F32R) for i in range(2)]
        y_slot = [sb(f"y_slot{i}", [P, D]) for i in range(4)]
        leaf_scope.close()
        scope = route_scope = ExitStack()
        below_route = sb("below_route", [P, set0_words])
        FT = F * NT
        right = sb("right", [P, FT, NODES])
        reach = [sb(f"reach{k}", [P, FT, 2 ** k]) for k in range(1, 5)]
        onehot = reach[3]
        onehot_h = sb("onehot_h", [P, F, (NT + 1) * LEAVES], F16)
        pairs = sb("pairs", [P, F, (NT + 1) * LEAVES], F16)
        fours = sb("fours", [P, F, (NT + 1) * LEAVES], F16)
        before = sb("before", [P, P], F16)
        ones_h = sb("ones_h", [P, P], F16)
        n_leaf = sb("n_leaf", [P, F * LEAVES], I32)
        n_tiles_i = sb("n_tiles_i", [P, F * LEAVES], I32)
        scan = [sb(f"scan{i}", [P, F, LEAVES]) for i in range(5)]
        n_tiles = sb("n_tiles", [P, F, LEAVES])
        base = sb("base", [P, F, LEAVES])
        place = sb("place", [P, FT, LEAVES])
        pos = sb("pos", [P, FT])
        part_i = sb("part_i", [P, 2 * FT], I32)
        part = sb("part", [P, 2 * FT])
        iota_i = sb("iota_i", [P, P], I32)
        iota_f = sb("iota_f", [P, P])
        token_i = sb("token_i", [P, NT], I32)
        token_f = sb("token_f", [P, NT])
        lo_hot = sb("lo_hot", [P, FT, P], F16)
        hi_hot = sb("hi_hot", [P, FT, HI_PAD])
        hi_tok = sb("hi_tok", [P, FT, HI_PAD], F16)
        leaf_cmp = sb("leaf_cmp", [P, F * HI_PAD, LEAVES])
        leaf_f = sb("leaf_f", [P, F * HI_PAD])
        leaf_m = sb("leaf_m", [P, F * HI_PAD])
        route_scope.close()
        scope = self_scope = ExitStack()
        kT_hi, kT_lo, v_hi, v_lo = [None] * B, [None] * B, [None] * B, [None] * B

        def key_buffers(b):
            kT_hi[b] = sb(f"kT_hi{b}", [P, KD, SQ], F32R)
            kT_lo[b] = sb(f"kT_lo{b}", [P, KD, SQ], F32R)
            v_hi[b] = sb(f"v_hi{b}", [P, TQ, D], F32R)
            v_lo[b] = sb(f"v_lo{b}", [P, TQ, D], F32R)

        key_buffers(1)
        q_rows = sb("q_rows", [P, D])
        sq_hi = sb("sq_hi", [P, D], F32R)
        sq_lo = sb("sq_lo", [P, D], F32R)
        sPT_hi = sb("sPT_hi", [P, SQ], F32R)
        sPT_lo = sb("sPT_lo", [P, SQ], F32R)
        sprobs = sb("sprobs", [P, SQ])
        above_queries = sb("above_queries", [P, set0_words - (2 * KD * SQ + 2 * TQ * D + 3 * D + 3 * SQ)])
        key_buffers(0)
        k_rows = sb("k_rows", [P, D])
        v_rows = sb("v_rows", [P, D])
        kv_index = [sb(f"kv_index{i}", [P, 1], I32) for i in range(2)]
        q_index = sb("q_index", [P, 1], I32)
        sraw_max = sb("sraw_max", [P, 1])
        sneg_max = sb("sneg_max", [P, 1])
        srow_sum = sb("srow_sum", [P, NT])
        sinv_sum = sb("sinv_sum", [P, 1])
        mid_tile = sb("mid_tile", [P, D])
        out_tile = sb("out_tile", [P, D])
        self_scope.close()

        ident_zero = sem("ident_zero")
        ident_ready = sem("ident_ready")
        wq_in = sem("wq_in")
        wk_in = sem("wk_in")
        wv_in = sem("wv_in")
        wo_in = sem("wo_in")
        cols_in = sem("cols_in")
        cols_filled = sem("cols_filled")
        columns_ready = sem("columns_ready")
        node_in = sem("node_in")
        wT_filled = sem("wT_filled")
        wqT_ready = sem("wqT_ready")
        wkT_ready = sem("wkT_ready")
        wvT_ready = sem("wvT_ready")
        node_filled = sem("node_filled")
        nodeT_ready = sem("nodeT_ready")
        M_filled = sem("M_filled")
        M_full_ready = sem("M_full_ready")
        M_gained = sem("M_gained")
        M_hi_ready = sem("M_hi_ready")
        M_ready = sem("M_ready")
        N_filled = sem("N_filled")
        N_hi_ready = sem("N_hi_ready")
        N_ready = sem("N_ready")
        broadcast_ready = sem("broadcast_ready")
        bias_filled = sem("bias_filled")
        bias_ready = sem("bias_ready")
        c_in0 = sem("c_in0")
        c_in1 = sem("c_in1")
        c_in2 = sem("c_in2")
        c_in3 = sem("c_in3")
        c_more0 = sem("c_more0")
        c_more1 = sem("c_more1")
        c_stats_ready = sem("c_stats_ready")
        c_moments_ready = sem("c_moments_ready")
        c_var_ready = sem("c_var_ready")
        c_var_step = sem("c_var_step")
        c_rooted = sem("c_rooted")
        x_rooted = sem("x_rooted")
        mid_rooted = sem("mid_rooted")
        half_ready = sem("half_ready")
        c_normed = sem("c_normed")
        c_hi_ready = sem("c_hi_ready")
        c_lo_ready = sem("c_lo_ready")
        c_turned = sem("c_turned")
        cT_hi_ready = sem("cT_hi_ready")
        cT_lo_ready = sem("cT_lo_ready")
        x_in = sem("x_in")
        x_norm_step = sem("x_norm_step")
        x_normed = sem("x_normed")
        x_turned = sem("x_turned")
        xT_hi_ready = sem("xT_hi_ready")
        xT_lo_ready = sem("xT_lo_ready")
        q_filled = sem("q_filled")
        q_tile_ready = sem("q_tile_ready")
        q_turned = sem("q_turned")
        q_hi_ready = sem("q_hi_ready")
        q_ready = sem("q_ready")
        scored = sem("scored")
        three_scored = sem("three_scored")
        part_max_ready = sem("part_max_ready")
        raw_max_ready = sem("raw_max_ready")
        max_ready = sem("max_ready")
        exp_ready = sem("exp_ready")
        probs_turned = sem("probs_turned")
        PT_hi_ready = sem("PT_hi_ready")
        PT_ready = sem("PT_ready")
        z_filled = sem("z_filled")
        inv_ready = sem("inv_ready")
        z_ready = sem("z_ready")
        z_turned = sem("z_turned")
        zT_ready = sem("zT_ready")
        zT_hi_ready = sem("zT_hi_ready")
        zT_lo_ready = sem("zT_lo_ready")
        res_in = sem("res_in")
        res_ready = sem("res_ready")
        o_filled = sem("o_filled")
        mid_ready = sem("mid_ready")
        mid_norm_step = sem("mid_norm_step")
        mid_normed = sem("mid_normed")
        mid_stored = sem("mid_stored")
        norm_stored = sem("norm_stored")
        n_turned = sem("n_turned")
        nT_ready = sem("nT_ready")
        nodes_filled = sem("nodes_filled")
        nodes_ready = sem("nodes_ready")
        route_consts = sem("route_consts")
        route_step = sem("route_step")
        onehots_ready = sem("onehots_ready")
        ranks_filled = sem("ranks_filled")
        split_ready = sem("split_ready")
        slots_filled = sem("slots_filled")
        tile_leaf_ready = sem("tile_leaf_ready")
        tables_ready = sem("tables_ready")
        w1_in = sem("w1_in")
        b1_in = sem("b1_in")
        b2_in = sem("b2_in")
        w2_first_in = sem("w2_first_in")
        w2_in = sem("w2_in")
        w2_hi_ready = sem("w2_hi_ready")
        w2_lo_ready = sem("w2_lo_ready")
        b2_hi_ready = sem("b2_hi_ready")
        b2_ready = sem("b2_ready")
        b2_placed = sem("b2_placed")
        hT_ones = sem("hT_ones")
        index_ready = sem("index_ready")
        slot_in0 = sem("slot_in0")
        slot_in1 = sem("slot_in1")
        slot_in2 = sem("slot_in2")
        slot_in3 = sem("slot_in3")
        slot_turned = sem("slot_turned")
        slotT_ready = sem("slotT_ready")
        w1_leaf_ready = sem("w1_leaf_ready")
        b1_turned = sem("b1_turned")
        b1_placed = sem("b1_placed")
        h_filled = sem("h_filled")
        hidden_ready = sem("hidden_ready")
        hT_hi_ready = sem("hT_hi_ready")
        hT_ready = sem("hT_ready")
        hT_one_ready = sem("hT_one_ready")
        y_filled = sem("y_filled")
        y_ready = sem("y_ready")
        y_stored0 = sem("y_stored0")
        y_stored1 = sem("y_stored1")
        y_stored2 = sem("y_stored2")
        y_stored3 = sem("y_stored3")
        kv_index_ready = sem("kv_index_ready")
        k_in = sem("k_in")
        v_in = sem("v_in")
        sk_turned = sem("sk_turned")
        kT_hi_ready = sem("kT_hi_ready")
        kT_ready = sem("kT_ready")
        v_hi_ready = sem("v_hi_ready")
        v_ready = sem("v_ready")
        q_index_ready = sem("q_index_ready")
        sq_in = sem("sq_in")
        sq_turned = sem("sq_turned")
        sq_hi_ready = sem("sq_hi_ready")
        sq_ready = sem("sq_ready")
        s_scored = sem("s_scored")
        s_raw_max_ready = sem("s_raw_max_ready")
        s_max_ready = sem("s_max_ready")
        s_exp_ready = sem("s_exp_ready")
        s_turned = sem("s_turned")
        sPT_hi_ready = sem("sPT_hi_ready")
        sPT_ready = sem("sPT_ready")
        sz_filled = sem("sz_filled")
        s_inv_ready = sem("s_inv_ready")
        mid_in = sem("mid_in")
        out_ready = sem("out_ready")
        out_stored = sem("out_stored")
        passed = {nc.vector.engine: sem("vector_passed"), nc.gpsimd.engine: sem("gpsimd_passed")}

        def split_product(pe, dst, left, right, first=True, last=True):
            pe.matmul(dst, left[0], right[0], start=first, stop=False)
            pe.matmul(dst, left[0], right[1], start=False, stop=False)
            return pe.matmul(dst, left[1], right[0], start=False, stop=last)

        def at_least(engine, semaphore, value):
            if not (isinstance(value, int) and value <= 0):
                engine.wait_ge(semaphore, value)

        def wait_apart(engine, semaphore, value):
            engine.wait_ge(semaphore, value)
            if not isinstance(value, int):
                engine.sem_inc(passed[engine.engine], 1)

        def measure(dve, src, stats, moments, var, step, at, scale=1.0, plus=EPS):
            nc.vector.bn_stats(stats[:, :], src).then_inc(step, 1)
            wait_apart(dve, step, at + 1)
            nc.vector.bn_aggr(moments[:, :], stats[:, :]).then_inc(step, 1)
            dve.wait_ge(step, at + 2)
            nc.vector.tensor_scalar(var[:, :], moments[:, 1:2], scale, plus, ALU.mult, ALU.add).then_inc(step, 1)

        def root(pool, rstd, var, step, at, rooted):
            pool.wait_ge(step, at + 3)
            nc.gpsimd.tensor_tensor(rstd[:, :], var[:, :], minus_half[:, 0:1], ALU.pow).then_inc(rooted, 1)

        def walk(engine, step, n0, split_leaf=None, key_tile=None):

            def turn(i):
                for k in range(4):
                    step(i * 4 + (k + 3), (k + 3 + n0) % 4)
                    if split_leaf and k % 2:
                        split_leaf(i * 2 + k // 2, i)
                    if key_tile and k == 3:
                        key_tile(i)

            for m in range(3):
                step(m, (m + n0) % 4)
            turn(0)
            with engine.Fori(1, TQ - 1) as i:
                turn(i)
            for m in range(SLOT_TILES, SLOT_TILES + 2):
                step(m, (m + n0) % 4)
                if split_leaf:
                    split_leaf(LEAVES - 2 + m - SLOT_TILES, LEAVES // 2 - 1)
                if key_tile and m > SLOT_TILES:
                    key_tile(TQ - 1)

        W2_IN = 16

        def stored_in(f, q):
            return 16 * ((f * SLOT_TILES + 3 - q) // 4)

        def w2_in_before(f):
            return W2_IN * (f - 1) * (LEAVES // 2 - 1)

        assert SLOT_TILES == 4 * (TQ - 1) + 3 and LEAVES == 2 * TQ and B == 2

        BOTH, TRANSPOSED, STRAIGHT, STATISTICS = range(4)

        def cross_steps(engine, step):
            step(0, True, False, False, True, STATISTICS)
            step(1, True, True, False, True, STATISTICS)
            with engine.Fori(2, TQ) as n:
                step(n, True, True, True, True, STATISTICS)
            step(TQ, False, True, True, False, TRANSPOSED)
            step(TQ, True, False, False, True, STRAIGHT)
            step(TQ + 1, True, True, True, True)
            with engine.Fori(TQ + 2, NT - 1) as n:
                step(n, True, True, True, True)
            step(NT - 1, True, True, True, False)
            step(NT, False, True, True, False)
            step(NT + 1, False, False, True, False)

        def self_steps(engine, step):
            step(0, 0, None, True)
            step(1, 0, 0, True)
            with engine.Fori(2, TQ) as n:
                step(n, 0, 0, True)
            step(TQ, 1, 0, False)
            with engine.Fori(TQ + 1, NT - 1) as n:
                step(n, 1, 1, False)
            step(NT - 1, 1, 1, False)
            step(NT, None, 1, False)

        block = top.enter_context(nc.Block())

        @block.sync
        def _(sp):
            blocks = "(k p) n -> p k n"
            sp.dma_start(wq_raw[:, :, :], Wq.rearrange(blocks, p=P)).then_inc(wq_in, 16)
            sp.dma_start(wk_raw[:, :, :], Wk.rearrange(blocks, p=P)).then_inc(wk_in, 16)
            row = 0
            for src, k in vectors:
                sp.dma_start(vector_rows[row:row + k, :], src.rearrange("(k p) -> k p", p=P)).then_inc(cols_in, 16)
                row += k
            sp.dma_start(out_bias[:, :], bo.rearrange("(a n) -> a n", a=1).broadcast_to([P, D])).then_inc(cols_in, 16)
            sp.dma_start(g2B[:, :], ln2_g.rearrange("(a n) -> a n", a=1).broadcast_to([P, DC])).then_inc(cols_in, 16)
            for f, tree in enumerate(trees):
                own = slice(f * NODES, (f + 1) * NODES)
                sp.dma_start(node_raw[own, :], tree["node_w"]).then_inc(node_in, 16)
                sp.dma_start(node_bias[:, own], tree["node_b"].rearrange("(a n) -> a n", a=1).broadcast_to([P, NODES])
                             ).then_inc(node_in, 16)
            sp.dma_start(wv_raw[:, :, :], Wv.rearrange(blocks, p=P)).then_inc(wv_in, 16)

            c_in = [c_in0, c_in1, c_in2, c_in3]

            def context_load(t, slot):
                sp.dma_start(c_raw[slot][:, :], ctx_rows[ds(t * P, P), :]).then_inc(c_in[slot], 16)

            def query_load(n):
                at_least(sp, x_normed, n)
                sp.dma_start(x_raw[:, :], x_rows[ds(n * P, P), :]).then_inc(x_in, 16)

            for slot in range(4):
                context_load(slot, slot)
            sp.dma_start(wo_raw[:, :, :], Wo.rearrange(blocks, p=P)).then_inc(wo_in, 16)
            query_load(0)
            with sp.Fori(1, TC // 4) as i:
                for slot in range(4):
                    sp.wait_ge(c_stats_ready, i * 4 + (slot - 3))
                    context_load(i * 4 + slot, slot)

            def first_tiles(passing):
                for slot in range(4):
                    if passing == BOTH:
                        sp.wait_ge(c_stats_ready, TC + slot - 3)
                    elif passing == TRANSPOSED:
                        sp.wait_ge(c_stats_ready, B * TC)
                        sp.wait_ge(c_normed, TC)
                    else:
                        sp.wait_ge(c_normed, passing * TC + slot - 3)
                    context_load(slot if passing == BOTH else TC + slot, slot)

            def further_tiles(passing):
                with sp.Fori(1, TC // 4) as i:
                    for slot in range(4):
                        sp.wait_ge(c_normed, i * 4 + (passing * TC + slot - 3))
                        context_load(i * 4 + (slot if passing == BOTH else TC + slot), slot)

            def more_tiles(n):
                for slot, landed in enumerate((c_more0, c_more1)):
                    if isinstance(n, int) and n == 0:
                        sp.wait_ge(c_normed, TC)
                    else:
                        sp.wait_ge(c_stats_ready, n * 2 + (TC - 1 + slot))
                    sp.dma_start(c_raw[slot][:, :], ctx_rows[ds((n * 2 + (TC + slot)) * P, P), :]).then_inc(landed, 16)

            def cross_rows(n, query_ahead, beside=None):
                if query_ahead:
                    query_load(n + 3)
                sp.dma_start(x_res[:, :], x_rows[ds(n * P, P), :]).then_inc(res_in, 16)
                if beside:
                    beside()
                sp.wait_ge(mid_ready, n + 1)
                sp.dma_start(mid_rows[ds(n * P, P), :], x_mid[:, :]).then_inc(mid_stored, 16)
                sp.wait_ge(mid_normed, n + 1)
                sp.dma_start(norm_rows[ds(n * P, P), :], x_norm[:, :]).then_inc(norm_stored, 16)

            first_tiles(BOTH)
            further_tiles(BOTH)
            query_load(1)
            more_tiles(0)
            query_load(2)
            more_tiles(1)
            sp.wait_ge(M_ready, 1)
            sp.wait_ge(N_ready, 1)
            sp.wait_ge(bias_ready, 2)
            with sp.Fori(0, TQ - 2) as n:
                cross_rows(n, True, lambda: more_tiles(n + 2))

            def refill():
                first_tiles(TRANSPOSED)
                further_tiles(TRANSPOSED)
                first_tiles(STRAIGHT)

            cross_rows(TQ - 2, True, refill)
            cross_rows(TQ - 1, True, lambda: further_tiles(STRAIGHT))
            with sp.Fori(TQ, NT - 3) as n:
                cross_rows(n, True)
            cross_rows(NT - 3, False)

            def rows_w1(f, k):
                quarter = ds(k * (LEAVES // 4), LEAVES // 4)
                sp.dma_start(w1[f % 2][:, quarter, 0:KD * HID],
                             trees[f]["w1"][quarter, :, :].rearrange("l (p k) h -> p l (k h)", k=KD)).then_inc(w1_in, 16)

            def rows_b(f):
                sp.dma_start(b2_raw[:, :], trees[f]["b2"]).then_inc(b2_in, 16)
                for half in range(2):
                    sp.dma_start(b1_rows[:, half * HID:(half + 1) * HID], trees[f]["b1"]).then_inc(b1_in, 16)

            def first_w1():
                sp.wait_ge(scored, NT)
                for k in range(4):
                    rows_w1(0, k)

            def first_w2():
                sp.dma_start(w2_raw[0][0:HID], trees[0]["w2"].rearrange("l h n -> h l n")).then_inc(w2_first_in, 16)
                sp.wait_ge(z_filled, NT)
                rows_b(0)

            cross_rows(NT - 2, False, first_w1)
            cross_rows(NT - 1, False, first_w2)

            def leaf_w2(f, l, n):
                sp.dma_start(w2_raw[f % 2][0:HID, ds(l, n), :], trees[f]["w2"][ds(l, n), :, :].rearrange("l h n -> h l n")
                             ).then_inc(w2_in, 16)

            def place_b2(f):
                sp.wait_ge(b2_ready, f + 1)
                for row, src in ((HID, b2_hi), (HID + 1, b2_lo)):
                    sp.dma_start(w2_lo[f % 2][row:row + 1, :, :].rearrange("a l n -> a (l n)").bitcast(F32),
                                 src[:, :].bitcast(F32)).then_inc(b2_placed, 16)

            def leaf_weights(f):
                sp.wait_ge(tables_ready, F)
                sp.wait_ge(b2_placed, 32 * f)
                sp.wait_ge(w2_lo_ready, LEAVES * f)
                sp.wait_ge(b1_placed, f)
                if f >= 2:
                    sp.wait_ge(y_filled, SLOT_TILES * (f - 1))
                    sp.wait_ge(w1_leaf_ready, SLOT_TILES * (f - 1))
                rows_b(f)
                leaf_w2(f, 0, 4)

            place_b2(0)
            y_stored = [y_stored0, y_stored1, y_stored2, y_stored3]
            for f in range(F):
                n0 = SLOT_TILES * f

                def store(j, slot):
                    sp.wait_ge(y_ready, j + (n0 + 1))
                    sp.dma_start(slot_rows[f][ds(j * P, P), :], y_slot[slot][:, :]).then_inc(y_stored[slot], 16)

                if f + 1 < F:
                    leaf_weights(f + 1)
                store(0, n0 % 4)
                store(1, (n0 + 1) % 4)
                if f + 1 < F:
                    place_b2(f + 1)
                for turns in (range(4), range(4, LEAVES // 2 - 2)):
                    with sp.Fori(turns.start, turns.stop) as i:
                        for k in range(2, 6):
                            store(i * 4 + k, (n0 + k) % 4)
                            if f + 1 < F and k == 3 and turns.start == 0:
                                rows_w1(f + 1, i)
                        if f + 1 < F:
                            sp.wait_ge(w2_in, i * W2_IN + (w2_in_before(f + 1) + W2_IN))
                            leaf_w2(f + 1, i * 2 + 4, 2)
                for j in range((LEAVES // 2 - 2) * 4 + 2, SLOT_TILES):
                    store(j, (j + n0) % 4)

            for q in range(4):
                sp.wait_ge(y_stored[q], stored_in(F, q))
            with sp.Fori(0, NT) as n:
                sp.dma_start(mid_tile[:, :], mid_rows[ds(n * P, P), :]).then_inc(mid_in, 16)
                sp.wait_ge(out_ready, n + 1)
                sp.dma_start(out_rows[ds(n * P, P), :], out_tile[:, :]).then_inc(out_stored, 16)
            sp.wait_ge(out_stored, 16 * NT)
            sp.wait_ge(mid_stored, 16 * NT)
            sp.wait_ge(norm_stored, 16 * NT)

        @block.tensor
        def _(pe):
            pe.wait_ge(ident_ready, 1)

            def turn_weights(raw, kin, dst_bank):
                for e in range(KE):
                    for k in range(kin):
                        last = pe.transpose(dst_bank(e)[:, k * P:(k + 1) * P], raw[:, k, e * P:(e + 1) * P], ident[:, :])
                    last.then_inc(wT_filled, 1)

            pe.wait_ge(wq_in, 16)
            turn_weights(wq_raw, KD, bank)
            pe.wait_ge(cols_in, 16 * (len(vectors) + 2))
            pe.transpose(pE[:, 0:NV], vector_rows[:, :], ident[0:NV, 0:NV]).then_inc(cols_filled, 1)
            pe.wait_ge(wk_in, 16)
            pe.wait_ge(columns_ready, 1)
            turn_weights(wk_raw, KC, lambda e: (pT[0], pT[1], pZ, pE)[e])
            pe.wait_ge(wv_in, 16)
            pe.wait_ge(wqT_ready, KE)
            turn_weights(wv_raw, KC, bank)
            pe.wait_ge(wkT_ready, KE)
            pe.wait_ge(node_in, 16 * 2 * F)
            for k in range(KD):
                last = pe.transpose(pE[:, k * F * NODES:(k + 1) * F * NODES], node_raw[:, k * P:(k + 1) * P],
                                    ident[0:F * NODES, 0:F * NODES])
            last.then_inc(node_filled, 1)
            m_bank = (pT[0], pT[1], pZ, pT[0])
            for k in range(KD):
                if k == 3:
                    pe.wait_ge(M_full_ready, 1)
                for e in range(KE):
                    last = pe.matmul(m_bank[k][:, 0:DC], wqT[:, e, k * P:(k + 1) * P], wkT[:, e, :],
                                     start=e == 0, stop=e == KE - 1)
                last.then_inc(M_filled, 1)
            def turn_context(passing, t, slot):
                psum = (pT[1], pZ)[slot % 2] if passing == BOTH else bank(slot)
                pe.wait_ge(c_normed, t + (TC * passing + 1))
                at_least(pe, cT_lo_ready, t - 1 if passing == BOTH else t + (TC * passing - 3))
                for k in range(KC):
                    last = pe.transpose(psum[:, k * P:(k + 1) * P], c_norm[slot][:, k * P:(k + 1) * P], ident[:, :])
                last.then_inc(c_turned, 1)

            def turn_x(n):
                pe.wait_ge(x_normed, n + 1)
                for k in range(KD):
                    last = pe.transpose(pT[0][:, k * P:(k + 1) * P], x_hat[:, k * P:(k + 1) * P], ident[:, :])
                last.then_inc(x_turned, 1)

            def project_query(n, psum=pT[1]):
                pe.wait_ge(xT_lo_ready, n + 1)
                for k in range(KD):
                    own = slice(k * P, (k + 1) * P)
                    last = split_product(pe, psum[:, 0:DC], (xT_hi[:, own], xT_lo[:, own]),
                                         (M_hi[:, k, :], M_lo[:, k, :]), k == 0, k == KD - 1)
                last.then_inc(q_filled, 1)

            def turn_q_tile(n):
                pe.wait_ge(q_tile_ready, n + 1)
                for c in range(KC):
                    last = pe.transpose(pT[0][:, c * P:(c + 1) * P], q_tile[:, c * P:(c + 1) * P], ident[:, :])
                last.then_inc(q_turned, 1)

            def turn_probs(n, j):
                pe.wait_ge(exp_ready, n + 1)
                at_least(pe, PT_ready, n * SBANKS + (j - 1))
                queries = min(n + 2, NT) if isinstance(n, int) else n + 2
                if j == 0:
                    pe.wait_ge(q_ready, queries)
                if j == 1:
                    pe.wait_ge(q_tile_ready, queries)
                for k in range(4):
                    blk = (4 * j + k) * P
                    last = pe.transpose(pT[j % 2][:, k * P:(k + 1) * P], probs[:, blk:blk + P], ident[:, :])
                last.then_inc(probs_turned, 1)

            def score(n, j):
                if j == 0:
                    pe.wait_ge(q_ready, n + 1)
                    if isinstance(n, int) and n % TQ == 0:
                        pe.wait_ge(cT_lo_ready, TC * (n // TQ + 1))
                for c in range(KC):
                    last = split_product(pe, bank(j), (q_hi[:, c, :], q_lo[:, c, :]),
                                         (ctxT_hi[:, c, j * BANK:(j + 1) * BANK], ctxT_lo[:, c, j * BANK:(j + 1) * BANK]),
                                         c == 0, c == KC - 1)
                if j == SBANKS - 1:
                    last.then_inc(scored, 1)
                if j == SBANKS - 2 and isinstance(n, int) and n % TQ == 0:
                    last.then_inc(three_scored, 1)

            def weigh(n, part):
                pe.wait_ge(PT_ready, n * SBANKS + (part + 1))
                if part == 0:
                    if isinstance(n, int) and n % TQ == 0:
                        pe.wait_ge(c_lo_ready, TC * (n // TQ + 1))
                    at_least(pe, z_ready, n)
                for t in range(part * TC // SBANKS, (part + 1) * TC // SBANKS):
                    last = split_product(pe, pZ[:, 0:DC], (PT_hi[:, t * P:(t + 1) * P], PT_lo[:, t * P:(t + 1) * P]),
                                         (ctx_hi[:, t, :], ctx_lo[:, t, :]), t == 0, t == TC - 1)
                if part == SBANKS - 1:
                    last.then_inc(z_filled, 1)

            def turn_z(e):
                pe.wait_ge(z_ready, e + 1)
                at_least(pe, nodes_ready, e)
                for c in range(KC):
                    last = pe.transpose(pE[:, c * P:(c + 1) * P], z_tile[:, c * P:(c + 1) * P], ident[:, :])
                last.then_inc(z_turned, 1)

            def project_out(e):
                pe.wait_ge(zT_lo_ready, e + 1)
                for c in range(KC):
                    cols = slice(c * P, (c + 1) * P)
                    last = split_product(pe, pE[:, :], (zT_hi[:, cols], zT_lo[:, cols]), (N_hi[:, c, :], N_lo[:, c, :]),
                                         c == 0, c == KC - 1)
                last.then_inc(o_filled, 1)

            def turn_norm(e):
                pe.wait_ge(mid_normed, e + 1)
                for k in range(KD):
                    last = pe.transpose(pE[:, k * P:(k + 1) * P], x_norm[:, k * P:(k + 1) * P], ident[:, :])
                last.then_inc(n_turned, 1)

            def score_nodes(e):
                pe.wait_ge(nT_ready, e + 1)
                for k in range(KD):
                    last = pe.matmul(pE[:, 0:F * NODES], x_normT[:, k * P:(k + 1) * P], nodeT[:, k, :],
                                     start=k == 0, stop=k == KD - 1)
                last.then_inc(nodes_filled, 1)

            def step(n, front, back, tail, ahead, passing=None):
                no_scores = back and not front
                if isinstance(n, int) and n == 1:
                    pe.wait_ge(bias_ready, 2)
                for j in range(SBANKS):
                    if back:
                        turn_probs(n - 1, j)
                    if passing == TRANSPOSED:
                        turn_context(passing, j, j)
                    if tail and j == 3 and not no_scores:
                        project_out(n - 2)
                    if front:
                        score(n, j)
                    if tail and j == 0:
                        turn_z(n - 2)
                    if ahead and not back:
                        if j == 0:
                            turn_x(n + 1)
                        if j == 2:
                            project_query(n + 1)
                if ahead and not back:
                    turn_q_tile(n + 1)
                    if n == 0:
                        fold_out_bias()
                    return
                if ahead:
                    pe.wait_ge(PT_ready, n * SBANKS - 1)
                    turn_x(n + 1)
                for part in range(4):
                    if back:
                        weigh(n - 1, part)
                    if tail and part == 0 and no_scores:
                        project_out(n - 2)
                    if tail and part == (2 if no_scores else 1):
                        turn_norm(n - 2)
                    if ahead and part == 1:
                        project_query(n + 1)
                    if tail and part == (3 if no_scores else 2):
                        score_nodes(n - 2)
                    if ahead and part == 2:
                        turn_q_tile(n + 1)
                    if passing == TRANSPOSED and part < 3:
                        for slot in range(4):
                            turn_context(passing, (part + 1) * 4 + slot, slot)

            def fold_out_bias():
                for e in range(KE):
                    last = pe.matmul(pE[:, :], bvB[:, e, :], wo_raw[:, e, :], start=e == 0, stop=e == KE - 1)
                last.then_inc(bias_filled, 1)

            def fold_N(c, e):
                last = pe.matmul(bank(c), wvT[:, e, c * P:(c + 1) * P], wo_raw[:, e, :], start=e == 0, stop=e == KE - 1)
                if e == KE - 1:
                    last.then_inc(N_filled, 1)

            def fold_u(i):
                if i < KE:
                    last = pe.matmul(pE[:, 0:DC], bqB[:, i, :], wkT[:, i, :], start=i == 0, stop=False)
                else:
                    k = i - KE
                    last = pe.matmul(pE[:, 0:DC], b1B[:, k, :], M_full[:, k, :], start=False, stop=k == KD - 1)
                if i == KE + KD - 1:
                    last.then_inc(bias_filled, 1)

            assert KC == 3 and KE == KD == 4 and TC == 16
            pe.wait_ge(wvT_ready, KE)
            pe.wait_ge(wo_in, 16)
            for c in range(KC - 1):
                for e in range(KE):
                    fold_N(c, e)
            pe.wait_ge(M_full_ready, KD)
            for t in range(4):
                turn_context(BOTH, t, t)
                fold_N(KC - 1, t)
            turn_x(0)
            pe.wait_ge(nodeT_ready, 1)
            pe.wait_ge(broadcast_ready, 1)
            for t in range(4, 12):
                turn_context(BOTH, t, t % 4)
                fold_u(t - 4)
            turn_context(BOTH, 12, 0)
            turn_context(BOTH, 13, 1)
            pe.wait_ge(M_ready, 1)
            project_query(0, bank(3))
            turn_context(BOTH, 14, 2)
            turn_context(BOTH, 15, 3)
            turn_q_tile(0)
            pe.wait_ge(N_ready, 1)
            cross_steps(pe, step)

            def turn_b1(f):
                pe.wait_ge(b1_in, 32 * (f + 1))
                pe.transpose(pE[:, 0:LEAVES], b1_rows[:, :], ident[0:LEAVES, 0:LEAVES]).then_inc(b1_turned, 1)

            pe.wait_ge(nodes_ready, NT)
            turn_b1(0)
            pe.wait_ge(route_consts, 4)
            W = (NT + 1) * LEAVES
            pe.wait_ge(onehots_ready, 1)
            for f in range(F):
                for back in range(1, NT, 4):
                    pe.matmul(bank(f)[:, back * LEAVES:W], ones_h[:, :], fours[:, f, 0:W - back * LEAVES],
                              start=back == 1, stop=False, skip_group_check=True)
                last = pe.matmul(bank(f)[:, 0:W], before[:, :], onehot_h[:, f, :], start=False, stop=True,
                                 skip_group_check=True)
            last.then_inc(ranks_filled, 1)
            pe.wait_ge(b1_placed, 1)

            def find_slots(f):
                pe.wait_ge(split_ready, f + 1)
                for t in range(NT):
                    last = pe.matmul((pT[1], pZ, pE)[f][:, 0:HI_PAD], lo_hot[:, f * NT + t, :],
                                     hi_tok[:, f * NT + t, :], start=t == 0, stop=t == NT - 1)
                last.then_inc(slots_filled, 1)

            find_slots(0)
            pe.wait_ge(tables_ready, 1)

            def keys_turned(t, psum):
                pe.wait_ge(k_in, (t + 1) * 16)
                at_least(pe, kT_ready, t)
                for k in range(KD):
                    last = pe.transpose(psum[:, k * P:(k + 1) * P], k_rows[:, k * P:(k + 1) * P], ident[:, :])
                last.then_inc(sk_turned, 1)

            for f in range(F):
                n0 = SLOT_TILES * f
                slot_in = [slot_in0, slot_in1, slot_in2, slot_in3]
                def turn_rows(j, q):
                    pe.wait_ge(slot_in[q], (j + (n0 + 4 - q)) * 4)
                    at_least(pe, slotT_ready, j + (n0 - 1))
                    rows = x_slot[q][:, :].rearrange("n (p k) -> n k p", k=KD)
                    for k in range(KD):
                        last = pe.transpose(bank(q % 2)[:, k * P:(k + 1) * P], rows[:, k, :], ident[:, :])
                    last.then_inc(slot_turned, 1)

                def first_layer(j, q):
                    pe.wait_ge(slotT_ready, j + (n0 + 1))
                    pe.wait_ge(w1_leaf_ready, j + (n0 + 1))
                    at_least(pe, hidden_ready, j + (n0 - 1))
                    for k in range(KD):
                        last = pe.matmul(pT[q][0:HID, 0:P], w1_leaf[q][:, k * HID:(k + 1) * HID],
                                         x_slotT[q][:, k * P:(k + 1) * P], start=k == 0, stop=k == KD - 1)
                    last.then_inc(h_filled, 1)

                def second_layer(j, q):
                    leaf = pe.value_load(tile_leaf[0:1, ds(j + f * HI_PAD, 1)], min_val=0, max_val=LEAVES - 1)
                    pe.wait_ge(hT_ready, j + (n0 + 1))
                    pe.wait_ge(hT_one_ready, j + (n0 + 1))
                    at_least(pe, y_ready, j + (n0 - 1))
                    pe.matmul(bank(2 + q), hT[q][:, :], w2_hi[f % 2][:, ds(leaf, 1), :], start=True, stop=False)
                    pe.matmul(bank(2 + q), hT_one[q][0:HID + 2, :], w2_lo[f % 2][0:HID + 2, ds(leaf, 1), :],
                              start=False, stop=True).then_inc(y_filled, 1)

                def step(m, q):
                    edge = isinstance(m, int)
                    if edge and m == SLOT_TILES and f + 1 < F:
                        pe.wait_ge(tables_ready, F)
                        turn_b1(f + 1)
                    if not edge or m < SLOT_TILES:
                        turn_rows(m, q)
                    if not edge or 1 <= m <= SLOT_TILES:
                        first_layer(m - 1, (q + 1) % 2)
                    if f == 0 and edge and m in (1, 2):
                        find_slots(m)
                    if edge and m == 2:
                        pe.wait_ge(w2_lo_ready, LEAVES * (f + 1))
                        pe.wait_ge(b2_placed, 32 * (f + 1))
                        pe.wait_ge(hT_ones, 2)
                    if not edge or 2 <= m:
                        second_layer(m - 2, q % 2)

                def turn_keys(t):
                    if isinstance(t, int) and t == 0:
                        pe.wait_ge(b1_placed, F)
                    keys_turned(t, pE)

                walk(pe, step, n0, key_tile=turn_keys if f == F - 1 else None)

            def turn_query(n):
                pe.wait_ge(sq_in, (n + 1) * 16)
                for k in range(KD):
                    last = pe.transpose(pE[:, k * P:(k + 1) * P], q_rows[:, k * P:(k + 1) * P], ident[:, :])
                last.then_inc(sq_turned, 1)

            def sturn(n, j):
                pe.wait_ge(s_exp_ready, n + 1)
                at_least(pe, sPT_ready, n * KBANKS + (j - 1))
                for k in range(4):
                    blk = (4 * j + k) * P
                    last = pe.transpose(pT[j % 2][:, k * P:(k + 1) * P], sprobs[:, blk:blk + P], ident[:, :])
                last.then_inc(s_turned, 1)

            def sscore(n, j, b):
                if j == 0:
                    pe.wait_ge(sq_ready, n + 1)
                for k in range(KD):
                    cols = slice(k * P, (k + 1) * P)
                    keys = slice(j * BANK, (j + 1) * BANK)
                    last = split_product(pe, bank(j), (sq_hi[:, cols], sq_lo[:, cols]),
                                         (kT_hi[b][:, k, keys], kT_lo[b][:, k, keys]), k == 0, k == KD - 1)
                if j == KBANKS - 1:
                    last.then_inc(s_scored, 1)

            def sweigh(n, half, b):
                pe.wait_ge(sPT_ready, n * KBANKS + (half + 1))
                if half == 0:
                    at_least(pe, out_ready, n)
                for t in range(half * TQ // 2, (half + 1) * TQ // 2):
                    last = split_product(pe, pZ[:, :], (sPT_hi[:, t * P:(t + 1) * P], sPT_lo[:, t * P:(t + 1) * P]),
                                         (v_hi[b][:, t, :], v_lo[b][:, t, :]), t == 0, t == TQ - 1)
                if half:
                    last.then_inc(sz_filled, 1)

            def step(n, front, back, key):
                if isinstance(n, int) and n in (0, TQ):
                    pe.wait_ge(kT_ready, n + TQ)
                    pe.wait_ge(v_ready, n + TQ)
                for j in range(KBANKS):
                    if back is not None:
                        sturn(n - 1, j)
                    if front is not None:
                        sscore(n, j, front)
                if key:
                    keys_turned(n + TQ, bank(2))
                if not isinstance(n, int) or n + 1 < NT:
                    pe.wait_ge(sq_ready, n + 1)
                    turn_query(n + 1)
                if back is not None:
                    sweigh(n - 1, 0, back)
                    sweigh(n - 1, 1, back)

            pe.wait_ge(kT_ready, TQ)
            turn_query(0)
            pe.wait_ge(sq_ready, 1)
            self_steps(pe, step)

        @block.scalar
        def _(act):
            for e in range(KE):
                act.wait_ge(wT_filled, e + 1)
                nc.scalar.copy(wqT[:, e, :], bank(e)).then_inc(wqT_ready, 1)
            for e in range(KE):
                act.wait_ge(wT_filled, 2 * KE + e + 1)
                nc.scalar.copy(wvT[:, e, :], bank(e)[:, 0:DC]).then_inc(wvT_ready, 1)
            m_bank = (pT[0], pT[1], pZ, pT[0])
            for k in range(KD):
                act.wait_ge(M_filled, k + 1)
                nc.scalar.copy(M_full[:, k, :], m_bank[k][:, 0:DC]).then_inc(M_full_ready, 1)
            def N_high(c):
                act.wait_ge(N_filled, c + 1)
                nc.scalar.copy(N_hi[:, c, :], bank(c)).then_inc(N_hi_ready, 1)

            def high(passing, t, slot):
                act.wait_ge(c_normed, t + (TC * passing + 1))
                nc.scalar.copy(ctx_hi[:, ds(t, 1), :], c_norm[slot][:, :]).then_inc(c_hi_ready, 1)

            def turned_high(passing, t, slot):
                act.wait_ge(c_turned, t + (TC * passing + 1))
                psum = (pT[1], pZ)[slot % 2] if passing == BOTH else bank(slot)
                nc.scalar.copy(ctxT_hi[:, :, ds(t * P, P)], psum[:, 0:DC].rearrange("p (k n) -> p k n", k=KC)
                               ).then_inc(cT_hi_ready, 1)

            def straight(groups):
                with act.Fori(groups.start, groups.stop) as i:
                    for slot in range(4):
                        high(STRAIGHT, i * 4 + slot, slot)

            def x_high(n):
                act.wait_ge(x_turned, n + 1)
                at_least(act, q_filled, n)
                nc.scalar.copy(xT_hi[:, :], pT[0][:, :]).then_inc(xT_hi_ready, 1)

            def query_high(n):
                act.wait_ge(q_turned, n + 1)
                at_least(act, scored, n)
                nc.scalar.copy(q_hi[:, :, :], pT[0][:, 0:DC].rearrange("p (c n) -> p c n", c=KC)).then_inc(q_hi_ready, 1)

            def probs_hi(n, j):
                act.wait_ge(probs_turned, n * SBANKS + (j + 1))
                if j == 0:
                    at_least(act, z_filled, n)
                nc.scalar.copy(PT_hi[:, j * BANK:(j + 1) * BANK], pT[j % 2][:, :]).then_inc(PT_hi_ready, 1)

            def exp(n):
                act.wait_ge(max_ready, n + 1)
                at_least(act, probs_turned, n * SBANKS)
                nc.scalar.activation(probs[:, :], pS[:, 0:SC], ACT.Exp, bias=neg_max[:, 0:1], scale=CROSS_SCALE,
                                     accum_out=row_sum[:, ds(n, 1)]).then_inc(exp_ready, 1)

            def z_hi(e):
                act.wait_ge(zT_ready, (e + 1) * KC)
                nc.scalar.copy(zT_hi[:, :], zT[:, :]).then_inc(zT_hi_ready, 1)

            def norm_T(e):
                act.wait_ge(n_turned, e + 1)
                nc.scalar.copy(x_normT[:, :], pE[:, :]).then_inc(nT_ready, 1)

            def step(n, front, back, tail, ahead, passing=None):
                for j in range(SBANKS):
                    if back:
                        probs_hi(n - 1, j)
                    if passing == TRANSPOSED:
                        turned_high(passing, j, j)
                    if tail and j == 1:
                        z_hi(n - 2)
                if passing == TRANSPOSED:
                    with act.Fori(1, 3) as i:
                        for slot in range(4):
                            turned_high(passing, i * 4 + slot, slot)
                if ahead:
                    x_high(n + 1)
                if passing == STRAIGHT:
                    act.wait_ge(z_filled, TQ)
                    straight(range(2))
                if ahead and not back:
                    query_high(n + 1)
                if front:
                    exp(n)
                if tail:
                    norm_T(n - 2)
                if ahead and back:
                    query_high(n + 1)
                if passing == TRANSPOSED:
                    with act.Fori(3, TC // 4) as i:
                        for slot in range(4):
                            turned_high(passing, i * 4 + slot, slot)
                if passing == STRAIGHT:
                    straight(range(2, TC // 4))

            def highs(tiles):
                for t in tiles:
                    high(BOTH, t, t % 4)
                    if t > tiles.start:
                        turned_high(BOTH, t - 1, (t - 1) % 4)
                turned_high(BOTH, tiles.stop - 1, (tiles.stop - 1) % 4)

            N_high(0)
            act.wait_ge(M_gained, KD)
            nc.scalar.copy(M_hi[:, :, :], M_gain[:, :, :]).then_inc(M_hi_ready, 1)
            N_high(1)
            highs(range(4))
            N_high(2)
            x_high(0)
            highs(range(4, TC))
            query_high(0)
            cross_steps(act, step)

            def b2_high(f):
                act.wait_ge(b2_in, 16 * (f + 1))
                nc.scalar.copy(b2_hi[:, :], b2_raw[:, :]).then_inc(b2_hi_ready, 1)

            def w2_high(f, l, i):
                landed = W2_IN if isinstance(i, int) and i == 0 else i * W2_IN
                act.wait_ge(w2_in, landed + w2_in_before(f))
                raw = w2_raw[f % 2][0:HID, ds(l, 1), :]
                nc.scalar.copy(w2_hi[f % 2][0:HID, ds(l, 1), :], raw).then_inc(w2_hi_ready, 1)
                nc.scalar.copy(w2_hi[f % 2][HID:P, ds(l, 1), :], raw).then_inc(w2_hi_ready, 1)

            def key_high(t, t0=0):
                b = t0 // TQ
                act.wait_ge(sk_turned, t + (t0 + 1))
                nc.scalar.copy(kT_hi[b][:, :, ds(t * P, P)], (bank(2) if b else pE[:, :]).rearrange("p (k n) -> p k n", k=KD)
                               ).then_inc(kT_hi_ready, 1)
                act.wait_ge(v_in, (t + (t0 + 1)) * 16)
                nc.scalar.copy(v_hi[b][:, ds(t, 1), :], v_rows[:, :]).then_inc(v_hi_ready, 1)

            b2_high(0)
            act.wait_ge(w2_first_in, 16)
            act.wait_ge(z_filled, NT)
            for l in range(0, LEAVES, 4):
                for half in range(2):
                    nc.scalar.copy(w2_hi[0][half * HID:(half + 1) * HID, l:l + 4, :], w2_raw[0][0:HID, l:l + 4, :]
                                   ).then_inc(w2_hi_ready, 4)
            for f in range(F):
                n0 = SLOT_TILES * f

                def take_w1(j, q):
                    leaf = act.value_load(tile_leaf[0:1, ds(j + f * HI_PAD, 1)], min_val=0, max_val=LEAVES - 1)
                    at_least(act, h_filled, j + (n0 - 1))
                    at_least(act, hidden_ready, j + (n0 - 1))
                    nc.scalar.copy(w1_leaf[q][:, :], w1[f % 2][:, ds(leaf, 1), :]).then_inc(w1_leaf_ready, 1)

                def rows_T(j, q):
                    act.wait_ge(slot_turned, j + (n0 + 1))
                    at_least(act, h_filled, j + (n0 - 1))
                    nc.scalar.copy(x_slotT[q][:, :], bank(q)).then_inc(slotT_ready, 1)

                def hidden_one(j, q):
                    act.wait_ge(hidden_ready, j + (n0 + 1))
                    at_least(act, y_filled, j + (n0 - 1))
                    if isinstance(j, int) and j + n0 == 0:
                        act.wait_ge(hT_ones, 2)
                    nc.scalar.copy(hT_one[q][0:HID, :], hidden_T[q][:, :]).then_inc(hT_one_ready, 1)

                def step(m, q):
                    edge = isinstance(m, int)
                    if not edge or m < SLOT_TILES:
                        take_w1(m, q % 2)
                        rows_T(m, q % 2)
                    if not edge or 1 <= m <= SLOT_TILES:
                        hidden_one(m - 1, (q + 1) % 2)
                    if edge and m == 2 and f + 1 < F:
                        b2_high(f + 1)

                act.wait_ge(w1_in, 16 * 4 * (f + 1))
                act.wait_ge(b1_placed, f + 1)
                if f == 0:
                    act.wait_ge(tile_leaf_ready, 1)
                walk(act, step, n0, (lambda l, i: w2_high(f + 1, l, i)) if f + 1 < F else None,
                     key_high if f == F - 1 else None)

            def query(n):
                act.wait_ge(sq_turned, n + 1)
                at_least(act, s_scored, n)
                nc.scalar.copy(sq_hi[:, :], pE[:, :]).then_inc(sq_hi_ready, 1)

            def sprobs_hi(n, j):
                act.wait_ge(s_turned, n * KBANKS + (j + 1))
                if j == 0:
                    at_least(act, sz_filled, n)
                nc.scalar.copy(sPT_hi[:, j * BANK:(j + 1) * BANK], pT[j % 2][:, :]).then_inc(sPT_hi_ready, 1)

            def sexp(n):
                act.wait_ge(s_max_ready, n + 1)
                at_least(act, s_turned, n * KBANKS)
                nc.scalar.activation(sprobs[:, :], pS[:, 0:SQ], ACT.Exp, bias=sneg_max[:, 0:1], scale=SELF_SCALE,
                                     accum_out=srow_sum[:, ds(n, 1)]).then_inc(s_exp_ready, 1)

            def step(n, front, back, key):
                for j in range(KBANKS):
                    if back is not None:
                        sprobs_hi(n - 1, j)
                if front is not None and back is None:
                    query(n + 1)
                if front is not None:
                    sexp(n)
                    if back is not None and (not isinstance(n, int) or n + 1 < NT):
                        query(n + 1)
                if key:
                    key_high(n, TQ)

            query(0)
            self_steps(act, step)

        @block.vector
        def _(dve):
            dve.wait_ge(cols_filled, 1)
            nc.vector.tensor_copy(columns[:, :], pE[:, 0:NV]).then_inc(columns_ready, 1)
            dve.wait_ge(columns_ready, 1)
            for wide, column, blocks in ((bvB, bvc, KE), (bqB, bqc, KE), (b1B, b1c, KD)):
                for k in range(blocks):
                    last = nc.vector.tensor_copy(wide[:, k, :], column[:, k:k + 1].broadcast_to([P, P]))
            last.then_inc(broadcast_ready, 1)
            for e in range(KE):
                dve.wait_ge(wT_filled, KE + e + 1)
                nc.vector.tensor_copy(wkT[:, e, :], (pT[0], pT[1], pZ, pE)[e][:, 0:DC]).then_inc(wkT_ready, 1)
            dve.wait_ge(node_filled, 1)
            nc.vector.tensor_copy(nodeT[:, :, :].rearrange("p k n -> p (k n)"), pE[:, 0:KD * F * NODES]).then_inc(nodeT_ready, 1)
            c_in = [c_in0, c_in1, c_in2, c_in3]

            def context_stats(t, slot, landed=None, count=0):
                if landed is None:
                    dve.wait_ge(c_in[slot], (t + (4 - slot)) * 4)
                else:
                    dve.wait_ge(landed, count)
                at_least(dve, c_moments_ready, t - 1)
                nc.vector.bn_stats(c_stats[slot % 2][:, :], c_raw[slot][:, :]).then_inc(c_stats_ready, 1)

            def context_moments(t, slot):
                at_least(dve, c_var_step, 2 * (t - 1))
                wait_apart(dve, c_stats_ready, t + 1)
                nc.vector.bn_aggr(c_moments[slot % 2][:, :], c_stats[slot % 2][:, :]).then_inc(c_moments_ready, 1)

            def context_keep(t, slot):
                dve.wait_ge(c_moments_ready, t + 1)
                nc.vector.tensor_copy(c_mean[:, ds(t, 1)], c_moments[slot % 2][:, 0:1]).then_inc(c_var_step, 1)
                nc.vector.tensor_scalar(c_var[:, ds(t, 1)], c_moments[slot % 2][:, 1:2], EPS, None, ALU.add).then_inc(c_var_step, 1)

            def context_measure(t, slot):
                edge = isinstance(t, int)
                if not edge or t < TC:
                    context_stats(t, slot)
                if not edge or 1 <= t <= TC:
                    context_moments(t - 1, (slot - 1) % 4)
                if not edge or t >= 2:
                    context_keep(t - 2, (slot - 2) % 4)

            for t in range(4):
                context_measure(t, t)
            with dve.Fori(1, TC // 4) as i:
                for slot in range(4):
                    context_measure(i * 4 + slot, slot)
            for t in range(TC, TC + 2):
                context_measure(t, t % 4)

            def measure_more(n):
                for slot, landed in enumerate((c_more0, c_more1)):
                    context_stats(n * 2 + (TC + slot), slot, landed, (n + 1) * 16)
                for slot in range(2):
                    context_moments(n * 2 + (TC + slot), slot)
                for slot in range(2):
                    context_keep(n * 2 + (TC + slot), slot)

            dve.wait_ge(M_full_ready, KD)
            for k in range(KD):
                nc.vector.scalar_tensor_tensor(M_gain[:, k, :], M_full[:, k, :], g1c[:, k:k + 1], g2B[:, :],
                                               ALU.mult, ALU.mult).then_inc(M_gained, 1)

            def x_norm_tile(n):
                dve.wait_ge(x_in, (n + 1) * 16)
                measure(dve, x_raw[:, :], x_stats, x_moments, x_var, x_norm_step, n * 3, 1.0 + EPS, EPS * EPS)

            def x_apply(n):
                dve.wait_ge(x_rooted, n + 1)
                at_least(dve, x_turned, n)
                nc.vector.tensor_scalar(x_hat[:, :], x_raw[:, :], x_moments[:, 0:1], x_rstd[:, 0:1],
                                        ALU.subtract, ALU.mult).then_inc(x_normed, 1)

            def x_low(n):
                dve.wait_ge(xT_hi_ready, n + 1)
                nc.vector.tensor_tensor(xT_lo[:, :], pT[0][:, :], xT_hi[:, :].bitcast(F32), ALU.subtract).then_inc(xT_lo_ready, 1)

            def query(n, psum=pT[1]):
                dve.wait_ge(q_filled, n + 1)
                at_least(dve, q_turned, n)
                nc.vector.tensor_tensor(q_tile[:, :], psum[:, 0:DC], u_gain[:, :], ALU.add).then_inc(q_tile_ready, 1)

            def query_low(n):
                dve.wait_ge(q_hi_ready, n + 1)
                nc.vector.tensor_tensor(q_lo[:, :, :], pT[0][:, 0:DC].rearrange("p (c n) -> p c n", c=KC),
                                        q_hi[:, :, :].bitcast(F32), ALU.subtract).then_inc(q_ready, 1)

            def norm(passing, t, slot):
                dve.wait_ge(c_in[slot], (t + (TC * (passing + 1) + 4 - slot)) * 4)
                if passing == BOTH:
                    at_least(dve, c_turned, t - 3)
                    at_least(dve, c_lo_ready, t - 3)
                elif passing == TRANSPOSED:
                    dve.wait_ge(c_lo_ready, TC)
                    dve.wait_ge(c_turned, t + (TC - 3))
                else:
                    dve.wait_ge(c_turned, B * TC)
                    dve.wait_ge(c_lo_ready, t + (TC - 3))
                tile = t if passing == BOTH else t + TC
                nc.vector.tensor_scalar(c_norm[slot][:, :], c_raw[slot][:, :], c_mean[:, ds(tile, 1)],
                                        c_rstd[:, ds(tile, 1)], ALU.subtract, ALU.mult).then_inc(c_normed, 1)

            def low(passing, t, slot):
                dve.wait_ge(cT_hi_ready, t + (TC * passing + 1))
                psum = (pT[1], pZ)[slot % 2] if passing == BOTH else bank(slot)
                nc.vector.tensor_tensor(ctxT_lo[:, :, ds(t * P, P)], psum[:, 0:DC].rearrange("p (k n) -> p k n", k=KC),
                                        ctxT_hi[:, :, ds(t * P, P)].bitcast(F32), ALU.subtract).then_inc(cT_lo_ready, 1)

            def norms(i):
                for slot in range(4):
                    norm(TRANSPOSED, i * 4 + slot, slot)

            def lows(i):
                for slot in range(4):
                    low(TRANSPOSED, i * 4 + slot, slot)

            def straight(groups):
                with dve.Fori(groups.start, groups.stop) as i:
                    for slot in range(4):
                        norm(STRAIGHT, i * 4 + slot, slot)

            def probs_lo(n, j):
                dve.wait_ge(PT_hi_ready, n * SBANKS + (j + 1))
                cols = slice(j * BANK, (j + 1) * BANK)
                nc.vector.tensor_tensor(PT_lo[:, cols], pT[j % 2][:, :], PT_hi[:, cols].bitcast(F32), ALU.subtract
                                        ).then_inc(PT_ready, 1)

            def early_max(n):
                dve.wait_ge(three_scored, n // TQ + 1)
                nc.vector.tensor_reduce(part_max[:, 0:1], pS[:, 0:SC - BANK], AX.X, ALU.max).then_inc(part_max_ready, 1)

            def row_max(n):
                dve.wait_ge(scored, n + 1)
                if isinstance(n, int) and n % TQ == 0:
                    nc.vector.tensor_reduce(part_max[:, 1:2], pS[:, SC - BANK:SC], AX.X, ALU.max).then_inc(part_max_ready, 1)
                    dve.wait_ge(part_max_ready, 2 * (n // TQ + 1))
                    row = part_max[:, :]
                else:
                    row = pS[:, 0:SC]
                nc.vector.tensor_reduce(raw_max[:, :], row, AX.X, ALU.max).then_inc(raw_max_ready, 1)
                dve.wait_ge(raw_max_ready, n + 1)
                nc.vector.tensor_scalar(neg_max[:, :], raw_max[:, :], -CROSS_SCALE, None, ALU.mult).then_inc(max_ready, 1)

            def normalise(n):
                dve.wait_ge(exp_ready, n + 1)
                nc.vector.reciprocal(inv_sum[:, :], row_sum[:, ds(n, 1)]).then_inc(inv_ready, 1)
                dve.wait_ge(inv_ready, n + 1)
                dve.wait_ge(z_filled, n + 1)
                at_least(dve, z_turned, n)
                nc.vector.tensor_scalar(z_tile[:, :], pZ[:, 0:DC], inv_sum[:, 0:1], None, ALU.mult).then_inc(z_ready, 1)

            def affine(e):
                dve.wait_ge(z_turned, e + 1)
                at_least(dve, zT_lo_ready, e)
                for c in range(KC):
                    cols = slice(c * P, (c + 1) * P)
                    nc.vector.tensor_scalar(zT[:, cols], pE[:, cols], g2c[:, c:c + 1], b2c[:, c:c + 1],
                                            ALU.mult, ALU.add).then_inc(zT_ready, 1)

            def residual(e):
                dve.wait_ge(o_filled, e + 1)
                dve.wait_ge(res_ready, e + 1)
                at_least(dve, mid_stored, e * 16)
                nc.vector.tensor_tensor(x_mid[:, :], pE[:, :], x_resb[:, :], ALU.add).then_inc(mid_ready, 1)

            def measure_mid(e):
                dve.wait_ge(mid_ready, e + 1)
                measure(dve, x_mid[:, :], mid_stats, mid_moments, mid_var, mid_norm_step, e * 3)

            def norm_mid(e):
                dve.wait_ge(mid_rooted, e + 1)
                at_least(dve, norm_stored, e * 16)
                at_least(dve, n_turned, e)
                nc.vector.tensor_scalar(x_norm[:, :], x_mid[:, :], mid_moments[:, 0:1], mid_rstd[:, 0:1],
                                        ALU.subtract, ALU.mult).then_inc(mid_normed, 1)

            def nodes(e):
                dve.wait_ge(nodes_filled, e + 1)
                nc.vector.tensor_tensor(node_scores[:, ds(e, 1), :], pE[:, 0:F * NODES], node_bias[:, :], ALU.add
                                        ).then_inc(nodes_ready, 1)

            def step(n, front, back, tail, ahead, passing=None):
                if passing == TRANSPOSED:
                    dve.wait_ge(c_rooted, B)
                    norms(0)
                for j in range(SBANKS):
                    if back:
                        probs_lo(n - 1, j)
                    if passing == TRANSPOSED:
                        low(passing, j, j)
                    if tail and j == 1:
                        affine(n - 2)
                    if ahead and j == 1 and passing != STRAIGHT:
                        x_norm_tile(n + 1)
                    if ahead and j == 2:
                        x_apply(n + 1)
                        if passing == STRAIGHT:
                            straight(range(1))
                    if passing == STATISTICS and j == 3:
                        measure_more(n)
                if passing == TRANSPOSED:
                    norms(1)
                if tail:
                    residual(n - 2)
                    measure_mid(n - 2)
                if passing == TRANSPOSED:
                    lows(1)
                if ahead and not back:
                    x_low(n + 1)
                    early_max(n)
                    query(n + 1)
                if passing == STRAIGHT:
                    straight(range(1, 2))
                if front:
                    row_max(n)
                if tail:
                    norm_mid(n - 2)
                if ahead and back:
                    x_low(n + 1)
                    query(n + 1)
                if ahead:
                    query_low(n + 1)
                if isinstance(n, int) and n == 0:
                    dve.wait_ge(bias_filled, 2)
                    nc.vector.tensor_tensor(out_bias[:, :], pE[:, :], out_bias[:, :], ALU.add).then_inc(bias_ready, 1)
                if passing == TRANSPOSED:
                    with dve.Fori(2, TC // 4) as i:
                        norms(i)
                        lows(i)
                    x_norm_tile(n + 1)
                if passing == STRAIGHT:
                    straight(range(2, TC // 4))
                if back and not front:
                    normalise(n - 1)
                if tail:
                    nodes(n - 2)
                if back and front:
                    normalise(n - 1)

            def N_low(c):
                dve.wait_ge(N_hi_ready, c + 1)
                return nc.vector.tensor_tensor(N_lo[:, c, :], bank(c), N_hi[:, c, :].bitcast(F32), ALU.subtract)

            def tiles(span):
                for t in span:
                    norm(BOTH, t, t % 4)
                    if t >= 2:
                        low(BOTH, t - 2, (t - 2) % 4)

            x_norm_tile(0)
            dve.wait_ge(c_rooted, 1)
            tiles(range(4))
            dve.wait_ge(M_hi_ready, 1)
            nc.vector.tensor_tensor(M_lo[:, :, :], M_gain[:, :, :], M_hi[:, :, :].bitcast(F32), ALU.subtract).then_inc(M_ready, 1)
            x_apply(0)
            N_low(0)
            tiles(range(4, 6))
            x_low(0)
            N_low(1)
            tiles(range(6, 10))
            N_low(2).then_inc(N_ready, 1)
            tiles(range(10, 14))
            norm(BOTH, 14, 2)
            norm(BOTH, 15, 3)
            dve.wait_ge(bias_filled, 1)
            nc.vector.tensor_tensor(u_gain[:, :], pE[:, 0:DC], g2B[:, :], ALU.mult).then_inc(bias_ready, 1)
            low(BOTH, 12, 0)
            low(BOTH, 13, 1)
            dve.wait_ge(bias_ready, 1)
            query(0, bank(3))
            low(BOTH, 14, 2)
            low(BOTH, 15, 3)
            query_low(0)
            cross_steps(dve, step)

            count = [0]

            def then(instruction):
                count[0] += 1
                instruction.then_inc(route_step, 1)
                dve.wait_ge(route_step, count[0])

            v = nc.vector
            dve.wait_ge(norm_stored, 16 * NT)
            dve.wait_ge(mid_stored, 16 * NT)
            dve.wait_ge(nodes_ready, NT)
            then(v.tensor_scalar(right[:, :, :].rearrange("p (f t) n -> p t f n", f=F),
                                 node_scores[:, :, :].rearrange("p t (f n) -> p t f n", f=F), 0.0, None, ALU.is_ge))
            for k in range(len(reach)):
                wide = reach[k][:, :, :].rearrange("p t (n side) -> p t n side", side=2)
                own = right[:, :, 2 ** k - 1:2 ** (k + 1) - 1]
                if k == 0:
                    v.tensor_copy(wide[:, :, :, 1], own)
                    then(v.tensor_scalar(wide[:, :, :, 0], own, -1.0, 1.0, ALU.mult, ALU.add))
                else:
                    then(v.tensor_tensor(wide[:, :, :, 1], reach[k - 1][:, :, :], own, ALU.mult))
                    then(v.tensor_tensor(wide[:, :, :, 0], reach[k - 1][:, :, :], wide[:, :, :, 1], ALU.subtract))
            L = LEAVES
            then(v.tensor_copy(onehot_h[:, :, 0:NT * L], onehot[:, :, :].rearrange("p (f t) l -> p f (t l)", f=F)))
            v.tensor_copy(pairs[:, :, 0:L], onehot_h[:, :, 0:L])
            then(v.tensor_tensor(pairs[:, :, L:NT * L], onehot_h[:, :, L:NT * L], onehot_h[:, :, 0:(NT - 1) * L], ALU.add))
            v.tensor_copy(fours[:, :, 0:2 * L], pairs[:, :, 0:2 * L])
            v.tensor_tensor(fours[:, :, 2 * L:NT * L], pairs[:, :, 2 * L:NT * L], pairs[:, :, 0:(NT - 2) * L], ALU.add
                            ).then_inc(onehots_ready, 1)
            dve.wait_ge(route_consts, 6)
            v.tensor_copy(iota_f[:, :], iota_i[:, :])
            then(v.tensor_copy(token_f[:, :], token_i[:, :]))
            dve.wait_ge(b1_turned, 1)
            v.tensor_copy(w1[0][:, :, KD * HID], pE[:, 0:LEAVES]).then_inc(b1_placed, 1)
            dve.wait_ge(w2_hi_ready, 2 * 4)
            v.tensor_tensor(w2_lo[0][0:HID, 0:4, :], w2_raw[0][0:HID, 0:4, :], w2_hi[0][0:HID, 0:4, :].bitcast(F32),
                            ALU.subtract).then_inc(w2_lo_ready, 4)
            dve.wait_ge(ranks_filled, 1)
            counts = pS[:, 0:F * BANK].rearrange("p (f n) -> p f n", f=F)[:, :, NT * LEAVES:(NT + 1) * LEAVES]
            then(v.tensor_scalar(n_leaf[:, :].rearrange("p (f l) -> p f l", f=F), counts, float(P - 1), None, ALU.add))
            then(v.tensor_single_scalar(n_tiles_i[:, :], n_leaf[:, :], P.bit_length() - 1, ALU.arith_shift_right))
            then(v.tensor_copy(n_tiles[:, :, :].rearrange("p f l -> p (f l)"), n_tiles_i[:, :]))
            src = n_tiles
            for k in range(4):
                d = 2 ** k
                v.tensor_copy(scan[k][:, :, 0:d], src[:, :, 0:d])
                then(v.tensor_tensor(scan[k][:, :, d:], src[:, :, d:], src[:, :, 0:LEAVES - d], ALU.add))
                src = scan[k]
            ends = src
            then(v.tensor_tensor(scan[4][:, :, :], ends[:, :, :], n_tiles[:, :, :], ALU.subtract))
            then(v.tensor_scalar(base[:, :, :], scan[4][:, :, :], float(P), None, ALU.mult))
            for f in range(F):
                own = place[:, f * NT:(f + 1) * NT, :]
                last = v.tensor_tensor(own, bank(f)[:, 0:NT * LEAVES].rearrange("p (t l) -> p t l", t=NT),
                                       base[:, f:f + 1, :].broadcast_to([P, NT, LEAVES]), ALU.add)
            then(last)
            then(v.tensor_tensor(place[:, :, :], place[:, :, :], onehot[:, :, :], ALU.mult))
            then(v.tensor_reduce(pos[:, :], place[:, :, :], AX.X, ALU.add))
            then(v.tensor_copy(token_slot[:, :], pos[:, :]))
            v.tensor_single_scalar(part_i[:, 0:FT], token_slot[:, :], P.bit_length() - 1, ALU.arith_shift_right)
            then(v.tensor_single_scalar(part_i[:, FT:2 * FT], token_slot[:, :], P - 1, ALU.bitwise_and))
            then(v.tensor_copy(part[:, :], part_i[:, :]))

            def one_hots(f):
                own = slice(f * NT, (f + 1) * NT)
                wide = [P, NT, HI_PAD]
                then(v.tensor_tensor(hi_hot[:, own, :], iota_f[:, 0:HI_PAD].rearrange("p (a n) -> p a n", a=1).broadcast_to(wide),
                                     part[:, own].rearrange("p (t a) -> p t a", a=1).broadcast_to(wide), ALU.is_equal))
                v.tensor_tensor(hi_tok[:, own, :], hi_hot[:, own, :],
                                token_f[:, :].rearrange("p (t a) -> p t a", a=1).broadcast_to(wide), ALU.mult)
                wide = [P, NT, P]
                v.tensor_tensor(lo_hot[:, own, :], iota_f[:, :].rearrange("p (a n) -> p a n", a=1).broadcast_to(wide),
                                part[:, FT + f * NT:FT + (f + 1) * NT].rearrange("p (t a) -> p t a", a=1).broadcast_to(wide),
                                ALU.is_equal).then_inc(split_ready, 1)

            def table(f):
                dve.wait_ge(slots_filled, f + 1)
                v.tensor_copy(slot_index[:, f * HI_PAD:(f + 1) * HI_PAD], (pT[1], pZ, pE)[f][:, 0:HI_PAD]
                              ).then_inc(tables_ready, 1)

            one_hots(0)
            table(0)
            for f in range(F):
                wide = [P, HI_PAD, LEAVES]
                last = v.tensor_tensor(leaf_cmp[:, f * HI_PAD:(f + 1) * HI_PAD, :],
                                       iota_f[:, 0:HI_PAD].rearrange("p (n a) -> p n a", a=1).broadcast_to(wide),
                                       ends[:, f:f + 1, :].broadcast_to(wide), ALU.is_ge)
            then(last)
            then(v.tensor_reduce(leaf_f[:, :], leaf_cmp[:, :, :], AX.X, ALU.add))
            then(v.tensor_scalar(leaf_m[:, :], leaf_f[:, :], float(LEAVES - 1), None, ALU.min))
            v.tensor_copy(tile_leaf[:, :], leaf_m[:, :]).then_inc(tile_leaf_ready, 1)
            one_hots(1)

            y_stored = [y_stored0, y_stored1, y_stored2, y_stored3]

            def key_low(t, t0=0):
                b = t0 // TQ
                dve.wait_ge(kT_hi_ready, t + (t0 + 1))
                v.tensor_tensor(kT_lo[b][:, :, ds(t * P, P)], (bank(2) if b else pE[:, :]).rearrange("p (k n) -> p k n", k=KD),
                                kT_hi[b][:, :, ds(t * P, P)].bitcast(F32), ALU.subtract).then_inc(kT_ready, 1)
                dve.wait_ge(v_hi_ready, t + (t0 + 1))
                v.tensor_tensor(v_lo[b][:, ds(t, 1), :], v_rows[:, :], v_hi[b][:, ds(t, 1), :].bitcast(F32), ALU.subtract
                                ).then_inc(v_ready, 1)

            for f in range(F):
                n0 = SLOT_TILES * f

                def hidden(j, q):
                    dve.wait_ge(h_filled, j + (n0 + 1))
                    at_least(dve, hT_one_ready, j + (n0 - 1))
                    v.tensor_scalar(hidden_T[q][:, :], pT[q][0:HID, 0:P], w1_leaf[q][0:HID, KD * HID:W1], 0.0,
                                    ALU.add, ALU.max).then_inc(hidden_ready, 1)
                    dve.wait_ge(hidden_ready, j + (n0 + 1))
                    at_least(dve, y_filled, j + (n0 - 1))
                    v.tensor_copy(hT[q][0:HID, :], hidden_T[q][:, :]).then_inc(hT_hi_ready, 1)
                    dve.wait_ge(hT_hi_ready, j + (n0 + 1))
                    v.tensor_tensor(hT[q][HID:P, :], hidden_T[q][:, :], hT[q][0:HID, :].bitcast(F32), ALU.subtract
                                    ).then_inc(hT_ready, 1)

                def result(j, q):
                    dve.wait_ge(y_filled, j + (n0 + 1))
                    at_least(dve, y_stored[q], (j + (n0 - q)) * 4)
                    v.tensor_copy(y_slot[q][:, :], bank(2 + q % 2)).then_inc(y_ready, 1)

                def step(m, q):
                    edge = isinstance(m, int)
                    if edge and m == SLOT_TILES and f + 1 < F:
                        dve.wait_ge(b1_turned, f + 2)
                        v.tensor_copy(w1[(f + 1) % 2][:, :, KD * HID], pE[:, 0:LEAVES]).then_inc(b1_placed, 1)
                    if not edge or 1 <= m <= SLOT_TILES:
                        hidden(m - 1, (q + 1) % 2)
                    if f == 0 and edge and m == 1:
                        one_hots(2)
                    if f == 0 and edge and m == 2:
                        table(1)
                        table(2)
                    if not edge or 2 <= m:
                        result(m - 2, (q + 2) % 4)
                    if edge and m == 2 and f + 1 < F:
                        dve.wait_ge(b2_hi_ready, f + 2)
                        v.tensor_tensor(b2_lo[:, :], b2_raw[:, :], b2_hi[:, :].bitcast(F32), ALU.subtract).then_inc(b2_ready, 1)

                def w2_low(l, i):
                    dve.wait_ge(w2_hi_ready, l * 2 + (2 * (f + 1) * LEAVES + 2))
                    v.tensor_tensor(w2_lo[(f + 1) % 2][0:HID, ds(l, 1), :], w2_raw[(f + 1) % 2][0:HID, ds(l, 1), :],
                                    w2_hi[(f + 1) % 2][0:HID, ds(l, 1), :].bitcast(F32),
                                    ALU.subtract).then_inc(w2_lo_ready, 1)

                walk(dve, step, n0, w2_low if f + 1 < F else None, key_low if f == F - 1 else None)

            for q in range(4):
                dve.wait_ge(y_stored[q], stored_in(F, q))

            def query(n):
                dve.wait_ge(sq_hi_ready, n + 1)
                v.tensor_tensor(sq_lo[:, :], pE[:, :], sq_hi[:, :].bitcast(F32), ALU.subtract).then_inc(sq_ready, 1)

            def sprobs_lo(n, j):
                dve.wait_ge(sPT_hi_ready, n * KBANKS + (j + 1))
                cols = slice(j * BANK, (j + 1) * BANK)
                v.tensor_tensor(sPT_lo[:, cols], pT[j % 2][:, :], sPT_hi[:, cols].bitcast(F32), ALU.subtract
                                ).then_inc(sPT_ready, 1)

            def srow_max(n):
                dve.wait_ge(s_scored, n + 1)
                v.tensor_reduce(sraw_max[:, :], pS[:, 0:SQ], AX.X, ALU.max).then_inc(s_raw_max_ready, 1)
                dve.wait_ge(s_raw_max_ready, n + 1)
                v.tensor_scalar(sneg_max[:, :], sraw_max[:, :], -SELF_SCALE, None, ALU.mult).then_inc(s_max_ready, 1)

            def result(n):
                dve.wait_ge(s_exp_ready, n + 1)
                at_least(dve, out_ready, n)
                v.reciprocal(sinv_sum[:, :], srow_sum[:, ds(n, 1)]).then_inc(s_inv_ready, 1)
                dve.wait_ge(s_inv_ready, n + 1)
                dve.wait_ge(sz_filled, n + 1)
                dve.wait_ge(mid_in, (n + 1) * 16)
                at_least(dve, out_stored, n * 16)
                v.scalar_tensor_tensor(out_tile[:, :], pZ[:, :], sinv_sum[:, 0:1], mid_tile[:, :], ALU.mult, ALU.add
                                       ).then_inc(out_ready, 1)

            def step(n, front, back, key):
                for j in range(KBANKS):
                    if back is not None:
                        sprobs_lo(n - 1, j)
                if front is not None:
                    srow_max(n)
                    if not isinstance(n, int) or n + 1 < NT:
                        query(n + 1)
                if key:
                    key_low(n, TQ)
                if back is not None:
                    result(n - 1)

            query(0)
            self_steps(dve, step)

        @block.gpsimd
        def _(pool):
            g = nc.gpsimd
            g.memset(ident[:, :], 0.0).then_inc(ident_zero, 1)
            pool.wait_ge(ident_zero, 1)
            g.affine_select(out=ident[:, :], in_=ident[:, :], compare_op=ALU.not_equal, fill=1.0, base=0,
                            pattern=[[-1, P]], channel_multiplier=1).then_inc(ident_ready, 1)

            g.memset(minus_half[:, :], -0.5).then_inc(half_ready, 1)
            pool.wait_ge(half_ready, 1)

            def x_root(n):
                root(pool, x_rstd, x_var, x_norm_step, n * 3, x_rooted)

            def tail(e):
                pool.wait_ge(res_in, (e + 1) * 16)
                at_least(pool, mid_ready, e)
                g.tensor_tensor(x_resb[:, :], x_res[:, :], out_bias[:, :], ALU.add).then_inc(res_ready, 1)
                pool.wait_ge(zT_hi_ready, e + 1)
                g.tensor_tensor(zT_lo[:, :], zT[:, :], zT_hi[:, :].bitcast(F32), ALU.subtract).then_inc(zT_lo_ready, 1)

            def mid_root(e):
                root(pool, mid_rstd, mid_var, mid_norm_step, e * 3, mid_rooted)

            def context_low(b):
                with pool.Fori(0, TC // 4) as i:
                    for slot in range(4):
                        t = i * 4 + slot
                        wait_apart(pool, c_hi_ready, t + (TC * b + 1))
                        g.tensor_tensor(ctx_lo[:, ds(t, 1), :], c_norm[slot][:, :], ctx_hi[:, ds(t, 1), :].bitcast(F32),
                                        ALU.subtract).then_inc(c_lo_ready, 1)

            def context_roots(b):
                pool.wait_ge(c_var_step, 2 * (b + 1) * TC)
                own = slice(b * TC, (b + 1) * TC)
                g.tensor_tensor(c_rstd[:, own], c_var[:, own], minus_half[:, 0:TC], ALU.pow).then_inc(c_rooted, 1)

            context_roots(0)
            x_root(0)
            context_low(0)
            x_root(1)
            x_root(2)
            with pool.Fori(0, TQ - 2) as e:
                tail(e)
                x_root(e + 3)
                mid_root(e)
            context_roots(1)
            tail(TQ - 2)
            mid_root(TQ - 2)
            x_root(TQ + 1)
            context_low(1)
            with pool.Fori(TQ - 1, NT - 3) as e:
                tail(e)
                x_root(e + 3)
                mid_root(e)
            for e in range(NT - 3, NT):
                tail(e)
                mid_root(e)

            pool.wait_ge(nodes_ready, NT)
            pool.wait_ge(norm_stored, 16 * NT)
            pool.wait_ge(mid_stored, 16 * NT)
            g.memset(ones_h[:, :], 1.0).then_inc(route_consts, 1)
            g.memset(before[:, :], 1.0).then_inc(route_consts, 1)
            g.memset(onehot_h[:, :, NT * LEAVES:], 0.0).then_inc(route_consts, 1)
            pool.wait_ge(route_consts, 3)
            g.affine_select(out=before[:, :], in_=before[:, :], compare_op=ALU.is_gt, fill=0.0, base=0,
                            pattern=[[1, P]], channel_multiplier=-1).then_inc(route_consts, 1)
            g.iota(iota_i[:, :], pattern=[[1, P]], base=0, channel_multiplier=0).then_inc(route_consts, 1)
            g.iota(token_i[:, :], pattern=[[P, NT]], base=0, channel_multiplier=1).then_inc(route_consts, 1)

            pool.wait_ge(route_consts, 6)
            pool.wait_ge(b2_hi_ready, 1)
            g.tensor_tensor(b2_lo[:, :], b2_raw[:, :], b2_hi[:, :].bitcast(F32), ALU.subtract).then_inc(b2_ready, 1)
            for q in range(2):
                g.memset(hT_one[q][HID:HID + 2, :].bitcast(F32), 1.0).then_inc(hT_ones, 1)
                pool.wait_ge(hT_ones, q + 1)
            for l in range(4, LEAVES, 4):
                pool.wait_ge(w2_hi_ready, 2 * (l + 4))
                g.tensor_tensor(w2_lo[0][0:HID, l:l + 4, :], w2_raw[0][0:HID, l:l + 4, :],
                                w2_hi[0][0:HID, l:l + 4, :].bitcast(F32), ALU.subtract).then_inc(w2_lo_ready, 4)
            slot_in = [slot_in0, slot_in1, slot_in2, slot_in3]
            y_stored = [y_stored0, y_stored1, y_stored2, y_stored3]

            def rows_of(f, index, rows, index_ready, n, n_index, landed):
                g.tensor_copy(index[:, :], token_slot[:, ds(n + f * NT, 1)]).then_inc(index_ready, 1)
                wait_apart(pool, index_ready, n_index)
                g.indirect_dma_start(out=rows[:, :], out_offset=None, in_=slot_rows[f],
                                     in_offset=bass.IndirectOffsetOnAxis(ap=index[:, 0:1], axis=0)).then_inc(landed, 16)

            def gather_keys(t, t0=0):
                n = t + t0
                if isinstance(n, int) and n == 0:
                    for q in range(4):
                        pool.wait_ge(y_stored[q], stored_in(2, q))
                at_least(pool, sk_turned, n)
                rows_of(0, kv_index[0], k_rows, kv_index_ready, n, n * 2 + 1, k_in)
                at_least(pool, v_ready, n)
                rows_of(1, kv_index[1], v_rows, kv_index_ready, n, n * 2 + 2, v_in)

            for f in range(F):
                n0 = SLOT_TILES * f
                pool.wait_ge(tables_ready, 1 if f == 0 else F)

                def gather(j, q):
                    at_least(pool, slot_turned, j + (n0 - 3))
                    at_least(pool, slot_in[q], (j + (n0 - q)) * 4)
                    g.tensor_copy(row_index[q][:, :], slot_index[:, ds(j + f * HI_PAD, 1)]).then_inc(index_ready, 1)
                    wait_apart(pool, index_ready, j + (n0 + 1))
                    g.indirect_dma_start(out=x_slot[q][:, :], out_offset=None, in_=norm_rows,
                                         in_offset=bass.IndirectOffsetOnAxis(ap=row_index[q][:, 0:1], axis=0)
                                         ).then_inc(slot_in[q], 16)

                def step(m, q):
                    if not isinstance(m, int) or m < SLOT_TILES:
                        gather(m, q)

                walk(pool, step, n0, key_tile=gather_keys if f == F - 1 else None)

            for q in range(4):
                pool.wait_ge(y_stored[q], stored_in(F, q))

            def gather_query(n):
                at_least(pool, sq_turned, n)
                rows_of(F - 1, q_index, q_rows, q_index_ready, n, n + 1, sq_in)

            gather_query(0)
            with pool.Fori(0, TQ) as n:
                gather_query(n + 1)
                gather_keys(n, TQ)
            with pool.Fori(TQ + 1, NT) as n:
                gather_query(n)


_TREES = ["k", "v", "q"]
_LEAF = ["node_w", "node_b", "w1", "b1", "w2", "b2"]
_XATTN = ["ln1_g", "ln1_b", "ln2_g", "ln2_b", "Wq", "bq", "Wk", "bk", "Wv", "bv", "Wo", "bo"]
_INS = ["x", "ctx_768"] + ["L0_xattn_" + n for n in _XATTN] + [f"L0_ffn_{t}_{n}" for t in _TREES for n in _LEAF]
_OUT = ((2, 1024, 512), "float32")


def kernel(**inputs):
    import concourse.bacc as _bacc
    from concourse.bass_utils import run_bass_kernel_spmd as _run

    nc = _bacc.Bacc("TRN2", target_bir_lowering=False, num_devices=1)
    arrays, aps = {}, {}
    for name in _INS:
        a = np.ascontiguousarray(inputs[name])
        arrays[f"in_{name}_dram"] = a
        aps[name] = nc.dram_tensor(f"in_{name}_dram", a.shape, mybir.dt.from_np(a.dtype), kind="ExternalInput").ap()
    out = nc.dram_tensor("out_0_dram", _OUT[0], mybir.dt.from_np(np.dtype(_OUT[1])), kind="ExternalOutput").ap()
    trees = [{n: aps[f"L0_ffn_{t}_{n}"] for n in _LEAF} for t in _TREES]
    build(nc, aps["x"], aps["ctx_768"], *[aps["L0_xattn_" + n] for n in _XATTN], trees, out)
    r = _run(nc, [arrays], core_ids=[0])
    return r.results[0]["out_0_dram"]
```
